# Optimizing a Trainium2 kernel written in Bass

```python
import numpy as np
import jax
import jax.numpy as jnp

def _softmax(x, axis=-1):
    return jax.nn.softmax(x, axis=axis)

def _gelu(x):
    return jax.nn.gelu(x, approximate=True)

def _silu(x):
    return jax.nn.silu(x)

def _sigmoid(x):
    return jax.nn.sigmoid(x)

def _layernorm(x, axis=-1, eps=1e-05):
    m = jnp.mean(x, axis=axis, keepdims=True)
    v = jnp.var(x, axis=axis, keepdims=True)
    return (x - m) / jnp.sqrt(v + eps)

def _scatter_add(tgt, idx, src, axis=0):
    return tgt.at[idx].add(src)

def _segment_sum(src, seg, n):
    return jax.ops.segment_sum(src, seg, n)
kernel_name = 'mk_decoder_postln_d1_seqx_r4_bb1e98'

def setup_inputs(seed: int=0):
    np.random.seed(seed)
    _w = jnp.asarray

    def _rec_inputs():
        import jax
        import jax.numpy as jnp
        _rk = jax.random.key(seed)
        x = 0.0002417 + 0.9998 * jax.random.normal(jax.random.fold_in(_rk, 1), (4, 1024, 256), jnp.float32)
        _lenS = 1024 - jax.random.randint(jax.random.fold_in(_rk, 7), (4,), 0, max(1, 1024 // 4) + 1, jnp.int32)
        _lenS2 = 77 - jax.random.randint(jax.random.fold_in(_rk, 8), (4,), 0, max(1, 77 // 4) + 1, jnp.int32)
        _ctx_1024P = jax.random.normal(jax.random.fold_in(_rk, 11), (4, 16, 256), jnp.float32)
        _ctx_1024c = jax.random.dirichlet(jax.random.fold_in(_rk, 511), 0.3 * jnp.ones((16,), jnp.float32), (4, 77))
        _ctx_1024t = jnp.einsum('bsk,bkd->bsd', _ctx_1024c, _ctx_1024P)
        _ctx_1024t = _ctx_1024t * jax.lax.rsqrt(jnp.mean(jnp.square(_ctx_1024t)) + 1e-12) * 0.953939
        ctx_1024 = 7.22013e-05 + 1.00017 * (_ctx_1024t + 0.3 * jax.random.normal(jax.random.fold_in(_rk, 611), (4, 77, 256), jnp.float32))
        return (x, ctx_1024)
    x, ctx_1024 = _rec_inputs()

    def _L0_attn_setup():
        import jax, jax.numpy as jnp
        import numpy as np
        import math
        D_MODEL = 256
        LN_EPS = 1e-05

        def _layer_norm(x):
            mu = jnp.mean(x, axis=-1, keepdims=True)
            var = jnp.var(x, axis=-1, keepdims=True)
            return (x - mu) * jax.lax.rsqrt(var + LN_EPS)
        key = jax.random.key(seed)
        ks = jax.random.split(key, 5)
        B, S, D = (4, 512, D_MODEL)
        scale = 1.0 / math.sqrt(D)
        x = jax.random.normal(ks[0], (B, S, D), dtype=jnp.float32)
        Wq = jax.random.normal(ks[1], (D, D), dtype=jnp.float32) * scale
        Wk = jax.random.normal(ks[2], (D, D), dtype=jnp.float32) * scale
        Wv = jax.random.normal(ks[3], (D, D), dtype=jnp.float32) * scale
        Wo = jax.random.normal(ks[4], (D, D), dtype=jnp.float32) * scale
        b = jnp.zeros((D,), dtype=jnp.float32)
        layerscale = 0.0001 * jnp.ones((D,), dtype=jnp.float32)
        return {'x': x, 'Wq': Wq, 'bq': b, 'Wk': Wk, 'bk': b, 'Wv': Wv, 'bv': b, 'Wo': Wo, 'bo': b, 'layerscale': layerscale}
    _L0_attn_all = _L0_attn_setup()
    _L0_attn_in = {k: v for k, v in _L0_attn_all.items() if k in ('Wq', 'bq', 'Wk', 'bk', 'Wv', 'bv', 'Wo', 'bo', 'layerscale')}
    del _L0_attn_all

    def _L0_xattn_setup():
        import jax, jax.numpy as jnp
        import numpy as np
        D_MODEL = 256
        NUM_HEADS = 16
        DEPTH = D_MODEL // NUM_HEADS

        def _split_heads(x):
            B, S, _ = x.shape
            return x.reshape(B, S, NUM_HEADS, DEPTH).transpose(0, 2, 1, 3)
        key = jax.random.key(seed)
        ks = jax.random.split(key, 11)
        B, S = (4, 512)
        scale = 1.0 / np.sqrt(D_MODEL)
        inp = {'v': jax.random.normal(ks[0], (B, S, D_MODEL), jnp.float32), 'k': jax.random.normal(ks[1], (B, S, D_MODEL), jnp.float32), 'q': jax.random.normal(ks[2], (B, S, D_MODEL), jnp.float32), 'wq_w': jax.random.normal(ks[3], (D_MODEL, D_MODEL), jnp.float32) * scale, 'wq_b': jnp.zeros((D_MODEL,), jnp.float32), 'wk_w': jax.random.normal(ks[4], (D_MODEL, D_MODEL), jnp.float32) * scale, 'wk_b': jnp.zeros((D_MODEL,), jnp.float32), 'wv_w': jax.random.normal(ks[5], (D_MODEL, D_MODEL), jnp.float32) * scale, 'wv_b': jnp.zeros((D_MODEL,), jnp.float32), 'dense_w': jax.random.normal(ks[6], (D_MODEL, D_MODEL), jnp.float32) * scale, 'dense_b': jnp.zeros((D_MODEL,), jnp.float32)}
        return inp
    _L0_xattn_all = _L0_xattn_setup()
    _L0_xattn_in = {k: v for k, v in _L0_xattn_all.items() if k in ('wq_w', 'wq_b', 'wk_w', 'wk_b', 'wv_w', 'wv_b', 'dense_w', 'dense_b')}
    del _L0_xattn_all

    def _L0_ffn_setup():
        import jax, jax.numpy as jnp
        import numpy as np
        DIM = 256

        def _reference_tuple_inner(x, W_r, W_k, W_v, mu_r, mu_k):
            B, T, C = x.shape
            x_prev = jnp.concatenate([jnp.zeros((B, 1, C), x.dtype), x[:, :-1, :]], axis=1)
            xr = mu_r * x + (1.0 - mu_r) * x_prev
            xk = mu_k * x + (1.0 - mu_k) * x_prev
            r = jax.nn.sigmoid(jnp.einsum('btc,dc->btd', xr, W_r))
            k = jnp.einsum('btc,dc->btd', xk, W_k)
            k_act = jnp.square(jax.nn.relu(k))
            out = r * jnp.einsum('btc,dc->btd', k_act, W_v)
            new_state = x[:, -1, :]
            return (out, new_state)
        key = jax.random.key(seed)
        ks = jax.random.split(key, 6)
        B, T, C = (8, 512, DIM)
        x = jax.random.normal(ks[0], (B, T, C), dtype=jnp.float32)
        s = 1.0 / np.sqrt(C)
        W_r = jax.random.uniform(ks[1], (C, C), jnp.float32, -s, s)
        W_k = jax.random.uniform(ks[2], (C, C), jnp.float32, -s, s)
        W_v = jax.random.uniform(ks[3], (C, C), jnp.float32, -s, s)
        mu_r = jax.random.uniform(ks[4], (C,), jnp.float32)
        mu_k = jax.random.uniform(ks[5], (C,), jnp.float32)
        return {'x': x, 'W_r': W_r, 'W_k': W_k, 'W_v': W_v, 'mu_r': mu_r, 'mu_k': mu_k}
    _L0_ffn_all = _L0_ffn_setup()
    _L0_ffn_in = {k: v for k, v in _L0_ffn_all.items() if k in ('W_r', 'W_k', 'W_v', 'mu_r', 'mu_k')}
    del _L0_ffn_all
    return {'x': x, 'ctx_1024': ctx_1024, 'L0_attn_Wq': _L0_attn_in['Wq'], 'L0_attn_bq': _L0_attn_in['bq'], 'L0_attn_Wk': _L0_attn_in['Wk'], 'L0_attn_bk': _L0_attn_in['bk'], 'L0_attn_Wv': _L0_attn_in['Wv'], 'L0_attn_bv': _L0_attn_in['bv'], 'L0_attn_Wo': _L0_attn_in['Wo'], 'L0_attn_bo': _L0_attn_in['bo'], 'L0_attn_layerscale': _L0_attn_in['layerscale'], 'L0_xattn_wq_w': _L0_xattn_in['wq_w'], 'L0_xattn_wq_b': _L0_xattn_in['wq_b'], 'L0_xattn_wk_w': _L0_xattn_in['wk_w'], 'L0_xattn_wk_b': _L0_xattn_in['wk_b'], 'L0_xattn_wv_w': _L0_xattn_in['wv_w'], 'L0_xattn_wv_b': _L0_xattn_in['wv_b'], 'L0_xattn_dense_w': _L0_xattn_in['dense_w'], 'L0_xattn_dense_b': _L0_xattn_in['dense_b'], 'L0_ffn_W_r': _L0_ffn_in['W_r'], 'L0_ffn_W_k': _L0_ffn_in['W_k'], 'L0_ffn_W_v': _L0_ffn_in['W_v'], 'L0_ffn_mu_r': _L0_ffn_in['mu_r'], 'L0_ffn_mu_k': _L0_ffn_in['mu_k']}

def reference(x, ctx_1024, L0_attn_Wq, L0_attn_bq, L0_attn_Wk, L0_attn_bk, L0_attn_Wv, L0_attn_bv, L0_attn_Wo, L0_attn_bo, L0_attn_layerscale, L0_xattn_wq_w, L0_xattn_wq_b, L0_xattn_wk_w, L0_xattn_wk_b, L0_xattn_wv_w, L0_xattn_wv_b, L0_xattn_dense_w, L0_xattn_dense_b, L0_ffn_W_r, L0_ffn_W_k, L0_ffn_W_v, L0_ffn_mu_r, L0_ffn_mu_k):
    import jax
    import jax.numpy as jnp

    def _L0_attn_ref(x, Wq, bq, Wk, bk, Wv, bv, Wo, bo, layerscale):
        import jax, jax.numpy as jnp
        import numpy as np
        import math
        D_MODEL = 256
        LN_EPS = 1e-05

        def _layer_norm(x):
            mu = jnp.mean(x, axis=-1, keepdims=True)
            var = jnp.var(x, axis=-1, keepdims=True)
            return (x - mu) * jax.lax.rsqrt(var + LN_EPS)
        B, S, D = x.shape
        q = jnp.einsum('bsd,ed->bse', x, Wq) + bq
        k = jnp.einsum('bsd,ed->bse', x, Wk) + bk
        v = jnp.einsum('bsd,ed->bse', x, Wv) + bv
        qn = _layer_norm(q)
        kn = _layer_norm(k)
        scores = jnp.einsum('bse,bte->bst', qn, kn) / jnp.sqrt(jnp.float32(D))
        attn = jax.nn.sigmoid(scores - jnp.log(jnp.float32(S)))
        out = jnp.einsum('bst,bte->bse', attn, v)
        proj = jnp.einsum('bsd,ed->bse', out, Wo) + bo
        return proj * layerscale

    def _L0_xattn_ref(v, k, q, wq_w, wq_b, wk_w, wk_b, wv_w, wv_b, dense_w, dense_b):
        import jax, jax.numpy as jnp
        import numpy as np
        D_MODEL = 256
        NUM_HEADS = 16
        DEPTH = D_MODEL // NUM_HEADS

        def _split_heads(x):
            B, S, _ = x.shape
            return x.reshape(B, S, NUM_HEADS, DEPTH).transpose(0, 2, 1, 3)
        B, S, _ = q.shape
        qh = _split_heads(q @ wq_w.T + wq_b)
        kh = _split_heads(k @ wk_w.T + wk_b)
        vh = _split_heads(v @ wv_w.T + wv_b)
        scale = 1.0 / jnp.sqrt(jnp.float32(DEPTH))
        logits = jnp.einsum('bhqd,bhkd->bhqk', qh, kh) * scale
        attn = jax.nn.softmax(logits, axis=-1)
        out = jnp.einsum('bhqk,bhkd->bhqd', attn, vh)
        out = out.transpose(0, 2, 1, 3).reshape(B, S, D_MODEL)
        return out @ dense_w.T + dense_b

    def _L0_ffn_ref(x, W_r, W_k, W_v, mu_r, mu_k):
        import jax, jax.numpy as jnp
        import numpy as np
        DIM = 256

        def _reference_tuple_inner(x, W_r, W_k, W_v, mu_r, mu_k):
            B, T, C = x.shape
            x_prev = jnp.concatenate([jnp.zeros((B, 1, C), x.dtype), x[:, :-1, :]], axis=1)
            xr = mu_r * x + (1.0 - mu_r) * x_prev
            xk = mu_k * x + (1.0 - mu_k) * x_prev
            r = jax.nn.sigmoid(jnp.einsum('btc,dc->btd', xr, W_r))
            k = jnp.einsum('btc,dc->btd', xk, W_k)
            k_act = jnp.square(jax.nn.relu(k))
            out = r * jnp.einsum('btc,dc->btd', k_act, W_v)
            new_state = x[:, -1, :]
            return (out, new_state)
        return _reference_tuple_inner(x, W_r, W_k, W_v, mu_r, mu_k)[0]
    x = _layernorm(x + _L0_attn_ref(x, L0_attn_Wq, L0_attn_bq, L0_attn_Wk, L0_attn_bk, L0_attn_Wv, L0_attn_bv, L0_attn_Wo, L0_attn_bo, L0_attn_layerscale), axis=-1)
    x = _layernorm(x + _L0_xattn_ref(ctx_1024, ctx_1024, x, L0_xattn_wq_w, L0_xattn_wq_b, L0_xattn_wk_w, L0_xattn_wk_b, L0_xattn_wv_w, L0_xattn_wv_b, L0_xattn_dense_w, L0_xattn_dense_b), axis=-1)
    x = _layernorm(x + _L0_ffn_ref(x, L0_ffn_W_r, L0_ffn_W_k, L0_ffn_W_v, L0_ffn_mu_r, L0_ffn_mu_k), axis=-1)
    return x

_drawn_inputs = setup_inputs


def setup_inputs(seed=0):
    import zlib

    import numpy as np

    out = dict(_drawn_inputs(seed))
    spreads = {'L0_attn_bq': (0.0, 2.0),
     'L0_attn_bk': (0.0, 2.0),
     'L0_attn_bv': (0.0, 2.0),
     'L0_attn_bo': (0.0, 2.0),
     'L0_attn_layerscale': (9.999999747378752e-05, 0.6),
     'L0_xattn_wq_b': (0.0, 0.407),
     'L0_xattn_wk_b': (0.0, 2.0),
     'L0_xattn_wv_b': (0.0, 0.1),
     'L0_xattn_dense_b': (0.0, 0.1)}
    factors = {'L0_attn_Wq': 64.0,
     'L0_attn_Wk': 64.0,
     'L0_attn_Wv': 64.0,
     'L0_attn_Wo': 64.0,
     'L0_ffn_W_r': 2.799,
     'L0_ffn_mu_r': 6.88}
    for name, (base, spread) in spreads.items():
        noise = np.random.default_rng([zlib.crc32(name.encode()), seed]).standard_normal(out[name].shape)
        drawn = base * np.exp(spread * noise) if base else spread * noise
        out[name] = jnp.asarray(drawn.astype(out[name].dtype))
    for name, factor in factors.items():
        out[name] = (out[name] * factor).astype(out[name].dtype)
    return out
```

```python
from contextlib import ExitStack

import numpy as np

import concourse.bass as bass
from concourse import mybir

F32 = mybir.dt.float32
F32R = mybir.dt.float32r
ALU = mybir.AluOpType
ACT = mybir.ActivationFunctionType
AX = mybir.AxisListType.X

P = 128
B, S, D = 4, 1024, 256
KC = D // P
NT = B * S // P
TB = S // P
NG = NT // 4
NJ = NT // 2
H, DH = 16, 16
SC = 77
HC = H // KC
W = HC * SC
RV = -(-W // P)
PW = KC * W
PPAD = W + RV * P
EPS = 1e-5
BANK = 512
RING = 5
S0 = 152
LOGIT_CUTS = [(0, 0, 360), (0, 360, W), (1, 0, 256), (1, 256, W)]


class Count:

    def __init__(self, sem, per=1):
        self.sem, self.per = sem, per

    def at(self, i, k=None):
        return self.sem, self.per * i + (self.per if k is None else k)


class Waiter:

    def __init__(self, eng):
        self.eng, self.seen = eng, {}

    def __call__(self, *pairs):
        for sem, value in pairs:
            if value > self.seen.get(sem.name, 0):
                self.seen[sem.name] = value
                self.eng.wait_ge(sem, value)


def self_attention_order():
    order = []
    for b in range(B + 1):
        load, attend = [], []
        if b < B:
            for t in range(TB + 2):
                i = b * TB + t
                if t < TB:
                    if t % 2 == 0:
                        load.append(("XT", i // 2))
                    load.append(("QK", i))
                    if t % 2 == 1:
                        load.append(("V", i // 2))
                if 1 <= t <= TB:
                    load.append(("QN", i - 1))
                if t >= 2:
                    load.append(("TQK", i - 2))
        if b > 0:
            for n in range(16 + 2):
                m = (b - 1) * 16 + n
                if n < 16:
                    attend.append(("ST", m))
                if n >= 2:
                    attend.append(("AV", m - 2))
                    if (m - 2) % 8 == 7:
                        g = (m - 2) // 8
                        attend += [("LN1", 4 * g + t) for t in range(4)]
                        attend += [("LN1B", 4 * g + t) for t in range(4)]
        n = max(len(load), len(attend))
        done = [0, 0]
        for k in range(1, n + 1):
            for w, seq in enumerate((load, attend)):
                upto = len(seq) * k // n
                order += seq[done[w]:upto]
                done[w] = upto
    return order


def cross_attention_order():
    order = []
    for s in range(-1, NJ + 2):
        j = s + 1
        if j < NJ and j % 4 == 0:
            order += [("KB", j // 4), ("VB", j // 4)]
        if j < NJ:
            order.append(("TX", j))
        if 0 <= s < NJ:
            order.append(("XS", 2 * s))
        if s >= 1 and 2 * s - 1 <= NT:
            order.append(("SM", 2 * s - 1))
            order += [("TP", 3 * (2 * s - 2) + u) for u in range(3)]
        if j < NJ:
            order.append(("XQ", j))
        if 0 <= s < NJ:
            order.append(("XS", 2 * s + 1))
            order.append(("SM", 2 * s))
        if 1 <= s <= NJ:
            order += [("TP", 3 * (2 * s - 1) + u) for u in range(3)]
            order.append(("PV", s - 1))
        if s >= 2:
            order.append(("XD", s - 2))
            order.append(("LN2B", s - 2))
    return order


def channel_mix_order():
    order = []
    for s in range(NJ + 3):
        if s < NJ:
            order.append(("TY", s))
        if 1 <= s <= NJ:
            order.append(("FR", s - 1))
            order.append(("FK", s - 1))
        if 2 <= s <= NJ + 1:
            order.append(("FV", s - 2))
        if s >= 3:
            order.append(("LN3B", s - 3))
    return order


def decoder_layer(nc, io):
    ctx = ExitStack()
    with ctx:
        def sem(name):
            return ctx.enter_context(nc.semaphore(name))

        def tensor(stack, name, shape, dt=F32):
            return stack.enter_context(nc.sbuf_tensor(name, shape, dt))

        big = ctx.enter_context(nc.psum_tensor("big", [P, 3 * BANK], F32))
        ring = ctx.enter_context(nc.psum_tensor("ring", [P, RING, BANK], F32))
        acc = big[:, 0:2 * BANK].rearrange("p (t d) -> p t d", d=D)
        logits = big[:, S0:S0 + PW]

        xs = tensor(ctx, "xs", [P, NT, D])
        ident = tensor(ctx, "ident", [P, P])
        consts = tensor(ctx, "consts", [P, 4])
        nlogs = tensor(ctx, "nlogs", [P, 1])
        eps2, half2 = consts[:, 0:2], consts[:, 2:4]

        names = {
            "XT.dma0": 16, "XT.dma1": 16, "XT.act": 1, "XT.pool": 1, "QK.pe": 1, "QK.dve": 5, "QK.pool": 2,
            "QN.dve": 2, "TQK.pe": 1, "TQK.act": 1, "TQK.dve": 1, "V.pe": 1, "V.dve": 1,
            "V.act": 1, "V.pool": 1, "ST.pe": 1, "ST.act": 2, "ST.dve": 1, "AV.pe": 1,
            "LN1.dve": 3, "LN1.pool": 2, "LN1B.dve": 1, "XS0.dma": 16, "XB.pool": 1,
            "KB.pool": 4, "KB.act": 2, "VB.pe": 4, "VB.dve": 5, "VB.act": 4, "VB.pool": 3,
            "TX.pe": 1, "TX.act": 1, "TX.dve": 1, "XR.pool": 1, "XQ.pe": 1, "XQ.act": 2,
            "XQ.dve": 2, "XS.pe": 1, "XS.dve": 2, "XS.act": 1, "SM.dve": 2, "SM.pool": 1,
            "TP.pe": 1, "TP.act": 1, "TP.dve": 1, "PV.pe": 1, "PV.act": 1, "PV.dve": 1,
            "XD.pe": 1, "XD.dve": 5, "XD.pool": 2, "LN2B.dve": 2,
            "TY.pe": 1, "TY.act": 1, "TY.pool": 2, "TY.dve": 5, "TY.hi": 1,
            "FR.pe": 1, "FR.act": 1, "FK.pe": 1, "FK.act": 2, "FK.dve": 2,
            "FV.pe": 1, "FV.dve": 6, "FV.pool": 2, "LN3B.dve": 2, "OUT.dma0": 16, "OUT.dma1": 16,
        }
        c = {name: Count(sem("s_" + name.replace(".", "_")), per) for name, per in names.items()}
        load_id, load1, load2, load3 = (sem(n) for n in ("load_id", "load1", "load2", "load3"))
        pre = {e: Count(sem("pre_" + e)) for e in ("pe", "act", "dve", "pool")}
        made = {e: 0 for e in pre}

        order1, order2, order3 = self_attention_order(), cross_attention_order(), channel_mix_order()
        let_go = {
            "QK": lambda i: c["QK.dve"].at(i, 1), "TQK": c["TQK.dve"].at, "V": c["V.dve"].at,
            "ST": lambda n: c["ST.act"].at(n, 1),
            "VB": lambda q: c["VB.dve"].at(q // 4, (1, 3, 4, 5)[q % 4]),
            "TX": c["TX.dve"].at, "XQ": c["XQ.dve"].at, "TP": c["TP.dve"].at, "PV": c["PV.dve"].at,
            "XD": lambda j: c["XD.dve"].at(j, 1), "TY": c["TY.act"].at, "FR": c["FR.act"].at,
            "FK": lambda j: c["FK.act"].at(j, 1), "FV": lambda j: c["FV.dve"].at(j, 1),
        }
        takers = []
        for kind, i in order1 + order2 + order3:
            if kind == "VB":
                takers += [("VB", 4 * i + q) for q in range(4)]
            elif kind in let_go:
                takers.append((kind, i))
        place = {step: n for n, step in enumerate(takers)}

        def bank(kind, i):
            return ring[:, place[kind, i] % RING, :]

        def bank_free(w, kind, i):
            n = place[kind, i]
            if n >= RING:
                k, m = takers[n - RING]
                w(let_go[k](m))

        def split_product(eng, out, stationary, moving, first=True, last=True, check=True):
            n = len(stationary)
            for k in range(n):
                (sh, sl), (mh, ml) = stationary[k], moving[k]
                for q, (s_, m_) in enumerate(((sh, mh), (sh, ml), (sl, mh))):
                    mm = eng.matmul(out, s_, m_, start=first and k == 0 and q == 0,
                                    stop=last and k == n - 1 and q == 2, skip_group_check=not check)
            return mm

        def hi_lo(pair, *at):
            return tuple(t[at] for t in pair)

        def f(ap):
            return ap.bitcast(F32)

        with ExitStack() as ph:
            wraw = tensor(ph, "wraw", [P, KC, 2 * D])
            w_qk = (tensor(ph, "wqk_hi", [P, KC, 2 * D], F32R), tensor(ph, "wqk_lo", [P, KC, 2 * D], F32R))
            wv_raw = tensor(ph, "wv_raw", [P, KC, D])
            wo_ls = tensor(ph, "wo_ls", [P, KC, D])
            w_vo = (tensor(ph, "wvo_hi", [P, KC, D], F32R), tensor(ph, "wvo_lo", [P, KC, D], F32R))
            bqk = tensor(ph, "bqk", [P, 2 * D])
            bvcol = tensor(ph, "bvcol", [P, KC])
            bvwide = tensor(ph, "bvwide", [P, KC, P])
            bvo = tensor(ph, "bvo", [P, D])
            bo = tensor(ph, "bo", [P, D])
            ls = tensor(ph, "ls", [P, D])
            xraw = tensor(ph, "xraw", [P, 2, KC, 2 * P])
            xT = (tensor(ph, "xT_hi", [P, 2, KC, 2 * P], F32R), tensor(ph, "xT_lo", [P, 2, KC, 2 * P], F32R))
            qk_sb = tensor(ph, "qk_sb", [P, 4, 2 * D])
            st1 = tensor(ph, "st1", [P, 4, 2, 6])
            mv1 = tensor(ph, "mv1", [P, 4, 2, 2])
            rs1 = tensor(ph, "rs1", [P, 4, 2])
            qkT = (tensor(ph, "qkT_hi", [P, 2, 4, S], F32R), tensor(ph, "qkT_lo", [P, 2, 4, S], F32R))
            v_sb = tensor(ph, "v_sb", [P, 2, 2 * D])
            vv = (tensor(ph, "v_hi", [P, 2, TB, D], F32R), tensor(ph, "v_lo", [P, 2, TB, D], F32R))
            NA = 3
            a_sb = tensor(ph, "a_sb", [P, NA, BANK])
            aT = (tensor(ph, "aT_hi", [P, NA, BANK], F32R), tensor(ph, "aT_lo", [P, NA, BANK], F32R))
            stl = tensor(ph, "stl", [P, 4, 6])
            mvl = tensor(ph, "mvl", [P, 4, 2])
            rsl = tensor(ph, "rsl", [P, 4])

            def bc(name, n=D):
                return io[name].rearrange("(o n) -> o n", o=1).to_broadcast([P, n])

            def col(name):
                return io[name]

            def rows(name):
                return io[name].rearrange("(k p) n -> p k n", p=P)

            xT_dram = rows("xT")
            x_dram = io["x"].rearrange("(i p) d -> p i d", p=P)
            NLOAD1 = 9 * 16
            PRE_WLO, PRE_WOLS, PRE_BVW, PRE_BO, PRE_VLO, PRE_BVO = range(1, 7)

            with nc.Block() as block:
                @block.sync
                def _(sp):
                    w = Waiter(sp)
                    sp.dma_start(wraw[:, :, 0:D], rows("wqT")).then_inc(load1, 16)
                    sp.dma_start(wraw[:, :, D:2 * D], rows("wkT")).then_inc(load1, 16)
                    for kind, i in order1:
                        if kind == "XT":
                            if i >= 2:
                                w(c["XT.pool"].at(i - 2))
                            sp.dma_start(xraw[:, i % 2], xT_dram[:, :, i * 2 * P:(i + 1) * 2 * P])\
                                .then_inc(c[f"XT.dma{i % 2}"].sem, 16)
                        if (kind, i) == ("XT", 1):
                            for g in range(NG):
                                sp.dma_start(xs[:, 4 * g:4 * g + 4, :], x_dram[:, 4 * g:4 * g + 4, :])\
                                    .then_inc(c["XS0.dma"].sem, 16)

                @block.scalar
                def _(act):
                    w = Waiter(act)
                    act.dma_start(wv_raw[:], rows("wv")).then_inc(load1, 16)
                    act.dma_start(wo_ls[:], rows("woT")).then_inc(load1, 16)
                    act.dma_start(ls[:], bc("ls")).then_inc(load1, 16)
                    act.dma_start(bvcol[:], col("bv")).then_inc(load1, 16)
                    act.dma_start(bqk[:, 0:D], bc("bq")).then_inc(load1, 16)
                    act.dma_start(bqk[:, D:2 * D], bc("bk")).then_inc(load1, 16)
                    act.dma_start(bo[:], bc("bo")).then_inc(load1, 16)
                    act.dma_start(ident[:], io["ident"]).then_inc(load_id, 16)
                    pre_done = False
                    for kind, i in order1:
                        if kind == "XT":
                            w(c[f"XT.dma{i % 2}"].at(i // 2))
                            if i >= 2:
                                w(c["QK.pe"].at(2 * (i - 2) + 1), c["V.pe"].at(i - 2))
                            act.activation(xT[0][:, i % 2], xraw[:, i % 2], ACT.Identity)\
                                .then_inc(c["XT.act"].sem, 1)
                            if not pre_done:
                                w(pre["pe"].at(0))
                                act.activation(w_vo[0][:].rearrange("p k d -> p (k d)"), big[:, 0:2 * D],
                                               ACT.Identity).then_inc(pre["act"].sem, 1)
                                pre_done = True
                        elif kind == "TQK":
                            b, t = divmod(i, TB)
                            w(c["TQK.pe"].at(i))
                            if b >= 2:
                                w(c["ST.pe"].at(16 * (b - 1) - 1))
                            act.activation(qkT[0][:, b % 2, :, t * P:(t + 1) * P],
                                           bank("TQK", i).rearrange("p (m t) -> p m t", m=4),
                                           ACT.Identity).then_inc(c["TQK.act"].sem, 1)
                        elif kind == "V":
                            b, t = divmod(i, TB // 2)
                            w(c["V.dve"].at(i))
                            if b >= 2:
                                w(c["AV.pe"].at(16 * (b - 1) - 1))
                            act.activation(vv[0][:, b % 2, 2 * t:2 * t + 2, :].rearrange("p t d -> p (t d)"),
                                           v_sb[:, i % 2], ACT.Identity).then_inc(c["V.act"].sem, 1)
                        elif kind == "ST":
                            w(c["ST.pe"].at(i))
                            if i >= NA:
                                w(c["ST.dve"].at(i - NA), c["AV.pe"].at(i - NA))
                            if i == 0:
                                w(pre["pool"].at(0))
                            act.activation(a_sb[:, i % NA], bank("ST", i), ACT.Sigmoid,
                                           bias=nlogs[:, 0:1], scale=1.0 / 16).then_inc(c["ST.act"].sem, 1)
                            w(c["ST.act"].at(i, 1))
                            act.activation(aT[0][:, i % NA], a_sb[:, i % NA], ACT.Identity)\
                                .then_inc(c["ST.act"].sem, 1)

                @block.gpsimd
                def _(pool):
                    w = Waiter(pool)
                    pool.memset(nlogs[:], -float(np.log(np.float32(S))))
                    pool.memset(consts[:, 0:2], EPS)
                    pool.memset(consts[:, 2:4], -0.5).then_inc(pre["pool"].sem, 1)
                    w(pre["pool"].at(0))
                    first = True
                    for kind, i in order1:
                        if kind == "XT":
                            w(c["XT.act"].at(i))
                            if i >= 2:
                                w(c["QK.pe"].at(2 * (i - 2) + 1), c["V.pe"].at(i - 2))
                            pool.tensor_tensor(xT[1][:, i % 2], xraw[:, i % 2], f(xT[0][:, i % 2]),
                                               ALU.subtract).then_inc(c["XT.pool"].sem, 1)
                        elif kind == "QK":
                            w(c["QK.dve"].at(i))
                            if i >= 4:
                                w(c["QN.dve"].at(i - 4))
                            r = rs1[:, i % 4]
                            pool.tensor_tensor(r, mv1[:, i % 4, :, 1], eps2, ALU.add)\
                                .then_inc(c["QK.pool"].sem, 1)
                            w(c["QK.pool"].at(i, 1))
                            pool.tensor_tensor(r, r, half2, ALU.pow).then_inc(c["QK.pool"].sem, 1)
                        elif kind == "V":
                            b, t = divmod(i, TB // 2)
                            w(c["V.act"].at(i))
                            if b >= 2:
                                w(c["AV.pe"].at(16 * (b - 1) - 1))
                            pool.tensor_tensor(vv[1][:, b % 2, 2 * t:2 * t + 2, :].rearrange("p t d -> p (t d)"),
                                               v_sb[:, i % 2],
                                               f(vv[0][:, b % 2, 2 * t:2 * t + 2, :].rearrange("p t d -> p (t d)")),
                                               ALU.subtract).then_inc(c["V.pool"].sem, 1)
                        elif kind == "ST" and i % 8 == 0:
                            g = i // 8
                            w(c["XS0.dma"].at(NG - 1), pre["dve"].at(PRE_BO))
                            pool.tensor_tensor(xs[:, 4 * g:4 * g + 4, :], xs[:, 4 * g:4 * g + 4, :],
                                               bo[:].rearrange("p (o d) -> p o d", o=1).to_broadcast([P, 4, D]),
                                               ALU.add).then_inc(c["XB.pool"].sem, 1)
                        elif kind == "LN1":
                            w(c["LN1.dve"].at(i))
                            if i >= 4:
                                w(c["LN1B.dve"].at(i - 4))
                            r = rsl[:, i % 4:i % 4 + 1]
                            pool.tensor_tensor(r, mvl[:, i % 4, 1:2], eps2[:, 0:1], ALU.add)\
                                .then_inc(c["LN1.pool"].sem, 1)
                            w(c["LN1.pool"].at(i, 1))
                            pool.tensor_tensor(r, r, half2[:, 0:1], ALU.pow).then_inc(c["LN1.pool"].sem, 1)

                @block.vector
                def _(dve):
                    w = Waiter(dve)
                    d = pre["dve"].sem
                    w((load1, NLOAD1))
                    dve.tensor_copy(w_qk[0][:], wraw[:]).then_inc(d, 1)
                    w((d, 1))
                    dve.tensor_tensor(w_qk[1][:], wraw[:], f(w_qk[0][:]), ALU.subtract).then_inc(d, 1)
                    dve.tensor_tensor(wo_ls[:], wo_ls[:],
                                      ls[:].rearrange("p (o d) -> p o d", o=1).to_broadcast([P, KC, D]),
                                      ALU.mult).then_inc(d, 1)
                    dve.tensor_copy(bvwide[:], bvcol[:].rearrange("p (k o) -> p k o", o=1)
                                    .to_broadcast([P, KC, P])).then_inc(d, 1)
                    dve.tensor_tensor(bo[:], bo[:], ls[:], ALU.mult).then_inc(d, 1)
                    w(pre["act"].at(0))
                    dve.tensor_tensor(w_vo[1][:].rearrange("p k d -> p (k d)"), big[:, 0:2 * D],
                                      f(w_vo[0][:].rearrange("p k d -> p (k d)")), ALU.subtract).then_inc(d, 1)
                    dve.tensor_copy(bvo[:], big[:, BANK:BANK + D]).then_inc(d, 1)
                    for kind, i in order1:
                        if kind == "QK":
                            w(c["QK.pe"].at(i))
                            if i >= 4:
                                w(c["TQK.pe"].at(i - 4))
                                w(c["QK.pool"].at(i - 4))
                            dve.tensor_tensor(qk_sb[:, i % 4], bank("QK", i), bqk[:], ALU.add)\
                                .then_inc(c["QK.dve"].sem, 1)
                            w(c["QK.dve"].at(i, 1))
                            for m in range(2):
                                dve.bn_stats(st1[:, i % 4, m], qk_sb[:, i % 4, m * D:(m + 1) * D])\
                                    .then_inc(c["QK.dve"].sem, 1)
                            for m in range(2):
                                w(c["QK.dve"].at(i, 2 + m))
                                dve.bn_aggr(mv1[:, i % 4, m], st1[:, i % 4, m]).then_inc(c["QK.dve"].sem, 1)
                        elif kind == "QN":
                            w(c["QK.pool"].at(i))
                            for m in range(2):
                                s_ = qk_sb[:, i % 4, m * D:(m + 1) * D]
                                dve.tensor_scalar(s_, s_, mv1[:, i % 4, m, 0:1], rs1[:, i % 4, m:m + 1],
                                                  ALU.subtract, ALU.mult).then_inc(c["QN.dve"].sem, 1)
                        elif kind == "TQK":
                            b, t = divmod(i, TB)
                            w(c["TQK.act"].at(i))
                            dve.tensor_tensor(qkT[1][:, b % 2, :, t * P:(t + 1) * P],
                                              bank("TQK", i).rearrange("p (m t) -> p m t", m=4),
                                              f(qkT[0][:, b % 2, :, t * P:(t + 1) * P]),
                                              ALU.subtract).then_inc(c["TQK.dve"].sem, 1)
                        elif kind == "V":
                            w(c["V.pe"].at(i))
                            if i >= 2:
                                w(c["V.pool"].at(i - 2))
                            if i == 0:
                                w(pre["dve"].at(PRE_BVO))
                            dve.tensor_tensor(v_sb[:, i % 2].rearrange("p (t d) -> p t d", t=2),
                                              bank("V", i).rearrange("p (t d) -> p t d", t=2),
                                              bvo[:].rearrange("p (o d) -> p o d", o=1).to_broadcast([P, 2, D]),
                                              ALU.add).then_inc(c["V.dve"].sem, 1)
                        elif kind == "ST":
                            w(c["ST.act"].at(i))
                            dve.tensor_tensor(aT[1][:, i % NA], a_sb[:, i % NA], f(aT[0][:, i % NA]),
                                              ALU.subtract).then_inc(c["ST.dve"].sem, 1)
                        elif kind == "LN1":
                            g, t = divmod(i, 4)
                            w(c["AV.pe"].at(8 * g + 7), c["XB.pool"].at(g))
                            dve.tensor_tensor(xs[:, i], acc[:, t], xs[:, i], ALU.add)\
                                .then_inc(c["LN1.dve"].sem, 1)
                            w(c["LN1.dve"].at(i, 1))
                            dve.bn_stats(stl[:, t], xs[:, i]).then_inc(c["LN1.dve"].sem, 1)
                            w(c["LN1.dve"].at(i, 2))
                            if i >= 4:
                                w(c["LN1.pool"].at(i - 4))
                            dve.bn_aggr(mvl[:, t], stl[:, t]).then_inc(c["LN1.dve"].sem, 1)
                        elif kind == "LN1B":
                            t = i % 4
                            w(c["LN1.pool"].at(i))
                            dve.tensor_scalar(xs[:, i], xs[:, i], mvl[:, t, 0:1], rsl[:, t:t + 1],
                                              ALU.subtract, ALU.mult).then_inc(c["LN1B.dve"].sem, 1)

                @block.tensor
                def _(pe):
                    w = Waiter(pe)
                    w(pre["dve"].at(PRE_BVW))
                    for m in range(KC):
                        for e in range(KC):
                            pe.matmul(big[:, m * D:(m + 1) * D], wv_raw[:, e, m * P:(m + 1) * P], wo_ls[:, e, :],
                                      start=e == 0, stop=e == KC - 1)
                    for e in range(KC):
                        mm = pe.matmul(big[:, BANK:BANK + D], bvwide[:, e, :], wo_ls[:, e, :],
                                       start=e == 0, stop=e == KC - 1)
                    mm.then_inc(pre["pe"].sem, 1)
                    w((load_id, 16))
                    for kind, i in order1:
                        if kind in let_go:
                            bank_free(w, kind, i)
                        if kind == "QK":
                            j, t = divmod(i, 2)
                            w(c["XT.act"].at(j), c["XT.pool"].at(j))
                            split_product(pe, bank("QK", i),
                                          [hi_lo(xT, slice(None), j % 2, k, slice(t * P, (t + 1) * P)) for k in range(KC)],
                                          [hi_lo(w_qk, slice(None), k) for k in range(KC)])\
                                .then_inc(c["QK.pe"].sem, 1)
                        elif kind == "V":
                            w(pre["dve"].at(PRE_VLO))
                            for t in range(2):
                                mm = split_product(pe, bank("V", i)[:, t * D:(t + 1) * D],
                                                   [hi_lo(xT, slice(None), i % 2, k, slice(t * P, (t + 1) * P)) for k in range(KC)],
                                                   [hi_lo(w_vo, slice(None), k) for k in range(KC)])
                            mm.then_inc(c["V.pe"].sem, 1)
                        elif kind == "TQK":
                            w(c["QN.dve"].at(i))
                            for m in range(4):
                                mm = pe.transpose(bank("TQK", i)[:, m * P:(m + 1) * P],
                                                  qk_sb[:, i % 4, m * P:(m + 1) * P], ident[:])
                            mm.then_inc(c["TQK.pe"].sem, 1)
                        elif kind == "ST":
                            g, kt = divmod(i, TB)
                            b = g // 2
                            w(c["TQK.dve"].at(max(TB * b + kt, 4 * g + 3)))
                            q0 = (g % 2) * BANK
                            split_product(pe, bank("ST", i),
                                          [hi_lo(qkT, slice(None), b % 2, 2 + e, slice(kt * P, (kt + 1) * P)) for e in range(KC)],
                                          [hi_lo(qkT, slice(None), b % 2, e, slice(q0, q0 + BANK)) for e in range(KC)])\
                                .then_inc(c["ST.pe"].sem, 1)
                        elif kind == "AV":
                            g, kt = divmod(i, TB)
                            b = g // 2
                            w(c["ST.dve"].at(i), c["V.pool"].at(TB // 2 * b + kt // 2))
                            if kt == 0:
                                w(c["LN1.dve"].at(4 * g - 1, 1) if g else pre["dve"].at(PRE_BVO))
                            for t in range(4):
                                mm = split_product(pe, acc[:, t],
                                                   [hi_lo(aT, slice(None), i % NA, slice(t * P, (t + 1) * P))],
                                                   [hi_lo(vv, slice(None), b % 2, kt)],
                                                   first=kt == 0 and t % 2 == 0, last=kt == TB - 1, check=False)
                            mm.then_inc(c["AV.pe"].sem, 1)

        with ExitStack() as ph:
            wx_raw = tensor(ph, "wx_raw", [P, 4, KC, D])
            w_x = (tensor(ph, "wx_hi", [P, 2, KC, D], F32R), tensor(ph, "wx_lo", [P, 2, KC, D], F32R))
            cT = tensor(ph, "cT", [P, KC, B * SC])
            kT = tensor(ph, "kT", [P, KC, B * SC])
            mask_k = tensor(ph, "mask_k", [P, HC])
            mask_v = tensor(ph, "mask_v", [P, RV, P])
            sel_raw = tensor(ph, "sel_raw", [SC, RV * P])
            sel = tensor(ph, "sel", [SC, RV * P], F32R)
            bqcol = tensor(ph, "bqcol", [P, KC])
            bkcol = tensor(ph, "bkcol", [P, KC])
            bxv = tensor(ph, "bxv", [P, D])
            bxd = tensor(ph, "bxd", [P, D])
            kb32 = tensor(ph, "kb32", [P, W])
            kb = (tensor(ph, "kb_hi", [P, 2, KC, W], F32R), tensor(ph, "kb_lo", [P, 2, KC, W], F32R))
            v32 = tensor(ph, "v32", [SC, D])
            vc = (tensor(ph, "vc_hi", [SC, D], F32R), tensor(ph, "vc_lo", [SC, D], F32R))
            vm = tensor(ph, "vm", [P, 2, KC, P])
            vb = (tensor(ph, "vb_hi", [P, 2, RV, KC, P], F32R), tensor(ph, "vb_lo", [P, 2, RV, KC, P], F32R))
            x1T = (tensor(ph, "x1T_hi", [P, 2, BANK], F32R), tensor(ph, "x1T_lo", [P, 2, BANK], F32R))
            xqT = (tensor(ph, "xqT_hi", [P, 2, BANK], F32R), tensor(ph, "xqT_lo", [P, 2, BANK], F32R))
            NP = 3
            p_sb = tensor(ph, "p_sb", [P, NP, PPAD])
            mx = tensor(ph, "mx", [P, 2, H])
            sm = tensor(ph, "sm", [P, 2, H])
            rc = tensor(ph, "rc", [P, 2, H])
            pT = (tensor(ph, "pT_hi", [P, 2, 2 * RV, 2 * P], F32R), tensor(ph, "pT_lo", [P, 2, 2 * RV, 2 * P], F32R))
            oT = (tensor(ph, "oT_hi", [P, 2, BANK], F32R), tensor(ph, "oT_lo", [P, 2, BANK], F32R))
            st2 = tensor(ph, "st2", [P, 2, 2, 6])
            mv2 = tensor(ph, "mv2", [P, 2, 2, 2])
            rs2 = tensor(ph, "rs2", [P, 2, 2])
            XQW, XDW, XKW, XVW = range(4)
            NLOAD2 = 12 * 16
            pre2 = {e: Count(sem("pre2_" + e)) for e in ("pe", "act", "dve", "pool")}

            def heads(ap):
                return ap.rearrange("p (h k) -> p h k", k=SC)

            def per_head(ap):
                return ap.rearrange("p (h o) -> p h o", o=1).to_broadcast([P, H, SC])

            with nc.Block() as block:
                def phase1_over(w):
                    w(c["AV.pe"].at(16 * B - 1), c["TQK.dve"].at(NT - 1), c["ST.dve"].at(16 * B - 1),
                      c["V.pool"].at(NJ - 1), c["LN1B.dve"].at(NT - 1))

                @block.sync
                def _(sp):
                    w = Waiter(sp)
                    phase1_over(w)
                    for n, name in enumerate(("xwqT", "xwdT", "xwkT", "xwvT")):
                        sp.dma_start(wx_raw[:, n], rows(name)).then_inc(load2, 16)
                    sp.dma_start(cT[:], rows("cT")).then_inc(load2, 16)
                    sp.dma_start(mask_k[:], io["mask_k"]).then_inc(load2, 16)
                    sp.dma_start(mask_v[:], io["mask_v"]).then_inc(load2, 16)
                    sp.dma_start(sel_raw[:], io["sel"]).then_inc(load2, 16)
                    sp.dma_start(bqcol[:], col("xbq")).then_inc(load2, 16)
                    sp.dma_start(bkcol[:], col("xbk")).then_inc(load2, 16)
                    sp.dma_start(bxv[:], bc("xbv")).then_inc(load2, 16)
                    sp.dma_start(bxd[:], bc("xbd")).then_inc(load2, 16)

                @block.scalar
                def _(act):
                    w = Waiter(act)
                    phase1_over(w)
                    w((load2, NLOAD2), pre2["pe"].at(0))
                    for e in range(KC):
                        act.activation(kT[:, e, :], ring[:, e, 0:B * SC], ACT.Identity, bias=bkcol[:, e:e + 1])\
                            .then_inc(pre2["act"].sem, 1)
                    for kind, i in order2:
                        if kind == "KB":
                            for e in range(KC):
                                w(c["KB.pool"].at(i, 2 * e + 1))
                                if i >= 2:
                                    w(c["XS.pe"].at(TB * (i - 1) - 1))
                                act.activation(kb[0][:, i % 2, e, :], kb32[:], ACT.Identity)\
                                    .then_inc(c["KB.act"].sem, 1)
                        elif kind == "VB":
                            w(c["VB.dve"].at(i, 1))
                            if i >= 1:
                                w(c["VB.pe"].at(i - 1))
                            act.activation(vc[0][:], v32[:], ACT.Identity).then_inc(c["VB.act"].sem, 1)
                            for q in range(3):
                                r0, r1 = 2 * q, min(2 * q + 2, RV)
                                w(c["VB.dve"].at(i, 3 + q))
                                if i >= 2:
                                    w(c["PV.pe"].at(TB // 2 * (i - 1) - 1))
                                act.activation(vb[0][:, i % 2, r0:r1].rearrange("p r k d -> p (r k d)"),
                                               vm[:, 0:r1 - r0].rearrange("p r k d -> p (r k d)"), ACT.Identity)\
                                    .then_inc(c["VB.act"].sem, 1)
                        elif kind == "TX":
                            w(c["TX.pe"].at(i))
                            if i >= 2:
                                w(c["XQ.pe"].at(i - 2))
                            act.activation(x1T[0][:, i % 2], bank("TX", i), ACT.Identity)\
                                .then_inc(c["TX.act"].sem, 1)
                        elif kind == "XQ":
                            w(c["XQ.pe"].at(i))
                            if i >= 2:
                                w(c["XS.pe"].at(2 * (i - 2) + 1))
                            for e in range(KC):
                                cut = slice(e * D, (e + 1) * D)
                                act.activation(xqT[0][:, i % 2, cut], bank("XQ", i)[:, cut], ACT.Identity,
                                               bias=bqcol[:, e:e + 1]).then_inc(c["XQ.act"].sem, 1)
                        elif kind == "XS":
                            w(c["XS.dve"].at(i))
                            act.activation(p_sb[:, i % NP, 0:PW], p_sb[:, i % NP, 0:PW], ACT.Exp)\
                                .then_inc(c["XS.act"].sem, 1)
                        elif kind == "TP":
                            t, u = divmod(i, 3)
                            j, k0, k1 = t // 2, 4 * u, min(4 * u + 4, 2 * RV)
                            w(c["TP.pe"].at(i))
                            if j >= 2:
                                w(c["PV.pe"].at(j - 2))
                            half = slice((t % 2) * P, (t % 2 + 1) * P)
                            act.activation(pT[0][:, j % 2, k0:k1, half],
                                           bank("TP", i)[:, 0:(k1 - k0) * P].rearrange("p (k t) -> p k t", t=P),
                                           ACT.Identity).then_inc(c["TP.act"].sem, 1)
                        elif kind == "PV":
                            w(c["PV.pe"].at(i))
                            if i >= 2:
                                w(c["XD.pe"].at(i - 2))
                            act.activation(oT[0][:, i % 2], bank("PV", i), ACT.Identity)\
                                .then_inc(c["PV.act"].sem, 1)

                @block.gpsimd
                def _(pool):
                    w = Waiter(pool)
                    phase1_over(w)
                    for n in range(NP):
                        ms = pool.memset(p_sb[:, n, PW:PPAD], 0.0)
                    ms.then_inc(pre2["pool"].sem, 1)
                    w((load2, NLOAD2), pre2["act"].at(KC - 1))
                    for kind, i in order2:
                        if kind == "KB":
                            for e in range(KC):
                                w(c["KB.act"].at(i, e), c["KB.pool"].at(i, 2 * e))
                                pool.tensor_tensor(heads(kb32[:]),
                                                   kT[:, e, i * SC:(i + 1) * SC].rearrange("p (o k) -> p o k", o=1)
                                                   .to_broadcast([P, HC, SC]),
                                                   mask_k[:].rearrange("p (h o) -> p h o", o=1)
                                                   .to_broadcast([P, HC, SC]), ALU.mult)\
                                    .then_inc(c["KB.pool"].sem, 1)
                                w(c["KB.act"].at(i, e + 1))
                                pool.tensor_tensor(kb[1][:, i % 2, e, :], kb32[:], f(kb[0][:, i % 2, e, :]),
                                                   ALU.subtract).then_inc(c["KB.pool"].sem, 1)
                        elif kind == "VB":
                            for q in range(3):
                                r0, r1 = 2 * q, min(2 * q + 2, RV)
                                w(c["VB.act"].at(i, 2 + q))
                                pool.tensor_tensor(vb[1][:, i % 2, r0:r1].rearrange("p r k d -> p (r k d)"),
                                                   vm[:, 0:r1 - r0].rearrange("p r k d -> p (r k d)"),
                                                   f(vb[0][:, i % 2, r0:r1].rearrange("p r k d -> p (r k d)")),
                                                   ALU.subtract).then_inc(c["VB.pool"].sem, 1)
                        elif kind == "XQ":
                            w(c["TX.pe"].at(i))
                            pool.tensor_tensor(xs[:, 2 * i:2 * i + 2, :], xs[:, 2 * i:2 * i + 2, :],
                                               bxd[:].rearrange("p (o d) -> p o d", o=1).to_broadcast([P, 2, D]),
                                               ALU.add).then_inc(c["XR.pool"].sem, 1)
                        elif kind == "SM":
                            w(c["SM.dve"].at(i))
                            pool.tensor_tensor(heads(p_sb[:, i % NP, 0:PW]), heads(p_sb[:, i % NP, 0:PW]),
                                               per_head(rc[:, i % 2]), ALU.mult).then_inc(c["SM.pool"].sem, 1)
                        elif kind == "XD":
                            w(c["XD.dve"].at(i))
                            if i >= 2:
                                w(c["LN2B.dve"].at(i - 2))
                            r = rs2[:, i % 2]
                            pool.tensor_tensor(r, mv2[:, i % 2, :, 1], eps2, ALU.add)\
                                .then_inc(c["XD.pool"].sem, 1)
                            w(c["XD.pool"].at(i, 1))
                            pool.tensor_tensor(r, r, half2, ALU.pow).then_inc(c["XD.pool"].sem, 1)

                @block.vector
                def _(dve):
                    w = Waiter(dve)
                    phase1_over(w)
                    w((load2, NLOAD2))
                    dve.tensor_copy(w_x[0][:], wx_raw[:, 0:2]).then_inc(pre2["dve"].sem, 1)
                    w(pre2["dve"].at(0))
                    dve.tensor_tensor(w_x[1][:].rearrange("p m k d -> p (m k d)"),
                                      wx_raw[:, 0:2].rearrange("p m k d -> p (m k d)"),
                                      f(w_x[0][:].rearrange("p m k d -> p (m k d)")), ALU.subtract)\
                        .then_inc(pre2["dve"].sem, 1)
                    dve.tensor_copy(sel[:], sel_raw[:]).then_inc(pre2["dve"].sem, 1)
                    for kind, i in order2:
                        if kind == "VB":
                            w(c["VB.pe"].at(i, 1))
                            if i >= 1:
                                w(c["VB.act"].at(i - 1, 1))
                            dve.tensor_tensor(v32[:], bank("VB", 4 * i)[0:SC, 0:D], bxv[0:SC, :], ALU.add)\
                                .then_inc(c["VB.dve"].sem, 1)
                            w(c["VB.act"].at(i, 1))
                            if i >= 1:
                                w(c["VB.pe"].at(i - 1))
                            dve.tensor_tensor(vc[1][:], v32[:], f(vc[0][:]), ALU.subtract)\
                                .then_inc(c["VB.dve"].sem, 1)
                            for q in range(3):
                                r0, r1 = 2 * q, min(2 * q + 2, RV)
                                w(c["VB.pe"].at(i, 2 + q))
                                if q or i:
                                    w(c["VB.pool"].at(i, q))
                                dve.tensor_tensor(vm[:, 0:r1 - r0],
                                                  bank("VB", 4 * i + 1 + q)[:, 0:(r1 - r0) * D]
                                                  .rearrange("p (r k d) -> p r k d", k=KC, d=P),
                                                  mask_v[:, r0:r1].rearrange("p r (o d) -> p r o d", o=1)
                                                  .to_broadcast([P, r1 - r0, KC, P]), ALU.mult)\
                                    .then_inc(c["VB.dve"].sem, 1)
                        elif kind == "TX":
                            w(c["TX.act"].at(i))
                            dve.tensor_tensor(x1T[1][:, i % 2], bank("TX", i), f(x1T[0][:, i % 2]), ALU.subtract)\
                                .then_inc(c["TX.dve"].sem, 1)
                        elif kind == "XQ":
                            for e in range(KC):
                                cut = slice(e * D, (e + 1) * D)
                                w(c["XQ.act"].at(i))
                                dve.scalar_tensor_tensor(out=xqT[1][:, i % 2, cut], in0=bank("XQ", i)[:, cut],
                                                         scalar=bqcol[:, e:e + 1], in1=f(xqT[0][:, i % 2, cut]),
                                                         op0=ALU.add, op1=ALU.subtract)\
                                    .then_inc(c["XQ.dve"].sem, 1)
                        elif kind == "XS":
                            w(c["XS.pe"].at(i))
                            dve.tensor_reduce(mx[:, i % 2], heads(logits), AX, ALU.max)\
                                .then_inc(c["XS.dve"].sem, 1)
                            w(c["XS.dve"].at(i, 1))
                            if i >= NP:
                                w(c["TP.pe"].at(3 * (i - NP) + 2))
                            dve.tensor_tensor(heads(p_sb[:, i % NP, 0:PW]), heads(logits), per_head(mx[:, i % 2]),
                                              ALU.subtract).then_inc(c["XS.dve"].sem, 1)
                        elif kind == "SM":
                            w(c["XS.act"].at(i))
                            dve.tensor_reduce(sm[:, i % 2], heads(p_sb[:, i % NP, 0:PW]), AX, ALU.add)\
                                .then_inc(c["SM.dve"].sem, 1)
                            w(c["SM.dve"].at(i, 1))
                            if i >= 2:
                                w(c["SM.pool"].at(i - 2))
                            dve.reciprocal(rc[:, i % 2], sm[:, i % 2]).then_inc(c["SM.dve"].sem, 1)
                        elif kind == "TP":
                            t, u = divmod(i, 3)
                            j, k0, k1 = t // 2, 4 * u, min(4 * u + 4, 2 * RV)
                            half = slice((t % 2) * P, (t % 2 + 1) * P)
                            w(c["TP.act"].at(i))
                            dve.tensor_tensor(pT[1][:, j % 2, k0:k1, half],
                                              bank("TP", i)[:, 0:(k1 - k0) * P].rearrange("p (k t) -> p k t", t=P),
                                              f(pT[0][:, j % 2, k0:k1, half]), ALU.subtract)\
                                .then_inc(c["TP.dve"].sem, 1)
                        elif kind == "PV":
                            w(c["PV.act"].at(i))
                            dve.tensor_tensor(oT[1][:, i % 2], bank("PV", i), f(oT[0][:, i % 2]), ALU.subtract)\
                                .then_inc(c["PV.dve"].sem, 1)
                        elif kind == "XD":
                            w(c["XD.pe"].at(i), c["XR.pool"].at(i))
                            x2 = xs[:, 2 * i:2 * i + 2, :]
                            dve.tensor_tensor(x2, bank("XD", i).rearrange("p (t d) -> p t d", t=2), x2, ALU.add)\
                                .then_inc(c["XD.dve"].sem, 1)
                            w(c["XD.dve"].at(i, 1))
                            for t in range(2):
                                dve.bn_stats(st2[:, i % 2, t], xs[:, 2 * i + t]).then_inc(c["XD.dve"].sem, 1)
                            if i >= 2:
                                w(c["XD.pool"].at(i - 2))
                            for t in range(2):
                                w(c["XD.dve"].at(i, 2 + t))
                                dve.bn_aggr(mv2[:, i % 2, t], st2[:, i % 2, t]).then_inc(c["XD.dve"].sem, 1)
                        elif kind == "LN2B":
                            w(c["XD.pool"].at(i))
                            for t in range(2):
                                x2 = xs[:, 2 * i + t]
                                dve.tensor_scalar(x2, x2, mv2[:, i % 2, t, 0:1], rs2[:, i % 2, t:t + 1],
                                                  ALU.subtract, ALU.mult).then_inc(c["LN2B.dve"].sem, 1)

                @block.tensor
                def _(pe):
                    w = Waiter(pe)
                    phase1_over(w)
                    w((load2, NLOAD2))
                    for e in range(KC):
                        for k in range(KC):
                            mm = pe.matmul(ring[:, e, 0:B * SC], wx_raw[:, XKW, k, e * P:(e + 1) * P], cT[:, k, :],
                                           start=k == 0, stop=k == KC - 1)
                    mm.then_inc(pre2["pe"].sem, 1)
                    w(pre2["dve"].at(2), pre2["act"].at(KC - 1), pre2["pool"].at(0))
                    for kind, i in order2:
                        if kind in let_go and kind != "VB":
                            bank_free(w, kind, i)
                        if kind == "VB":
                            bank_free(w, "VB", 4 * i)
                            for k in range(KC):
                                mm = pe.matmul(bank("VB", 4 * i)[0:SC, 0:D], cT[:, k, i * SC:(i + 1) * SC],
                                               wx_raw[:, XVW, k, :], start=k == 0, stop=k == KC - 1)
                            mm.then_inc(c["VB.pe"].sem, 1)
                            w(c["VB.dve"].at(i, 2))
                            for q in range(3):
                                bank_free(w, "VB", 4 * i + 1 + q)
                                for r in range(2 * q, min(2 * q + 2, RV)):
                                    for n in range(2):
                                        mm = pe.matmul(bank("VB", 4 * i + 1 + q)[:, (r % 2) * D:(r % 2 + 1) * D],
                                                       sel[:, r * P:(r + 1) * P], vc[n][:], start=n == 0, stop=n == 1)
                                mm.then_inc(c["VB.pe"].sem, 1)
                        elif kind == "TX":
                            for k in range(KC):
                                for t in range(2):
                                    mm = pe.transpose(bank("TX", i)[:, k * D + t * P:k * D + (t + 1) * P],
                                                      xs[:, 2 * i + t, k * P:(k + 1) * P], ident[:])
                            mm.then_inc(c["TX.pe"].sem, 1)
                        elif kind == "XQ":
                            w(c["TX.dve"].at(i))
                            for e in range(KC):
                                mm = split_product(pe, bank("XQ", i)[:, e * D:(e + 1) * D],
                                                   [hi_lo(w_x, slice(None), XQW, k, slice(e * P, (e + 1) * P)) for k in range(KC)],
                                                   [hi_lo(x1T, slice(None), i % 2, slice(k * D, (k + 1) * D)) for k in range(KC)])
                            mm.then_inc(c["XQ.pe"].sem, 1)
                        elif kind == "XS":
                            j, t = divmod(i, 2)
                            b = i // TB
                            w(c["XQ.dve"].at(j), c["KB.pool"].at(b))
                            if i:
                                w(c["XS.dve"].at(i - 1))
                            for part, lo, hi in LOGIT_CUTS:
                                mm = split_product(pe, logits[:, part * W + lo:part * W + hi],
                                                   [hi_lo(xqT, slice(None), j % 2, slice(part * D + t * P, part * D + (t + 1) * P))],
                                                   [hi_lo(kb, slice(None), b % 2, part, slice(lo, hi))])
                            mm.then_inc(c["XS.pe"].sem, 1)
                        elif kind == "TP":
                            t, u = divmod(i, 3)
                            w(c["SM.pool"].at(t))
                            for k in range(4 * u, min(4 * u + 4, 2 * RV)):
                                c0 = (k // RV) * W + (k % RV) * P
                                mm = pe.transpose(bank("TP", i)[:, (k % 4) * P:(k % 4 + 1) * P],
                                                  p_sb[:, t % NP, c0:c0 + P], ident[:])
                            mm.then_inc(c["TP.pe"].sem, 1)
                        elif kind == "PV":
                            b = i // (TB // 2)
                            w(c["TP.dve"].at(3 * (2 * i + 1) + 2), c["VB.pool"].at(b))
                            for k in range(KC):
                                mm = split_product(pe, bank("PV", i)[:, k * D:(k + 1) * D],
                                                   [hi_lo(vb, slice(None), b % 2, r, k) for r in range(RV)],
                                                   [hi_lo(pT, slice(None), i % 2, k * RV + r) for r in range(RV)])
                            mm.then_inc(c["PV.pe"].sem, 1)
                        elif kind == "XD":
                            w(c["PV.dve"].at(i))
                            for t in range(2):
                                mm = split_product(pe, bank("XD", i)[:, t * D:(t + 1) * D],
                                                   [hi_lo(oT, slice(None), i % 2, slice(k * D + t * P, k * D + (t + 1) * P)) for k in range(KC)],
                                                   [hi_lo(w_x, slice(None), XDW, k) for k in range(KC)])
                            mm.then_inc(c["XD.pe"].sem, 1)

        with ExitStack() as ph:
            wf_raw = tensor(ph, "wf_raw", [P, 3, KC, D])
            w_f = (tensor(ph, "wf_hi", [P, 3, KC, D], F32R), tensor(ph, "wf_lo", [P, 3, KC, D], F32R))
            mu = tensor(ph, "mu", [P, 2, KC])
            x2T = tensor(ph, "x2T", [P, 2, KC, 2 * P + 1])
            dd = tensor(ph, "dd", [P, 2, KC, 2 * P])
            xm = tensor(ph, "xm", [P, 2, 2, KC, 2 * P])
            xmT = (tensor(ph, "xmT_hi", [P, 2, 2, KC, 2 * P], F32R), tensor(ph, "xmT_lo", [P, 2, 2, KC, 2 * P], F32R))
            gate = tensor(ph, "gate", [P, 2, 2 * D])
            kr = tensor(ph, "kr", [P, 2, BANK])
            kk = tensor(ph, "kk", [P, 2, BANK])
            kkT = (tensor(ph, "kkT_hi", [P, 2, BANK], F32R), tensor(ph, "kkT_lo", [P, 2, BANK], F32R))
            st3 = tensor(ph, "st3", [P, 2, 2, 6])
            mv3 = tensor(ph, "mv3", [P, 2, 2, 2])
            rs3 = tensor(ph, "rs3", [P, 2, 2])
            y = tensor(ph, "y", [P, 2, 2, D])
            pre3 = Count(sem("pre3_dve"))
            NLOAD3 = 5 * 16
            MIX_R, MIX_K, VW = range(3)
            out_dram = io["out"].rearrange("(i p) d -> p i d", p=P)

            with nc.Block() as block:
                def phase2_over(w):
                    w(c["PV.pe"].at(NJ - 1), c["XD.pe"].at(NJ - 1), c["LN2B.dve"].at(NJ - 1),
                      c["XD.pool"].at(NJ - 1))

                @block.sync
                def _(sp):
                    w = Waiter(sp)
                    phase2_over(w)
                    for n, name in enumerate(("wrT", "wkcT", "wvcT")):
                        sp.dma_start(wf_raw[:, n], rows(name)).then_inc(load3, 16)
                    sp.dma_start(mu[:, 0], col("mu_r")).then_inc(load3, 16)
                    sp.dma_start(mu[:, 1], col("mu_k")).then_inc(load3, 16)
                    for kind, i in order3:
                        if kind == "LN3B":
                            w(c["LN3B.dve"].at(i))
                            sp.dma_start(out_dram[:, 2 * i:2 * i + 2, :], y[:, i % 2]).then_inc(c[f"OUT.dma{i % 2}"].sem, 16)
                    w(c["OUT.dma0"].at(NJ // 2 - 1), c["OUT.dma1"].at(NJ // 2 - 1))

                @block.scalar
                def _(act):
                    w = Waiter(act)
                    phase2_over(w)
                    for kind, i in order3:
                        if kind == "TY":
                            w(c["TY.pe"].at(i))
                            if i >= 2:
                                w(c["TY.dve"].at(i - 2), c["TY.pool"].at(i - 1))
                            act.activation(x2T[:, i % 2, :, 1:2 * P + 1],
                                           bank("TY", i).rearrange("p (k t) -> p k t", k=KC), ACT.Identity)\
                                .then_inc(c["TY.act"].sem, 1)
                            w(c["TY.dve"].at(i, 4))
                            if i >= 2:
                                w(c["FR.pe"].at(i - 2), c["FK.pe"].at(i - 2))
                            act.activation(xmT[0][:, i % 2].rearrange("p m k t -> p (m k t)"),
                                           xm[:, i % 2].rearrange("p m k t -> p (m k t)"), ACT.Identity)\
                                .then_inc(c["TY.hi"].sem, 1)
                        elif kind == "FR":
                            w(c["FR.pe"].at(i))
                            if i >= 2:
                                w(c["FV.dve"].at(i - 2, 1))
                            act.activation(gate[:, i % 2], bank("FR", i), ACT.Sigmoid).then_inc(c["FR.act"].sem, 1)
                        elif kind == "FK":
                            w(c["FK.pe"].at(i))
                            if i >= 2:
                                w(c["FK.dve"].at(i - 2))
                            act.activation(kr[:, i % 2], bank("FK", i), ACT.Relu).then_inc(c["FK.act"].sem, 1)
                            w(c["FK.dve"].at(i, 1))
                            if i >= 2:
                                w(c["FV.pe"].at(i - 2))
                            act.activation(kkT[0][:, i % 2], kk[:, i % 2], ACT.Identity)\
                                .then_inc(c["FK.act"].sem, 1)

                @block.gpsimd
                def _(pool):
                    w = Waiter(pool)
                    phase2_over(w)
                    for kind, i in order3:
                        if kind == "TY":
                            if i >= 2:
                                w(c["TY.dve"].at(i - 2))
                            if i % (TB // 2) == 0:
                                pool.memset(x2T[:, i % 2, :, 0:1], 0.0).then_inc(c["TY.pool"].sem, 1)
                            else:
                                w(c["TY.act"].at(i - 1))
                                pool.tensor_copy(x2T[:, i % 2, :, 0:1], x2T[:, (i - 1) % 2, :, 2 * P:2 * P + 1])\
                                    .then_inc(c["TY.pool"].sem, 1)
                            w(c["TY.act"].at(i), c["TY.pool"].at(i, 1))
                            pool.tensor_tensor(dd[:, i % 2], x2T[:, i % 2, :, 1:2 * P + 1], x2T[:, i % 2, :, 0:2 * P],
                                               ALU.subtract).then_inc(c["TY.pool"].sem, 1)
                        elif kind == "FV":
                            w(c["FV.dve"].at(i))
                            if i >= 2:
                                w(c["LN3B.dve"].at(i - 2))
                            r = rs3[:, i % 2]
                            pool.tensor_tensor(r, mv3[:, i % 2, :, 1], eps2, ALU.add).then_inc(c["FV.pool"].sem, 1)
                            w(c["FV.pool"].at(i, 1))
                            pool.tensor_tensor(r, r, half2, ALU.pow).then_inc(c["FV.pool"].sem, 1)

                @block.vector
                def _(dve):
                    w = Waiter(dve)
                    phase2_over(w)
                    w((load3, NLOAD3))
                    flat = "p m k d -> p (m k d)"
                    dve.tensor_copy(w_f[0][:], wf_raw[:]).then_inc(pre3.sem, 1)
                    w(pre3.at(0))
                    dve.tensor_tensor(w_f[1][:].rearrange(flat), wf_raw[:].rearrange(flat),
                                      f(w_f[0][:].rearrange(flat)), ALU.subtract).then_inc(pre3.sem, 1)
                    for kind, i in order3:
                        if kind == "TY":
                            w(c["TY.pool"].at(i))
                            if i >= 2:
                                w(c["TY.hi"].at(i - 2))
                            for m in range(2):
                                for k in range(KC):
                                    dve.scalar_tensor_tensor(out=xm[:, i % 2, m, k], in0=dd[:, i % 2, k],
                                                             scalar=mu[:, m, k:k + 1], in1=x2T[:, i % 2, k, 0:2 * P],
                                                             op0=ALU.mult, op1=ALU.add)\
                                        .then_inc(c["TY.dve"].sem, 1)
                            w(c["TY.hi"].at(i))
                            if i >= 2:
                                w(c["FR.pe"].at(i - 2), c["FK.pe"].at(i - 2))
                            dve.tensor_tensor(xmT[1][:, i % 2].rearrange("p m k t -> p (m k t)"),
                                              xm[:, i % 2].rearrange("p m k t -> p (m k t)"),
                                              f(xmT[0][:, i % 2].rearrange("p m k t -> p (m k t)")),
                                              ALU.subtract).then_inc(c["TY.dve"].sem, 1)
                        elif kind == "FK":
                            w(c["FK.act"].at(i, 1))
                            dve.tensor_tensor(kk[:, i % 2], kr[:, i % 2], kr[:, i % 2], ALU.mult)\
                                .then_inc(c["FK.dve"].sem, 1)
                            w(c["FK.act"].at(i))
                            if i >= 2:
                                w(c["FV.pe"].at(i - 2))
                            dve.tensor_tensor(kkT[1][:, i % 2], kk[:, i % 2], f(kkT[0][:, i % 2]), ALU.subtract)\
                                .then_inc(c["FK.dve"].sem, 1)
                        elif kind == "FV":
                            w(c["FV.pe"].at(i), c["FR.act"].at(i))
                            if i >= 2:
                                w(c[f"OUT.dma{i % 2}"].at(i // 2 - 1))
                            yy = y[:, i % 2]
                            dve.tensor_tensor(yy, bank("FV", i).rearrange("p (t d) -> p t d", t=2),
                                              gate[:, i % 2].rearrange("p (t d) -> p t d", t=2), ALU.mult)\
                                .then_inc(c["FV.dve"].sem, 1)
                            w(c["FV.dve"].at(i, 1))
                            dve.tensor_tensor(yy, yy, xs[:, 2 * i:2 * i + 2, :], ALU.add)\
                                .then_inc(c["FV.dve"].sem, 1)
                            w(c["FV.dve"].at(i, 2))
                            for t in range(2):
                                dve.bn_stats(st3[:, i % 2, t], y[:, i % 2, t]).then_inc(c["FV.dve"].sem, 1)
                            if i >= 2:
                                w(c["FV.pool"].at(i - 2))
                            for t in range(2):
                                w(c["FV.dve"].at(i, 3 + t))
                                dve.bn_aggr(mv3[:, i % 2, t], st3[:, i % 2, t]).then_inc(c["FV.dve"].sem, 1)
                        elif kind == "LN3B":
                            w(c["FV.pool"].at(i))
                            for t in range(2):
                                yt = y[:, i % 2, t]
                                dve.tensor_scalar(yt, yt, mv3[:, i % 2, t, 0:1], rs3[:, i % 2, t:t + 1],
                                                  ALU.subtract, ALU.mult).then_inc(c["LN3B.dve"].sem, 1)

                @block.tensor
                def _(pe):
                    w = Waiter(pe)
                    phase2_over(w)
                    w(pre3.at(1))
                    for kind, i in order3:
                        if kind in let_go:
                            bank_free(w, kind, i)
                        if kind == "TY":
                            for k in range(KC):
                                for t in range(2):
                                    mm = pe.transpose(bank("TY", i)[:, k * D + t * P:k * D + (t + 1) * P],
                                                      xs[:, 2 * i + t, k * P:(k + 1) * P], ident[:])
                            mm.then_inc(c["TY.pe"].sem, 1)
                        elif kind == "FR":
                            w(c["TY.dve"].at(i))
                            for t in range(2):
                                mm = split_product(pe, bank("FR", i)[:, t * D:(t + 1) * D],
                                                   [hi_lo(xmT, slice(None), i % 2, MIX_R, k, slice(t * P, (t + 1) * P)) for k in range(KC)],
                                                   [hi_lo(w_f, slice(None), MIX_R, k) for k in range(KC)])
                            mm.then_inc(c["FR.pe"].sem, 1)
                        elif kind == "FK":
                            for e in range(KC):
                                mm = split_product(pe, bank("FK", i)[:, e * D:(e + 1) * D],
                                                   [hi_lo(w_f, slice(None), MIX_K, k, slice(e * P, (e + 1) * P)) for k in range(KC)],
                                                   [hi_lo(xmT, slice(None), i % 2, MIX_K, k) for k in range(KC)])
                            mm.then_inc(c["FK.pe"].sem, 1)
                        elif kind == "FV":
                            w(c["FK.dve"].at(i))
                            for t in range(2):
                                mm = split_product(pe, bank("FV", i)[:, t * D:(t + 1) * D],
                                                   [hi_lo(kkT, slice(None), i % 2, slice(k * D + t * P, k * D + (t + 1) * P)) for k in range(KC)],
                                                   [hi_lo(w_f, slice(None), VW, k) for k in range(KC)])
                            mm.then_inc(c["FV.pe"].sem, 1)


def shape_constants():
    row = np.arange(P)
    mask_k = (row[:, None] // DH == np.arange(HC)[None, :]).astype(np.float32) * np.float32(DH ** -0.5)
    flat = np.arange(RV * P)
    sel = ((flat[None, :] % SC == np.arange(SC)[:, None]) & (flat[None, :] < W)).astype(np.float32)
    head = flat.reshape(RV, P).T // SC
    mask_v = (head[:, :, None] == (row // DH)[None, None, :]).astype(np.float32)
    return {"ident": np.eye(P, dtype=np.float32), "mask_k": mask_k, "sel": sel,
            "mask_v": np.ascontiguousarray(mask_v)}


def kernel(**inputs):
    import numpy as _np
    import concourse.bacc as _bacc
    from concourse.bass_utils import run_bass_kernel_spmd as _run

    a = {k: _np.asarray(v) for k, v in inputs.items()}
    x = a["x"].reshape(B * S, D)
    laid = {
        "x": x, "xT": x.T, "cT": a["ctx_1024"].reshape(B * SC, D).T,
        "wqT": a["L0_attn_Wq"].T, "wkT": a["L0_attn_Wk"].T, "wv": a["L0_attn_Wv"], "woT": a["L0_attn_Wo"].T,
        "bq": a["L0_attn_bq"], "bk": a["L0_attn_bk"], "bv": a["L0_attn_bv"], "bo": a["L0_attn_bo"],
        "ls": a["L0_attn_layerscale"],
        "xwqT": a["L0_xattn_wq_w"].T, "xwkT": a["L0_xattn_wk_w"].T, "xwvT": a["L0_xattn_wv_w"].T,
        "xwdT": a["L0_xattn_dense_w"].T,
        "xbq": a["L0_xattn_wq_b"], "xbk": a["L0_xattn_wk_b"], "xbv": a["L0_xattn_wv_b"],
        "xbd": a["L0_xattn_dense_b"],
        "wrT": a["L0_ffn_W_r"].T, "wkcT": a["L0_ffn_W_k"].T, "wvcT": a["L0_ffn_W_v"].T,
        "mu_r": a["L0_ffn_mu_r"], "mu_k": a["L0_ffn_mu_k"],
    }
    for name in ("bv", "xbq", "xbk", "mu_r", "mu_k"):
        laid[name] = laid[name].reshape(KC, P).T
    laid.update(shape_constants())
    nc = _bacc.Bacc("TRN2", target_bir_lowering=False, num_devices=1)
    arrays, io = {}, {}
    for name, v in laid.items():
        v = _np.ascontiguousarray(v)
        arrays[f"in_{name}"] = v
        io[name] = nc.dram_tensor(f"in_{name}", v.shape, mybir.dt.from_np(v.dtype), kind="ExternalInput").ap()
    io["out"] = nc.dram_tensor("out_y", (B * S, D), F32, kind="ExternalOutput").ap()
    decoder_layer(nc, io)
    r = _run(nc, [arrays], core_ids=[0])
    return r.results[0]["out_y"].reshape(B, S, D)
```

```python
from contextlib import ExitStack

import numpy as np

import concourse.bass as bass
from concourse import mybir

F32 = mybir.dt.float32
F32R = mybir.dt.float32r
ALU = mybir.AluOpType
ACT = mybir.ActivationFunctionType
AX = mybir.AxisListType.X

P = 128
B, S, D = 4, 1024, 256
KC = D // P
NT = B * S // P
TB = S // P
NG = NT // 4
NJ = NT // 2
H, DH = 16, 16
SC = 77
HC = H // KC
W = HC * SC
RV = -(-W // P)
PW = KC * W
PPAD = W + RV * P
EPS = 1e-5
BANK = 512
NX = 3
RING = 5
S0 = 152
LOGIT_CUTS = [(0, 0, 360), (0, 360, W), (1, 0, 256), (1, 256, W)]


class Count:

    def __init__(self, sem, per=1):
        self.sem, self.per = sem, per

    def at(self, i, k=None):
        return self.sem, self.per * i + (self.per if k is None else k)


class Waiter:

    def __init__(self, eng):
        self.eng, self.seen = eng, {}

    def __call__(self, *pairs):
        for sem, value in pairs:
            if value > self.seen.get(sem.name, 0):
                self.seen[sem.name] = value
                self.eng.wait_ge(sem, value)


def self_attention_order():
    order = [("XT", 0), ("XT", 1)]
    for b in range(B + 1):
        load, attend = [], []
        if b < B:
            for t in range(TB + 2):
                i = b * TB + t
                if t < TB:
                    if t % 2 == 0 and i // 2 + 2 < NJ:
                        load.append(("XT", i // 2 + 2))
                    load.append(("QK", i))
                    if i == 1:
                        load.append(("WV", 0))
                    if t % 2 == 1:
                        load.append(("V", i // 2))
                if 1 <= t <= TB:
                    load.append(("QN", i - 1))
                if t >= 2:
                    load.append(("TQK", i - 2))
        if b > 0:
            for n in range(16 + 2):
                m = (b - 1) * 16 + n
                if n < 16:
                    attend.append(("ST", m))
                if n >= 2:
                    attend.append(("AV", m - 2))
                    if (m - 2) % 8 == 7:
                        g = (m - 2) // 8
                        attend += [("LN1", 4 * g + t) for t in range(4)]
                        attend += [("LN1B", 4 * g + t) for t in range(4)]
        n = max(len(load), len(attend))
        done = [0, 0]
        for k in range(1, n + 1):
            for w, seq in enumerate((load, attend)):
                upto = len(seq) * k // n
                order += seq[done[w]:upto]
                done[w] = upto
    return order


def cross_attention_order():
    order = [("KB", 0), ("TX", 0), ("TX", 1), ("XQ", 0), ("VB", 0), ("VC", 0)]

    def put(kind, i, n=NT):
        if 0 <= i < n:
            order.append((kind, i))

    for i in range(NT + 12):
        s, odd = divmod(i, 2)
        put("XS", i)
        put("SM", i - 1)
        if not odd:
            put("LN2B", s - 5, NJ)
            for u in range(3):
                put("TP", 3 * (i - 3) + u, 3 * NT)
            put("EX", i)
            put("PV", s - 3, NJ)
            put("XQ", s + 1, NJ)
            if i % TB == 0 and i:
                put("VC", i // TB, B)
            if i % TB == TB - 2:
                put("VB", i // TB + 1, B)
        else:
            put("PW", s - 3, NJ)
            for u in range(3):
                put("TP", 3 * (i - 3) + u, 3 * NT)
            put("EX", i)
            put("XD", s - 4, NJ)
            put("TX", s + 2, NJ)
            if i % TB == 3:
                put("KB", i // TB + 1, B)
    return order


def channel_mix_order():
    order = []

    def put(kind, i):
        if 0 <= i < NJ:
            order.append((kind, i))

    for s in range(NJ + 6):
        put("FR", s - 3)
        put("FK", s - 3)
        put("TY", s)
        put("TH", s - 1)
        put("FV", s - 4)
        put("LN3B", s - 5)
    return order


def decoder_layer(nc, io):
    ctx = ExitStack()
    with ctx:
        def sem(name):
            return ctx.enter_context(nc.semaphore(name))

        def tensor(stack, name, shape, dt=F32):
            return stack.enter_context(nc.sbuf_tensor(name, shape, dt))

        big = ctx.enter_context(nc.psum_tensor("big", [P, 3 * BANK], F32))
        ring = ctx.enter_context(nc.psum_tensor("ring", [P, RING, BANK], F32))
        acc = big[:, 0:2 * BANK].rearrange("p (t d) -> p t d", d=D)
        logits = big[:, S0:S0 + PW]

        xs = tensor(ctx, "xs", [P, NT, D])
        ident = tensor(ctx, "ident", [P, P])
        consts = tensor(ctx, "consts", [P, 6])
        nlogs = tensor(ctx, "nlogs", [P, 1])
        eps2, half2, minus2 = consts[:, 0:2], consts[:, 2:4], consts[:, 4:6]

        names = {
            "XT.dma0": 16, "XT.dma1": 16, "XT.dma2": 16, "XT.act": 1, "XT.pool": 1, "QK.pe": 1, "QK.dve": 5, "QK.pool": 2,
            "QN.dve": 2, "TQK.pe": 1, "TQK.act": 1, "TQK.dve": 1, "V.pe": 1, "V.dve": 1,
            "V.act": 1, "V.pool": 1, "ST.pe": 1, "ST.act": 2, "ST.dve": 1, "AV.pe": 1,
            "LN1.dve": 3, "LN1.pool": 2, "LN1B.dve": 1, "XS0.dma": 16, "XB.pool": 1,
            "KB.pool": 4, "KB.act": 2, "VB.pe": 1, "VB.dve": 2, "VB.act": 1,
            "VC.pe": 3, "VC.dve": 3, "VC.act": 3, "VC.pool": 3,
            "TX.pe": 1, "TX.act": 1, "TX.dve": 1, "XR.pool": 1, "XQ.pe": 1, "XQ.act": 2,
            "XQ.dve": 2, "XS.pe": 1, "XS.dve": 2, "EX.act": 1, "SM.dve": 2, "SM.pool": 1,
            "TP.pe": 1, "TP.act": 1, "TP.dve": 1, "PV.pe": 1, "PV.act": 1, "PV.dve": 1,
            "XD.pe": 1, "XD.dve": 5, "XD.pool": 4, "LN2B.act": 2,
            "TY.pe": 1, "TY.act": 1, "TY.pool": 2, "TY.dve": 4, "TH.act": 1, "TH.pool": 1,
            "FR.pe": 1, "FR.act": 1, "FK.pe": 1, "FK.act": 3, "FK.dve": 1,
            "FV.pe": 1, "FV.dve": 6, "FV.pool": 2, "LN3B.dve": 2, "OUT.dma0": 16, "OUT.dma1": 16,
        }
        c = {name: Count(sem("s_" + name.replace(".", "_")), per) for name, per in names.items()}
        load_w, load_id, load1, load2, load3 = (sem(n) for n in ("load_w", "load_id", "load1", "load2", "load3"))
        pre = {e: Count(sem("pre_" + e)) for e in ("pe", "act", "dve", "pool")}
        made = {e: 0 for e in pre}

        order1, order2, order3 = self_attention_order(), cross_attention_order(), channel_mix_order()
        let_go = {
            "QK": lambda i: c["QK.dve"].at(i, 1), "TQK": c["TQK.dve"].at, "V": c["V.dve"].at,
            "ST": lambda n: c["ST.act"].at(n, 1),
            "VB": lambda i: c["VB.dve"].at(i, 1), "VC": lambda q: c["VC.dve"].at(q // 3, q % 3 + 1),
            "TX": c["TX.dve"].at, "XQ": c["XQ.dve"].at, "TP": c["TP.dve"].at, "PV": c["PV.dve"].at,
            "XD": lambda j: c["XD.dve"].at(j, 1), "TY": c["TY.act"].at, "FR": c["FR.act"].at,
            "FK": lambda j: c["FK.act"].at(j, 1), "FV": lambda j: c["FV.dve"].at(j, 1),
        }
        takers = []
        for kind, i in order1 + order2 + order3:
            if kind == "VC":
                takers += [("VC", 3 * i + q) for q in range(3)]
            elif kind in let_go:
                takers.append((kind, i))
        place = {step: n for n, step in enumerate(takers)}

        def bank(kind, i):
            return ring[:, place[kind, i] % RING, :]

        def bank_free(w, kind, i):
            n = place[kind, i]
            if n >= RING:
                k, m = takers[n - RING]
                w(let_go[k](m))

        def split_product(eng, out, stationary, moving, first=True, last=True, check=True):
            n = len(stationary)
            for k in range(n):
                (sh, sl), (mh, ml) = stationary[k], moving[k]
                for q, (s_, m_) in enumerate(((sh, mh), (sh, ml), (sl, mh))):
                    mm = eng.matmul(out, s_, m_, start=first and k == 0 and q == 0,
                                    stop=last and k == n - 1 and q == 2, skip_group_check=not check)
            return mm

        def hi_lo(pair, *at):
            return tuple(t[at] for t in pair)

        def f(ap):
            return ap.bitcast(F32)

        with ExitStack() as ph:
            wraw = tensor(ph, "wraw", [P, KC, 2 * D])
            w_qk = (tensor(ph, "wqk_hi", [P, KC, 2 * D], F32R), tensor(ph, "wqk_lo", [P, KC, 2 * D], F32R))
            wv_raw = tensor(ph, "wv_raw", [P, KC, D])
            wo_ls = tensor(ph, "wo_ls", [P, KC, D])
            w_vo = (tensor(ph, "wvo_hi", [P, KC, D], F32R), tensor(ph, "wvo_lo", [P, KC, D], F32R))
            bqk = tensor(ph, "bqk", [P, 2 * D])
            bvcol = tensor(ph, "bvcol", [P, KC])
            bvwide = tensor(ph, "bvwide", [P, KC, P])
            bvo = tensor(ph, "bvo", [P, D])
            bo = tensor(ph, "bo", [P, D])
            ls = tensor(ph, "ls", [P, D])
            xraw = tensor(ph, "xraw", [P, NX, KC, 2 * P])
            xT = (tensor(ph, "xT_hi", [P, NX, KC, 2 * P], F32R), tensor(ph, "xT_lo", [P, NX, KC, 2 * P], F32R))
            qk_sb = tensor(ph, "qk_sb", [P, 4, 2 * D])
            st1 = tensor(ph, "st1", [P, 4, 2, 6])
            mv1 = tensor(ph, "mv1", [P, 4, 2, 2])
            rs1 = tensor(ph, "rs1", [P, 4, 2])
            qkT = (tensor(ph, "qkT_hi", [P, 2, 4, S], F32R), tensor(ph, "qkT_lo", [P, 2, 4, S], F32R))
            v_sb = tensor(ph, "v_sb", [P, 2, 2 * D])
            vv = (tensor(ph, "v_hi", [P, 2, TB, D], F32R), tensor(ph, "v_lo", [P, 2, TB, D], F32R))
            NA = 3
            a_sb = tensor(ph, "a_sb", [P, NA, BANK])
            aT = (tensor(ph, "aT_hi", [P, NA, BANK], F32R), tensor(ph, "aT_lo", [P, NA, BANK], F32R))
            stl = tensor(ph, "stl", [P, 4, 6])
            mvl = tensor(ph, "mvl", [P, 4, 2])
            rsl = tensor(ph, "rsl", [P, 4])

            def bc(name, n=D):
                return io[name].rearrange("(o n) -> o n", o=1).to_broadcast([P, n])

            def col(name):
                return io[name]

            def rows(name):
                return io[name].rearrange("(k p) n -> p k n", p=P)

            xT_dram = rows("xT")
            x_dram = io["x"].rearrange("(i p) d -> p i d", p=P)
            NLOAD1 = 7 * 16
            PRE_WLO, PRE_WOLS, PRE_BVW, PRE_BO, PRE_VLO, PRE_BVO = range(1, 7)

            with nc.Block() as block:
                @block.sync
                def _(sp):
                    w = Waiter(sp)
                    sp.dma_start(wraw[:, :, 0:D], rows("wqT")).then_inc(load_w, 16)
                    sp.dma_start(wraw[:, :, D:2 * D], rows("wkT")).then_inc(load_w, 16)
                    for kind, i in order1:
                        if kind == "XT":
                            if i >= NX:
                                w(c["XT.pool"].at(i - NX))
                            sp.dma_start(xraw[:, i % NX], xT_dram[:, :, i * 2 * P:(i + 1) * 2 * P])\
                                .then_inc(c[f"XT.dma{i % NX}"].sem, 16)
                        if (kind, i) == ("XT", 1):
                            for g in range(NG):
                                sp.dma_start(xs[:, 4 * g:4 * g + 4, :], x_dram[:, 4 * g:4 * g + 4, :])\
                                    .then_inc(c["XS0.dma"].sem, 16)

                @block.scalar
                def _(act):
                    w = Waiter(act)
                    act.dma_start(wv_raw[:], rows("wv")).then_inc(load1, 16)
                    act.dma_start(wo_ls[:], rows("woT")).then_inc(load1, 16)
                    act.dma_start(ls[:], bc("ls")).then_inc(load1, 16)
                    act.dma_start(bvcol[:], col("bv")).then_inc(load1, 16)
                    act.dma_start(bqk[:, 0:D], bc("bq")).then_inc(load1, 16)
                    act.dma_start(bqk[:, D:2 * D], bc("bk")).then_inc(load1, 16)
                    act.dma_start(bo[:], bc("bo")).then_inc(load1, 16)
                    act.dma_start(ident[:], io["ident"]).then_inc(load_id, 16)
                    for kind, i in order1:
                        if kind == "XT":
                            w(c[f"XT.dma{i % NX}"].at(i // NX))
                            if i >= NX:
                                w(c["QK.pe"].at(2 * (i - NX) + 1), c["V.pe"].at(i - NX))
                            act.activation(xT[0][:, i % NX], xraw[:, i % NX], ACT.Identity)\
                                .then_inc(c["XT.act"].sem, 1)
                        elif kind == "WV":
                            w(pre["pe"].at(0))
                            act.activation(w_vo[0][:].rearrange("p k d -> p (k d)"), big[:, 0:2 * D],
                                           ACT.Identity).then_inc(pre["act"].sem, 1)
                        elif kind == "TQK":
                            b, t = divmod(i, TB)
                            w(c["TQK.pe"].at(i))
                            if b >= 2:
                                w(c["ST.pe"].at(16 * (b - 1) - 1))
                            act.activation(qkT[0][:, b % 2, :, t * P:(t + 1) * P],
                                           bank("TQK", i).rearrange("p (m t) -> p m t", m=4),
                                           ACT.Identity).then_inc(c["TQK.act"].sem, 1)
                        elif kind == "V":
                            b, t = divmod(i, TB // 2)
                            w(c["V.dve"].at(i))
                            if b >= 2:
                                w(c["AV.pe"].at(16 * (b - 1) - 1))
                            act.activation(vv[0][:, b % 2, 2 * t:2 * t + 2, :].rearrange("p t d -> p (t d)"),
                                           v_sb[:, i % 2], ACT.Identity).then_inc(c["V.act"].sem, 1)
                        elif kind == "ST":
                            w(c["ST.pe"].at(i))
                            if i >= NA:
                                w(c["ST.dve"].at(i - NA), c["AV.pe"].at(i - NA))
                            if i == 0:
                                w(pre["pool"].at(0))
                            act.activation(a_sb[:, i % NA], bank("ST", i), ACT.Sigmoid,
                                           bias=nlogs[:, 0:1], scale=1.0 / 16).then_inc(c["ST.act"].sem, 1)
                            w(c["ST.act"].at(i, 1))
                            act.activation(aT[0][:, i % NA], a_sb[:, i % NA], ACT.Identity)\
                                .then_inc(c["ST.act"].sem, 1)

                @block.gpsimd
                def _(pool):
                    w = Waiter(pool)
                    pool.memset(nlogs[:], -float(np.log(np.float32(S))))
                    pool.memset(consts[:, 0:2], EPS)
                    pool.memset(consts[:, 4:6], -1.0)
                    pool.memset(consts[:, 2:4], -0.5).then_inc(pre["pool"].sem, 1)
                    w(pre["pool"].at(0))
                    first = True
                    for kind, i in order1:
                        if kind == "XT":
                            w(c["XT.act"].at(i))
                            if i >= NX:
                                w(c["QK.pe"].at(2 * (i - NX) + 1), c["V.pe"].at(i - NX))
                            pool.tensor_tensor(xT[1][:, i % NX], xraw[:, i % NX], f(xT[0][:, i % NX]),
                                               ALU.subtract).then_inc(c["XT.pool"].sem, 1)
                        elif kind == "QK":
                            w(c["QK.dve"].at(i))
                            if i >= 4:
                                w(c["QN.dve"].at(i - 4))
                            r = rs1[:, i % 4]
                            pool.tensor_tensor(r, mv1[:, i % 4, :, 1], eps2, ALU.add)\
                                .then_inc(c["QK.pool"].sem, 1)
                            w(c["QK.pool"].at(i, 1))
                            pool.tensor_tensor(r, r, half2, ALU.pow).then_inc(c["QK.pool"].sem, 1)
                        elif kind == "V":
                            b, t = divmod(i, TB // 2)
                            w(c["V.act"].at(i))
                            if b >= 2:
                                w(c["AV.pe"].at(16 * (b - 1) - 1))
                            pool.tensor_tensor(vv[1][:, b % 2, 2 * t:2 * t + 2, :].rearrange("p t d -> p (t d)"),
                                               v_sb[:, i % 2],
                                               f(vv[0][:, b % 2, 2 * t:2 * t + 2, :].rearrange("p t d -> p (t d)")),
                                               ALU.subtract).then_inc(c["V.pool"].sem, 1)
                        elif kind == "ST" and i % 8 == 0:
                            g = i // 8
                            w(c["XS0.dma"].at(NG - 1), pre["dve"].at(PRE_BO))
                            pool.tensor_tensor(xs[:, 4 * g:4 * g + 4, :], xs[:, 4 * g:4 * g + 4, :],
                                               bo[:].rearrange("p (o d) -> p o d", o=1).to_broadcast([P, 4, D]),
                                               ALU.add).then_inc(c["XB.pool"].sem, 1)
                        elif kind == "LN1":
                            w(c["LN1.dve"].at(i))
                            if i >= 4:
                                w(c["LN1B.dve"].at(i - 4))
                            r = rsl[:, i % 4:i % 4 + 1]
                            pool.tensor_tensor(r, mvl[:, i % 4, 1:2], eps2[:, 0:1], ALU.add)\
                                .then_inc(c["LN1.pool"].sem, 1)
                            w(c["LN1.pool"].at(i, 1))
                            pool.tensor_tensor(r, r, half2[:, 0:1], ALU.pow).then_inc(c["LN1.pool"].sem, 1)

                @block.vector
                def _(dve):
                    w = Waiter(dve)
                    d = pre["dve"].sem
                    w((load_w, 32))
                    dve.tensor_copy(w_qk[0][:], wraw[:]).then_inc(d, 1)
                    w((d, 1))
                    dve.tensor_tensor(w_qk[1][:], wraw[:], f(w_qk[0][:]), ALU.subtract).then_inc(d, 1)
                    w((load1, NLOAD1))
                    dve.tensor_tensor(wo_ls[:], wo_ls[:],
                                      ls[:].rearrange("p (o d) -> p o d", o=1).to_broadcast([P, KC, D]),
                                      ALU.mult).then_inc(d, 1)
                    dve.tensor_copy(bvwide[:], bvcol[:].rearrange("p (k o) -> p k o", o=1)
                                    .to_broadcast([P, KC, P])).then_inc(d, 1)
                    dve.tensor_tensor(bo[:], bo[:], ls[:], ALU.mult).then_inc(d, 1)
                    for kind, i in order1:
                        if kind == "WV":
                            w(pre["act"].at(0))
                            dve.tensor_tensor(w_vo[1][:].rearrange("p k d -> p (k d)"), big[:, 0:2 * D],
                                              f(w_vo[0][:].rearrange("p k d -> p (k d)")), ALU.subtract).then_inc(d, 1)
                            dve.tensor_copy(bvo[:], big[:, BANK:BANK + D]).then_inc(d, 1)
                        if kind == "QK":
                            w(c["QK.pe"].at(i))
                            if i >= 4:
                                w(c["TQK.pe"].at(i - 4))
                                w(c["QK.pool"].at(i - 4))
                            dve.tensor_tensor(qk_sb[:, i % 4], bank("QK", i), bqk[:], ALU.add)\
                                .then_inc(c["QK.dve"].sem, 1)
                            w(c["QK.dve"].at(i, 1))
                            for m in range(2):
                                dve.bn_stats(st1[:, i % 4, m], qk_sb[:, i % 4, m * D:(m + 1) * D])\
                                    .then_inc(c["QK.dve"].sem, 1)
                            for m in range(2):
                                w(c["QK.dve"].at(i, 2 + m))
                                dve.bn_aggr(mv1[:, i % 4, m], st1[:, i % 4, m]).then_inc(c["QK.dve"].sem, 1)
                        elif kind == "QN":
                            w(c["QK.pool"].at(i))
                            for m in range(2):
                                s_ = qk_sb[:, i % 4, m * D:(m + 1) * D]
                                dve.tensor_scalar(s_, s_, mv1[:, i % 4, m, 0:1], rs1[:, i % 4, m:m + 1],
                                                  ALU.subtract, ALU.mult).then_inc(c["QN.dve"].sem, 1)
                        elif kind == "TQK":
                            b, t = divmod(i, TB)
                            w(c["TQK.act"].at(i))
                            dve.tensor_tensor(qkT[1][:, b % 2, :, t * P:(t + 1) * P],
                                              bank("TQK", i).rearrange("p (m t) -> p m t", m=4),
                                              f(qkT[0][:, b % 2, :, t * P:(t + 1) * P]),
                                              ALU.subtract).then_inc(c["TQK.dve"].sem, 1)
                        elif kind == "V":
                            w(c["V.pe"].at(i))
                            if i >= 2:
                                w(c["V.pool"].at(i - 2))
                            if i == 0:
                                w(pre["dve"].at(PRE_BVO))
                            dve.tensor_tensor(v_sb[:, i % 2].rearrange("p (t d) -> p t d", t=2),
                                              bank("V", i).rearrange("p (t d) -> p t d", t=2),
                                              bvo[:].rearrange("p (o d) -> p o d", o=1).to_broadcast([P, 2, D]),
                                              ALU.add).then_inc(c["V.dve"].sem, 1)
                        elif kind == "ST":
                            w(c["ST.act"].at(i))
                            dve.tensor_tensor(aT[1][:, i % NA], a_sb[:, i % NA], f(aT[0][:, i % NA]),
                                              ALU.subtract).then_inc(c["ST.dve"].sem, 1)
                        elif kind == "LN1":
                            g, t = divmod(i, 4)
                            w(c["AV.pe"].at(8 * g + 7), c["XB.pool"].at(g))
                            dve.tensor_tensor(xs[:, i], acc[:, t], xs[:, i], ALU.add)\
                                .then_inc(c["LN1.dve"].sem, 1)
                            w(c["LN1.dve"].at(i, 1))
                            dve.bn_stats(stl[:, t], xs[:, i]).then_inc(c["LN1.dve"].sem, 1)
                            w(c["LN1.dve"].at(i, 2))
                            if i >= 4:
                                w(c["LN1.pool"].at(i - 4))
                            dve.bn_aggr(mvl[:, t], stl[:, t]).then_inc(c["LN1.dve"].sem, 1)
                        elif kind == "LN1B":
                            t = i % 4
                            w(c["LN1.pool"].at(i))
                            dve.tensor_scalar(xs[:, i], xs[:, i], mvl[:, t, 0:1], rsl[:, t:t + 1],
                                              ALU.subtract, ALU.mult).then_inc(c["LN1B.dve"].sem, 1)

                @block.tensor
                def _(pe):
                    w = Waiter(pe)
                    w(pre["dve"].at(PRE_WLO), (load_id, 16))
                    for kind, i in order1:
                        if kind in let_go:
                            bank_free(w, kind, i)
                        if kind == "WV":
                            w(pre["dve"].at(PRE_BVW))
                            for m in range(KC):
                                for e in range(KC):
                                    pe.matmul(big[:, m * D:(m + 1) * D], wv_raw[:, e, m * P:(m + 1) * P],
                                              wo_ls[:, e, :], start=e == 0, stop=e == KC - 1)
                            for e in range(KC):
                                mm = pe.matmul(big[:, BANK:BANK + D], bvwide[:, e, :], wo_ls[:, e, :],
                                               start=e == 0, stop=e == KC - 1)
                            mm.then_inc(pre["pe"].sem, 1)
                        if kind == "QK":
                            j, t = divmod(i, 2)
                            w(c["XT.act"].at(j), c["XT.pool"].at(j))
                            split_product(pe, bank("QK", i),
                                          [hi_lo(xT, slice(None), j % NX, k, slice(t * P, (t + 1) * P)) for k in range(KC)],
                                          [hi_lo(w_qk, slice(None), k) for k in range(KC)])\
                                .then_inc(c["QK.pe"].sem, 1)
                        elif kind == "V":
                            w(pre["dve"].at(PRE_VLO))
                            for t in range(2):
                                mm = split_product(pe, bank("V", i)[:, t * D:(t + 1) * D],
                                                   [hi_lo(xT, slice(None), i % NX, k, slice(t * P, (t + 1) * P)) for k in range(KC)],
                                                   [hi_lo(w_vo, slice(None), k) for k in range(KC)])
                            mm.then_inc(c["V.pe"].sem, 1)
                        elif kind == "TQK":
                            w(c["QN.dve"].at(i))
                            for m in range(4):
                                mm = pe.transpose(bank("TQK", i)[:, m * P:(m + 1) * P],
                                                  qk_sb[:, i % 4, m * P:(m + 1) * P], ident[:])
                            mm.then_inc(c["TQK.pe"].sem, 1)
                        elif kind == "ST":
                            g, kt = divmod(i, TB)
                            b = g // 2
                            w(c["TQK.dve"].at(max(TB * b + kt, 4 * g + 3)))
                            q0 = (g % 2) * BANK
                            split_product(pe, bank("ST", i),
                                          [hi_lo(qkT, slice(None), b % 2, 2 + e, slice(kt * P, (kt + 1) * P)) for e in range(KC)],
                                          [hi_lo(qkT, slice(None), b % 2, e, slice(q0, q0 + BANK)) for e in range(KC)])\
                                .then_inc(c["ST.pe"].sem, 1)
                        elif kind == "AV":
                            g, kt = divmod(i, TB)
                            b = g // 2
                            w(c["ST.dve"].at(i), c["V.pool"].at(TB // 2 * b + kt // 2))
                            if kt == 0:
                                w(c["LN1.dve"].at(4 * g - 1, 1) if g else pre["dve"].at(PRE_BVO))
                            for t in range(4):
                                mm = split_product(pe, acc[:, t],
                                                   [hi_lo(aT, slice(None), i % NA, slice(t * P, (t + 1) * P))],
                                                   [hi_lo(vv, slice(None), b % 2, kt)],
                                                   first=kt == 0 and t % 2 == 0, last=kt == TB - 1, check=False)
                            mm.then_inc(c["AV.pe"].sem, 1)

        with ExitStack() as ph:
            wx_raw = tensor(ph, "wx_raw", [P, 4, KC, D])
            w_x = (tensor(ph, "wx_hi", [P, 2, KC, D], F32R), tensor(ph, "wx_lo", [P, 2, KC, D], F32R))
            cT = tensor(ph, "cT", [P, KC, B * SC])
            kT = tensor(ph, "kT", [P, KC, B * SC])
            mask_k = tensor(ph, "mask_k", [P, HC])
            mask_v = tensor(ph, "mask_v", [P, RV, P])
            sel_raw = tensor(ph, "sel_raw", [SC, RV * P])
            sel = tensor(ph, "sel", [SC, RV * P], F32R)
            bqcol = tensor(ph, "bqcol", [P, KC])
            bkcol = tensor(ph, "bkcol", [P, KC])
            bxv = tensor(ph, "bxv", [P, D])
            bxd = tensor(ph, "bxd", [P, D])
            kb32 = tensor(ph, "kb32", [P, W])
            kb = (tensor(ph, "kb_hi", [P, 2, KC, W], F32R), tensor(ph, "kb_lo", [P, 2, KC, W], F32R))
            v32 = tensor(ph, "v32", [SC, D])
            vc = (tensor(ph, "vc_hi", [SC, D], F32R), tensor(ph, "vc_lo", [SC, D], F32R))
            vm = tensor(ph, "vm", [P, 2, KC, P])
            vb = (tensor(ph, "vb_hi", [P, 2, RV, KC, P], F32R), tensor(ph, "vb_lo", [P, 2, RV, KC, P], F32R))
            x1T = (tensor(ph, "x1T_hi", [P, 2, BANK], F32R), tensor(ph, "x1T_lo", [P, 2, BANK], F32R))
            xqT = (tensor(ph, "xqT_hi", [P, 2, BANK], F32R), tensor(ph, "xqT_lo", [P, 2, BANK], F32R))
            NP = 4
            p_sb = tensor(ph, "p_sb", [P, NP, PPAD])
            mx = tensor(ph, "mx", [P, 2, H])
            sm = tensor(ph, "sm", [P, 2, H])
            rc = tensor(ph, "rc", [P, 2, H])
            pT = (tensor(ph, "pT_hi", [P, 2, 2 * RV, 2 * P], F32R), tensor(ph, "pT_lo", [P, 2, 2 * RV, 2 * P], F32R))
            oT = (tensor(ph, "oT_hi", [P, 2, BANK], F32R), tensor(ph, "oT_lo", [P, 2, BANK], F32R))
            st2 = tensor(ph, "st2", [P, 2, 2, 6])
            mv2 = tensor(ph, "mv2", [P, 2, 2, 2])
            rs2 = tensor(ph, "rs2", [P, 2, 2])
            nb2 = tensor(ph, "nb2", [P, 2, 2])
            XQW, XDW, XKW, XVW = range(4)
            NLOAD2 = 12 * 16
            pre2 = {e: Count(sem("pre2_" + e)) for e in ("pe", "act", "dve", "pool")}

            def heads(ap):
                return ap.rearrange("p (h k) -> p h k", k=SC)

            def per_head(ap):
                return ap.rearrange("p (h o) -> p h o", o=1).to_broadcast([P, H, SC])

            with nc.Block() as block:
                def phase1_over(w):
                    w(c["AV.pe"].at(16 * B - 1), c["TQK.dve"].at(NT - 1), c["ST.dve"].at(16 * B - 1),
                      c["V.pool"].at(NJ - 1), c["LN1B.dve"].at(NT - 1))

                @block.sync
                def _(sp):
                    w = Waiter(sp)
                    phase1_over(w)
                    for n, name in enumerate(("xwqT", "xwdT", "xwkT", "xwvT")):
                        sp.dma_start(wx_raw[:, n], rows(name)).then_inc(load2, 16)
                    sp.dma_start(cT[:], rows("cT")).then_inc(load2, 16)
                    sp.dma_start(mask_k[:], io["mask_k"]).then_inc(load2, 16)
                    sp.dma_start(mask_v[:], io["mask_v"]).then_inc(load2, 16)
                    sp.dma_start(sel_raw[:], io["sel"]).then_inc(load2, 16)
                    sp.dma_start(bqcol[:], col("xbq")).then_inc(load2, 16)
                    sp.dma_start(bkcol[:], col("xbk")).then_inc(load2, 16)
                    sp.dma_start(bxv[:], bc("xbv")).then_inc(load2, 16)
                    sp.dma_start(bxd[:], bc("xbd")).then_inc(load2, 16)

                @block.scalar
                def _(act):
                    w = Waiter(act)
                    phase1_over(w)
                    w((load2, NLOAD2), pre2["pe"].at(0))
                    for e in range(KC):
                        act.activation(kT[:, e, :], ring[:, e, 0:B * SC], ACT.Identity, bias=bkcol[:, e:e + 1])\
                            .then_inc(pre2["act"].sem, 1)
                    for kind, i in order2:
                        if kind == "KB":
                            for e in range(KC):
                                w(c["KB.pool"].at(i, 2 * e + 1))
                                if i >= 2:
                                    w(c["XS.pe"].at(TB * (i - 1) - 1))
                                act.activation(kb[0][:, i % 2, e, :], kb32[:], ACT.Identity)\
                                    .then_inc(c["KB.act"].sem, 1)
                        elif kind == "VB":
                            w(c["VB.dve"].at(i, 1))
                            if i >= 1:
                                w(c["VC.pe"].at(i - 1))
                            act.activation(vc[0][:], v32[:], ACT.Identity).then_inc(c["VB.act"].sem, 1)
                        elif kind == "VC":
                            for q in range(3):
                                r0, r1 = 2 * q, min(2 * q + 2, RV)
                                w(c["VC.dve"].at(i, 1 + q))
                                if i >= 2:
                                    w(c["PV.pe"].at(TB // 2 * (i - 1) - 1))
                                act.activation(vb[0][:, i % 2, r0:r1].rearrange("p r k d -> p (r k d)"),
                                               vm[:, 0:r1 - r0].rearrange("p r k d -> p (r k d)"), ACT.Identity)\
                                    .then_inc(c["VC.act"].sem, 1)
                        elif kind == "TX":
                            w(c["TX.pe"].at(i))
                            if i >= 2:
                                w(c["XQ.pe"].at(i - 2))
                            act.activation(x1T[0][:, i % 2], bank("TX", i), ACT.Identity)\
                                .then_inc(c["TX.act"].sem, 1)
                        elif kind == "XQ":
                            w(c["XQ.pe"].at(i))
                            if i >= 2:
                                w(c["XS.pe"].at(2 * (i - 2) + 1))
                            for e in range(KC):
                                cut = slice(e * D, (e + 1) * D)
                                act.activation(xqT[0][:, i % 2, cut], bank("XQ", i)[:, cut], ACT.Identity,
                                               bias=bqcol[:, e:e + 1]).then_inc(c["XQ.act"].sem, 1)
                        elif kind == "EX":
                            w(c["XS.dve"].at(i))
                            act.activation(p_sb[:, i % NP, 0:PW], p_sb[:, i % NP, 0:PW], ACT.Exp)\
                                .then_inc(c["EX.act"].sem, 1)
                        elif kind == "TP":
                            t, u = divmod(i, 3)
                            j, k0, k1 = t // 2, 4 * u, min(4 * u + 4, 2 * RV)
                            w(c["TP.pe"].at(i))
                            if j >= 2:
                                w(c["PV.pe"].at(j - 2))
                            half = slice((t % 2) * P, (t % 2 + 1) * P)
                            act.activation(pT[0][:, j % 2, k0:k1, half],
                                           bank("TP", i)[:, 0:(k1 - k0) * P].rearrange("p (k t) -> p k t", t=P),
                                           ACT.Identity).then_inc(c["TP.act"].sem, 1)
                        elif kind == "PW":
                            w(c["PV.pe"].at(i))
                            if i >= 2:
                                w(c["XD.pe"].at(i - 2))
                            act.activation(oT[0][:, i % 2], bank("PV", i), ACT.Identity)\
                                .then_inc(c["PV.act"].sem, 1)
                        elif kind == "LN2B":
                            w(c["XD.pool"].at(i))
                            for t in range(2):
                                x2 = xs[:, 2 * i + t]
                                act.activation(x2, x2, ACT.Identity, bias=nb2[:, i % 2, t:t + 1],
                                               scale=rs2[:, i % 2, t:t + 1]).then_inc(c["LN2B.act"].sem, 1)

                @block.gpsimd
                def _(pool):
                    w = Waiter(pool)
                    phase1_over(w)
                    for n in range(NP):
                        ms = pool.memset(p_sb[:, n, PW:PPAD], 0.0)
                    ms.then_inc(pre2["pool"].sem, 1)
                    w((load2, NLOAD2), pre2["act"].at(KC - 1))
                    for kind, i in order2:
                        if kind == "KB":
                            for e in range(KC):
                                w(c["KB.act"].at(i, e), c["KB.pool"].at(i, 2 * e))
                                pool.tensor_tensor(heads(kb32[:]),
                                                   kT[:, e, i * SC:(i + 1) * SC].rearrange("p (o k) -> p o k", o=1)
                                                   .to_broadcast([P, HC, SC]),
                                                   mask_k[:].rearrange("p (h o) -> p h o", o=1)
                                                   .to_broadcast([P, HC, SC]), ALU.mult)\
                                    .then_inc(c["KB.pool"].sem, 1)
                                w(c["KB.act"].at(i, e + 1))
                                pool.tensor_tensor(kb[1][:, i % 2, e, :], kb32[:], f(kb[0][:, i % 2, e, :]),
                                                   ALU.subtract).then_inc(c["KB.pool"].sem, 1)
                        elif kind == "VC":
                            for q in range(3):
                                r0, r1 = 2 * q, min(2 * q + 2, RV)
                                w(c["VC.act"].at(i, 1 + q))
                                pool.tensor_tensor(vb[1][:, i % 2, r0:r1].rearrange("p r k d -> p (r k d)"),
                                                   vm[:, 0:r1 - r0].rearrange("p r k d -> p (r k d)"),
                                                   f(vb[0][:, i % 2, r0:r1].rearrange("p r k d -> p (r k d)")),
                                                   ALU.subtract).then_inc(c["VC.pool"].sem, 1)
                        elif kind == "XQ":
                            w(c["TX.pe"].at(i))
                            pool.tensor_tensor(xs[:, 2 * i:2 * i + 2, :], xs[:, 2 * i:2 * i + 2, :],
                                               bxd[:].rearrange("p (o d) -> p o d", o=1).to_broadcast([P, 2, D]),
                                               ALU.add).then_inc(c["XR.pool"].sem, 1)
                        elif kind == "SM":
                            w(c["SM.dve"].at(i))
                            pool.tensor_tensor(heads(p_sb[:, i % NP, 0:PW]), heads(p_sb[:, i % NP, 0:PW]),
                                               per_head(rc[:, i % 2]), ALU.mult).then_inc(c["SM.pool"].sem, 1)
                        elif kind == "XD":
                            w(c["XD.dve"].at(i))
                            if i >= 2:
                                w(c["LN2B.act"].at(i - 2))
                            r, nb = rs2[:, i % 2], nb2[:, i % 2]
                            pool.tensor_tensor(r, mv2[:, i % 2, :, 1], eps2, ALU.add)\
                                .then_inc(c["XD.pool"].sem, 1)
                            pool.tensor_tensor(nb, mv2[:, i % 2, :, 0], minus2, ALU.mult)\
                                .then_inc(c["XD.pool"].sem, 1)
                            w(c["XD.pool"].at(i, 1))
                            pool.tensor_tensor(r, r, half2, ALU.pow).then_inc(c["XD.pool"].sem, 1)
                            w(c["XD.pool"].at(i, 3))
                            pool.tensor_tensor(nb, nb, r, ALU.mult).then_inc(c["XD.pool"].sem, 1)

                @block.vector
                def _(dve):
                    w = Waiter(dve)
                    phase1_over(w)
                    w((load2, NLOAD2))
                    dve.tensor_copy(w_x[0][:], wx_raw[:, 0:2]).then_inc(pre2["dve"].sem, 1)
                    w(pre2["dve"].at(0))
                    dve.tensor_tensor(w_x[1][:].rearrange("p m k d -> p (m k d)"),
                                      wx_raw[:, 0:2].rearrange("p m k d -> p (m k d)"),
                                      f(w_x[0][:].rearrange("p m k d -> p (m k d)")), ALU.subtract)\
                        .then_inc(pre2["dve"].sem, 1)
                    dve.tensor_copy(sel[:], sel_raw[:]).then_inc(pre2["dve"].sem, 1)
                    for kind, i in order2:
                        if kind == "VB":
                            w(c["VB.pe"].at(i))
                            dve.tensor_tensor(v32[:], bank("VB", i)[0:SC, 0:D], bxv[0:SC, :], ALU.add)\
                                .then_inc(c["VB.dve"].sem, 1)
                            w(c["VB.act"].at(i))
                            if i >= 1:
                                w(c["VC.pe"].at(i - 1))
                            dve.tensor_tensor(vc[1][:], v32[:], f(vc[0][:]), ALU.subtract)\
                                .then_inc(c["VB.dve"].sem, 1)
                        elif kind == "VC":
                            for q in range(3):
                                r0, r1 = 2 * q, min(2 * q + 2, RV)
                                w(c["VC.pe"].at(i, 1 + q))
                                if q or i:
                                    w(c["VC.pool"].at(i, q))
                                dve.tensor_tensor(vm[:, 0:r1 - r0],
                                                  bank("VC", 3 * i + q)[:, 0:(r1 - r0) * D]
                                                  .rearrange("p (r k d) -> p r k d", k=KC, d=P),
                                                  mask_v[:, r0:r1].rearrange("p r (o d) -> p r o d", o=1)
                                                  .to_broadcast([P, r1 - r0, KC, P]), ALU.mult)\
                                    .then_inc(c["VC.dve"].sem, 1)
                        elif kind == "TX":
                            w(c["TX.act"].at(i))
                            dve.tensor_tensor(x1T[1][:, i % 2], bank("TX", i), f(x1T[0][:, i % 2]), ALU.subtract)\
                                .then_inc(c["TX.dve"].sem, 1)
                        elif kind == "XQ":
                            for e in range(KC):
                                cut = slice(e * D, (e + 1) * D)
                                w(c["XQ.act"].at(i))
                                dve.scalar_tensor_tensor(out=xqT[1][:, i % 2, cut], in0=bank("XQ", i)[:, cut],
                                                         scalar=bqcol[:, e:e + 1], in1=f(xqT[0][:, i % 2, cut]),
                                                         op0=ALU.add, op1=ALU.subtract)\
                                    .then_inc(c["XQ.dve"].sem, 1)
                        elif kind == "XS":
                            w(c["XS.pe"].at(i))
                            dve.tensor_reduce(mx[:, i % 2], heads(logits), AX, ALU.max)\
                                .then_inc(c["XS.dve"].sem, 1)
                            w(c["XS.dve"].at(i, 1))
                            if i >= NP:
                                w(c["TP.pe"].at(3 * (i - NP) + 2))
                            dve.tensor_tensor(heads(p_sb[:, i % NP, 0:PW]), heads(logits), per_head(mx[:, i % 2]),
                                              ALU.subtract).then_inc(c["XS.dve"].sem, 1)
                        elif kind == "SM":
                            w(c["EX.act"].at(i))
                            dve.tensor_reduce(sm[:, i % 2], heads(p_sb[:, i % NP, 0:PW]), AX, ALU.add)\
                                .then_inc(c["SM.dve"].sem, 1)
                            w(c["SM.dve"].at(i, 1))
                            if i >= 2:
                                w(c["SM.pool"].at(i - 2))
                            dve.reciprocal(rc[:, i % 2], sm[:, i % 2]).then_inc(c["SM.dve"].sem, 1)
                        elif kind == "TP":
                            t, u = divmod(i, 3)
                            j, k0, k1 = t // 2, 4 * u, min(4 * u + 4, 2 * RV)
                            half = slice((t % 2) * P, (t % 2 + 1) * P)
                            w(c["TP.act"].at(i))
                            dve.tensor_tensor(pT[1][:, j % 2, k0:k1, half],
                                              bank("TP", i)[:, 0:(k1 - k0) * P].rearrange("p (k t) -> p k t", t=P),
                                              f(pT[0][:, j % 2, k0:k1, half]), ALU.subtract)\
                                .then_inc(c["TP.dve"].sem, 1)
                        elif kind == "PW":
                            w(c["PV.act"].at(i))
                            dve.tensor_tensor(oT[1][:, i % 2], bank("PV", i), f(oT[0][:, i % 2]), ALU.subtract)\
                                .then_inc(c["PV.dve"].sem, 1)
                        elif kind == "XD":
                            w(c["XD.pe"].at(i), c["XR.pool"].at(i))
                            x2 = xs[:, 2 * i:2 * i + 2, :]
                            dve.tensor_tensor(x2, bank("XD", i).rearrange("p (t d) -> p t d", t=2), x2, ALU.add)\
                                .then_inc(c["XD.dve"].sem, 1)
                            w(c["XD.dve"].at(i, 1))
                            for t in range(2):
                                dve.bn_stats(st2[:, i % 2, t], xs[:, 2 * i + t]).then_inc(c["XD.dve"].sem, 1)
                            if i >= 2:
                                w(c["XD.pool"].at(i - 2))
                            for t in range(2):
                                w(c["XD.dve"].at(i, 2 + t))
                                dve.bn_aggr(mv2[:, i % 2, t], st2[:, i % 2, t]).then_inc(c["XD.dve"].sem, 1)

                @block.tensor
                def _(pe):
                    w = Waiter(pe)
                    phase1_over(w)
                    w((load2, NLOAD2))
                    for e in range(KC):
                        for k in range(KC):
                            mm = pe.matmul(ring[:, e, 0:B * SC], wx_raw[:, XKW, k, e * P:(e + 1) * P], cT[:, k, :],
                                           start=k == 0, stop=k == KC - 1)
                    mm.then_inc(pre2["pe"].sem, 1)
                    w(pre2["dve"].at(2), pre2["act"].at(KC - 1), pre2["pool"].at(0))
                    for kind, i in order2:
                        if kind in let_go and kind != "VC":
                            bank_free(w, kind, i)
                        if kind == "VB":
                            for k in range(KC):
                                mm = pe.matmul(bank("VB", i)[0:SC, 0:D], cT[:, k, i * SC:(i + 1) * SC],
                                               wx_raw[:, XVW, k, :], start=k == 0, stop=k == KC - 1)
                            mm.then_inc(c["VB.pe"].sem, 1)
                        elif kind == "VC":
                            w(c["VB.dve"].at(i))
                            for q in range(3):
                                bank_free(w, "VC", 3 * i + q)
                                for r in range(2 * q, min(2 * q + 2, RV)):
                                    for n in range(2):
                                        mm = pe.matmul(bank("VC", 3 * i + q)[:, (r % 2) * D:(r % 2 + 1) * D],
                                                       sel[:, r * P:(r + 1) * P], vc[n][:], start=n == 0, stop=n == 1)
                                mm.then_inc(c["VC.pe"].sem, 1)
                        elif kind == "TX":
                            for k in range(KC):
                                for t in range(2):
                                    mm = pe.transpose(bank("TX", i)[:, k * D + t * P:k * D + (t + 1) * P],
                                                      xs[:, 2 * i + t, k * P:(k + 1) * P], ident[:])
                            mm.then_inc(c["TX.pe"].sem, 1)
                        elif kind == "XQ":
                            w(c["TX.dve"].at(i))
                            for e in range(KC):
                                mm = split_product(pe, bank("XQ", i)[:, e * D:(e + 1) * D],
                                                   [hi_lo(w_x, slice(None), XQW, k, slice(e * P, (e + 1) * P)) for k in range(KC)],
                                                   [hi_lo(x1T, slice(None), i % 2, slice(k * D, (k + 1) * D)) for k in range(KC)])
                            mm.then_inc(c["XQ.pe"].sem, 1)
                        elif kind == "XS":
                            j, t = divmod(i, 2)
                            b = i // TB
                            w(c["XQ.dve"].at(j), c["KB.pool"].at(b))
                            if i:
                                w(c["XS.dve"].at(i - 1))
                            for part, lo, hi in LOGIT_CUTS:
                                mm = split_product(pe, logits[:, part * W + lo:part * W + hi],
                                                   [hi_lo(xqT, slice(None), j % 2, slice(part * D + t * P, part * D + (t + 1) * P))],
                                                   [hi_lo(kb, slice(None), b % 2, part, slice(lo, hi))])
                            mm.then_inc(c["XS.pe"].sem, 1)
                        elif kind == "TP":
                            t, u = divmod(i, 3)
                            w(c["SM.pool"].at(t))
                            for k in range(4 * u, min(4 * u + 4, 2 * RV)):
                                c0 = (k // RV) * W + (k % RV) * P
                                mm = pe.transpose(bank("TP", i)[:, (k % 4) * P:(k % 4 + 1) * P],
                                                  p_sb[:, t % NP, c0:c0 + P], ident[:])
                            mm.then_inc(c["TP.pe"].sem, 1)
                        elif kind in ("PV", "PW"):
                            b, k = i // (TB // 2), int(kind == "PW")
                            w(c["TP.dve"].at(3 * (2 * i + 1) + 2), c["VC.pool"].at(b))
                            mm = split_product(pe, bank("PV", i)[:, k * D:(k + 1) * D],
                                               [hi_lo(vb, slice(None), b % 2, r, k) for r in range(RV)],
                                               [hi_lo(pT, slice(None), i % 2, k * RV + r) for r in range(RV)])
                            if k:
                                mm.then_inc(c["PV.pe"].sem, 1)
                        elif kind == "XD":
                            w(c["PV.dve"].at(i))
                            for t in range(2):
                                mm = split_product(pe, bank("XD", i)[:, t * D:(t + 1) * D],
                                                   [hi_lo(oT, slice(None), i % 2, slice(k * D + t * P, k * D + (t + 1) * P)) for k in range(KC)],
                                                   [hi_lo(w_x, slice(None), XDW, k) for k in range(KC)])
                            mm.then_inc(c["XD.pe"].sem, 1)

        with ExitStack() as ph:
            wf_raw = tensor(ph, "wf_raw", [P, 3, KC, D])
            w_f = (tensor(ph, "wf_hi", [P, 3, KC, D], F32R), tensor(ph, "wf_lo", [P, 3, KC, D], F32R))
            mu = tensor(ph, "mu", [P, 2, KC])
            NM = 3
            x2T = tensor(ph, "x2T", [P, 2, KC, 2 * P + 1])
            dd = tensor(ph, "dd", [P, 2, KC, 2 * P])
            xm = tensor(ph, "xm", [P, 2, 2, KC, 2 * P])
            xmT = (tensor(ph, "xmT_hi", [P, NM, 2, KC, 2 * P], F32R), tensor(ph, "xmT_lo", [P, NM, 2, KC, 2 * P], F32R))
            gate = tensor(ph, "gate", [P, 2, 2 * D])
            kr = tensor(ph, "kr", [P, 2, BANK])
            kk = tensor(ph, "kk", [P, 2, BANK])
            kkT = (tensor(ph, "kkT_hi", [P, 2, BANK], F32R), tensor(ph, "kkT_lo", [P, 2, BANK], F32R))
            st3 = tensor(ph, "st3", [P, 2, 2, 6])
            mv3 = tensor(ph, "mv3", [P, 2, 2, 2])
            rs3 = tensor(ph, "rs3", [P, 2, 2])
            y = tensor(ph, "y", [P, 2, 2, D])
            pre3 = Count(sem("pre3_dve"))
            NLOAD3 = 5 * 16
            MIX_R, MIX_K, VW = range(3)
            out_dram = io["out"].rearrange("(i p) d -> p i d", p=P)

            with nc.Block() as block:
                def phase2_over(w):
                    w(c["PV.pe"].at(NJ - 1), c["XD.pe"].at(NJ - 1), c["LN2B.act"].at(NJ - 1),
                      c["XD.pool"].at(NJ - 1))

                @block.sync
                def _(sp):
                    w = Waiter(sp)
                    phase2_over(w)
                    for n, name in enumerate(("wrT", "wkcT", "wvcT")):
                        sp.dma_start(wf_raw[:, n], rows(name)).then_inc(load3, 16)
                    sp.dma_start(mu[:, 0], col("mu_r")).then_inc(load3, 16)
                    sp.dma_start(mu[:, 1], col("mu_k")).then_inc(load3, 16)
                    for kind, i in order3:
                        if kind == "LN3B":
                            w(c["LN3B.dve"].at(i))
                            sp.dma_start(out_dram[:, 2 * i:2 * i + 2, :], y[:, i % 2]).then_inc(c[f"OUT.dma{i % 2}"].sem, 16)
                    w(c["OUT.dma0"].at(NJ // 2 - 1), c["OUT.dma1"].at(NJ // 2 - 1))

                @block.scalar
                def _(act):
                    w = Waiter(act)
                    phase2_over(w)
                    for kind, i in order3:
                        if kind == "TY":
                            w(c["TY.pe"].at(i))
                            if i >= 2:
                                w(c["TY.dve"].at(i - 2), c["TY.pool"].at(i - 1))
                            act.activation(x2T[:, i % 2, :, 1:2 * P + 1],
                                           bank("TY", i).rearrange("p (k t) -> p k t", k=KC), ACT.Identity)\
                                .then_inc(c["TY.act"].sem, 1)
                        elif kind == "TH":
                            w(c["TY.dve"].at(i))
                            if i >= NM:
                                w(c["FR.pe"].at(i - NM), c["FK.pe"].at(i - NM))
                            act.activation(xmT[0][:, i % NM].rearrange("p m k t -> p (m k t)"),
                                           xm[:, i % 2].rearrange("p m k t -> p (m k t)"), ACT.Identity)\
                                .then_inc(c["TH.act"].sem, 1)
                        elif kind == "FR":
                            w(c["FR.pe"].at(i))
                            if i >= 2:
                                w(c["FV.dve"].at(i - 2, 1))
                            act.activation(gate[:, i % 2], bank("FR", i), ACT.Sigmoid).then_inc(c["FR.act"].sem, 1)
                        elif kind == "FK":
                            w(c["FK.pe"].at(i))
                            if i >= 2:
                                w(c["FK.dve"].at(i - 2))
                            act.activation(kr[:, i % 2], bank("FK", i), ACT.Relu).then_inc(c["FK.act"].sem, 1)
                            w(c["FK.act"].at(i, 1))
                            if i >= 2:
                                w(c["FV.pe"].at(i - 2))
                            for square in (kkT[0], kk):
                                act.activation(square[:, i % 2], kr[:, i % 2], ACT.Square)\
                                    .then_inc(c["FK.act"].sem, 1)

                @block.gpsimd
                def _(pool):
                    w = Waiter(pool)
                    phase2_over(w)
                    for kind, i in order3:
                        if kind == "TY":
                            if i >= 2:
                                w(c["TY.dve"].at(i - 2))
                            if i % (TB // 2) == 0:
                                pool.memset(x2T[:, i % 2, :, 0:1], 0.0).then_inc(c["TY.pool"].sem, 1)
                            else:
                                w(c["TY.act"].at(i - 1))
                                pool.tensor_copy(x2T[:, i % 2, :, 0:1], x2T[:, (i - 1) % 2, :, 2 * P:2 * P + 1])\
                                    .then_inc(c["TY.pool"].sem, 1)
                            w(c["TY.act"].at(i), c["TY.pool"].at(i, 1))
                            pool.tensor_tensor(dd[:, i % 2], x2T[:, i % 2, :, 1:2 * P + 1], x2T[:, i % 2, :, 0:2 * P],
                                               ALU.subtract).then_inc(c["TY.pool"].sem, 1)
                        elif kind == "TH":
                            w(c["TH.act"].at(i))
                            if i >= NM:
                                w(c["FR.pe"].at(i - NM), c["FK.pe"].at(i - NM))
                            pool.tensor_tensor(xmT[1][:, i % NM].rearrange("p m k t -> p (m k t)"),
                                               xm[:, i % 2].rearrange("p m k t -> p (m k t)"),
                                               f(xmT[0][:, i % NM].rearrange("p m k t -> p (m k t)")),
                                               ALU.subtract).then_inc(c["TH.pool"].sem, 1)
                        elif kind == "FV":
                            w(c["FV.dve"].at(i))
                            if i >= 2:
                                w(c["LN3B.dve"].at(i - 2))
                            r = rs3[:, i % 2]
                            pool.tensor_tensor(r, mv3[:, i % 2, :, 1], eps2, ALU.add).then_inc(c["FV.pool"].sem, 1)
                            w(c["FV.pool"].at(i, 1))
                            pool.tensor_tensor(r, r, half2, ALU.pow).then_inc(c["FV.pool"].sem, 1)

                @block.vector
                def _(dve):
                    w = Waiter(dve)
                    phase2_over(w)
                    w((load3, NLOAD3))
                    flat = "p m k d -> p (m k d)"
                    dve.tensor_copy(w_f[0][:], wf_raw[:]).then_inc(pre3.sem, 1)
                    w(pre3.at(0))
                    dve.tensor_tensor(w_f[1][:].rearrange(flat), wf_raw[:].rearrange(flat),
                                      f(w_f[0][:].rearrange(flat)), ALU.subtract).then_inc(pre3.sem, 1)
                    for kind, i in order3:
                        if kind == "TY":
                            w(c["TY.pool"].at(i))
                            if i >= 2:
                                w(c["TH.pool"].at(i - 2))
                            for m in range(2):
                                for k in range(KC):
                                    dve.scalar_tensor_tensor(out=xm[:, i % 2, m, k], in0=dd[:, i % 2, k],
                                                             scalar=mu[:, m, k:k + 1], in1=x2T[:, i % 2, k, 0:2 * P],
                                                             op0=ALU.mult, op1=ALU.add)\
                                        .then_inc(c["TY.dve"].sem, 1)
                        elif kind == "FK":
                            w(c["FK.act"].at(i))
                            if i >= 2:
                                w(c["FV.pe"].at(i - 2))
                            dve.tensor_tensor(kkT[1][:, i % 2], kk[:, i % 2], f(kkT[0][:, i % 2]), ALU.subtract)\
                                .then_inc(c["FK.dve"].sem, 1)
                        elif kind == "FV":
                            w(c["FV.pe"].at(i), c["FR.act"].at(i))
                            if i >= 2:
                                w(c[f"OUT.dma{i % 2}"].at(i // 2 - 1))
                            yy = y[:, i % 2]
                            dve.tensor_tensor(yy, bank("FV", i).rearrange("p (t d) -> p t d", t=2),
                                              gate[:, i % 2].rearrange("p (t d) -> p t d", t=2), ALU.mult)\
                                .then_inc(c["FV.dve"].sem, 1)
                            w(c["FV.dve"].at(i, 1))
                            dve.tensor_tensor(yy, yy, xs[:, 2 * i:2 * i + 2, :], ALU.add)\
                                .then_inc(c["FV.dve"].sem, 1)
                            w(c["FV.dve"].at(i, 2))
                            for t in range(2):
                                dve.bn_stats(st3[:, i % 2, t], y[:, i % 2, t]).then_inc(c["FV.dve"].sem, 1)
                            if i >= 2:
                                w(c["FV.pool"].at(i - 2))
                            for t in range(2):
                                w(c["FV.dve"].at(i, 3 + t))
                                dve.bn_aggr(mv3[:, i % 2, t], st3[:, i % 2, t]).then_inc(c["FV.dve"].sem, 1)
                        elif kind == "LN3B":
                            w(c["FV.pool"].at(i))
                            for t in range(2):
                                yt = y[:, i % 2, t]
                                dve.tensor_scalar(yt, yt, mv3[:, i % 2, t, 0:1], rs3[:, i % 2, t:t + 1],
                                                  ALU.subtract, ALU.mult).then_inc(c["LN3B.dve"].sem, 1)

                @block.tensor
                def _(pe):
                    w = Waiter(pe)
                    phase2_over(w)
                    w(pre3.at(1))
                    for kind, i in order3:
                        if kind in let_go:
                            bank_free(w, kind, i)
                        if kind == "TY":
                            for k in range(KC):
                                for t in range(2):
                                    mm = pe.transpose(bank("TY", i)[:, k * D + t * P:k * D + (t + 1) * P],
                                                      xs[:, 2 * i + t, k * P:(k + 1) * P], ident[:])
                            mm.then_inc(c["TY.pe"].sem, 1)
                        elif kind == "FR":
                            w(c["TH.pool"].at(i))
                            for t in range(2):
                                mm = split_product(pe, bank("FR", i)[:, t * D:(t + 1) * D],
                                                   [hi_lo(xmT, slice(None), i % NM, MIX_R, k, slice(t * P, (t + 1) * P)) for k in range(KC)],
                                                   [hi_lo(w_f, slice(None), MIX_R, k) for k in range(KC)])
                            mm.then_inc(c["FR.pe"].sem, 1)
                        elif kind == "FK":
                            for e in range(KC):
                                mm = split_product(pe, bank("FK", i)[:, e * D:(e + 1) * D],
                                                   [hi_lo(w_f, slice(None), MIX_K, k, slice(e * P, (e + 1) * P)) for k in range(KC)],
                                                   [hi_lo(xmT, slice(None), i % NM, MIX_K, k) for k in range(KC)])
                            mm.then_inc(c["FK.pe"].sem, 1)
                        elif kind == "FV":
                            w(c["FK.dve"].at(i))
                            for t in range(2):
                                mm = split_product(pe, bank("FV", i)[:, t * D:(t + 1) * D],
                                                   [hi_lo(kkT, slice(None), i % 2, slice(k * D + t * P, k * D + (t + 1) * P)) for k in range(KC)],
                                                   [hi_lo(w_f, slice(None), VW, k) for k in range(KC)])
                            mm.then_inc(c["FV.pe"].sem, 1)


def shape_constants():
    row = np.arange(P)
    mask_k = (row[:, None] // DH == np.arange(HC)[None, :]).astype(np.float32) * np.float32(DH ** -0.5)
    flat = np.arange(RV * P)
    sel = ((flat[None, :] % SC == np.arange(SC)[:, None]) & (flat[None, :] < W)).astype(np.float32)
    head = flat.reshape(RV, P).T // SC
    mask_v = (head[:, :, None] == (row // DH)[None, None, :]).astype(np.float32)
    return {"ident": np.eye(P, dtype=np.float32), "mask_k": mask_k, "sel": sel,
            "mask_v": np.ascontiguousarray(mask_v)}


def kernel(**inputs):
    import numpy as _np
    import concourse.bacc as _bacc
    from concourse.bass_utils import run_bass_kernel_spmd as _run

    a = {k: _np.asarray(v) for k, v in inputs.items()}
    x = a["x"].reshape(B * S, D)
    laid = {
        "x": x, "xT": x.T, "cT": a["ctx_1024"].reshape(B * SC, D).T,
        "wqT": a["L0_attn_Wq"].T, "wkT": a["L0_attn_Wk"].T, "wv": a["L0_attn_Wv"], "woT": a["L0_attn_Wo"].T,
        "bq": a["L0_attn_bq"], "bk": a["L0_attn_bk"], "bv": a["L0_attn_bv"], "bo": a["L0_attn_bo"],
        "ls": a["L0_attn_layerscale"],
        "xwqT": a["L0_xattn_wq_w"].T, "xwkT": a["L0_xattn_wk_w"].T, "xwvT": a["L0_xattn_wv_w"].T,
        "xwdT": a["L0_xattn_dense_w"].T,
        "xbq": a["L0_xattn_wq_b"], "xbk": a["L0_xattn_wk_b"], "xbv": a["L0_xattn_wv_b"],
        "xbd": a["L0_xattn_dense_b"],
        "wrT": a["L0_ffn_W_r"].T, "wkcT": a["L0_ffn_W_k"].T, "wvcT": a["L0_ffn_W_v"].T,
        "mu_r": a["L0_ffn_mu_r"], "mu_k": a["L0_ffn_mu_k"],
    }
    for name in ("bv", "xbq", "xbk", "mu_r", "mu_k"):
        laid[name] = laid[name].reshape(KC, P).T
    laid.update(shape_constants())
    nc = _bacc.Bacc("TRN2", target_bir_lowering=False, num_devices=1)
    arrays, io = {}, {}
    for name, v in laid.items():
        v = _np.ascontiguousarray(v)
        arrays[f"in_{name}"] = v
        io[name] = nc.dram_tensor(f"in_{name}", v.shape, mybir.dt.from_np(v.dtype), kind="ExternalInput").ap()
    io["out"] = nc.dram_tensor("out_y", (B * S, D), F32, kind="ExternalOutput").ap()
    decoder_layer(nc, io)
    r = _run(nc, [arrays], core_ids=[0])
    return r.results[0]["out_y"].reshape(B, S, D)
```

```python
from contextlib import ExitStack

import numpy as np

import concourse.bass as bass
from concourse import mybir

F32 = mybir.dt.float32
F32R = mybir.dt.float32r
ALU = mybir.AluOpType
ACT = mybir.ActivationFunctionType
AX = mybir.AxisListType.X

P = 128
B, S, D = 4, 1024, 256
KC = D // P
NT = B * S // P
TB = S // P
NG = NT // 4
NJ = NT // 2
H, DH = 16, 16
SC = 77
HC = H // KC
SP = SC + 1
FO = SP // 2
WP = HC * SP
RV = -(-WP // P)
PW = KC * WP
PPAD = WP + RV * P
EPS = 1e-5
BANK = 512
NX = 3
NXR = 2
NA = 4
NAR = 3
NY = 3
NP = 4
P3_START = 32
RING = 5
PIECES = ((0, 5), (5, 11), (11, H))
NARROW = 256
WIDE = 5 * SC + 1
MIDDLE = 6 * SC
WK = WIDE + NARROW
KEYS = ((0, 0, 5, 0), (0, 5, 8, WIDE), (1, 8, 11, NARROW - 3 * SC), (1, 11, H, NARROW))
PRODUCTS = (((0, 0, WIDE, 0),),
            ((0, WIDE, WK, 0), (1, 0, NARROW, MIDDLE - NARROW)),
            ((1, NARROW, WK, 0),))


class Count:

    def __init__(self, sem, per=1):
        self.sem, self.per = sem, per

    def at(self, i, k=None):
        return self.sem, self.per * i + (self.per if k is None else k)


def steps(order, engine):
    return [(kind, i) for kind, i, engines in order if engine in engines]


class Waiter:

    def __init__(self, eng):
        self.eng, self.seen = eng, {}

    def __call__(self, *pairs):
        for sem, value in pairs:
            if value > self.seen.get(sem.name, 0):
                self.seen[sem.name] = value
                self.eng.wait_ge(sem, value)


LOAD_FROM = (-7.0, 1.0, 16.5, 31.0)
PROJECT = (
    ("XT", NJ, "first", (("S", -0.39), ("A", 1.56), ("G", -0.39))),
    ("QK", NT, "tile", (("P", -0.4), ("D", -0.4), ("G", -2.35))),
    ("WO", 1, "tile", (("D", -0.75), ("G", -3.3))),
    ("WV", 1, "second", (("P", 0.25), ("A", 0.55), ("D", 0.55))),
    ("QN", NT, "tile", (("D", 1.35),)),
    ("TQK", NT, "tile", (("P", 3.0), ("A", 3.0), ("D", 3.0))),
    ("V", NJ, "second", (("P", 1.4), ("D", 1.4), ("A", 2.2), ("G", 1.4))),
)
ATTEND = (
    ("ST", NG * TB, 1, (("P", 0.6), ("A", 0.6), ("G", 0.6), ("D", 1.6))),
    ("AV", NG * TB, 1, (("P", 3.8),)),
    ("XL", NG, TB, (("S", -1.8),)),
    ("LN1A", NG, TB, (("D", 10.6),)),
    ("LN1S", NG - 1, TB, (("D", 11.7), ("G", 11.7))),
    ("LN1B", NG - 1, TB, (("D", 13.9),)),
)

CROSS = (
    ("EX", "third", 0, (("A", 0.0),)),
    ("TP", "third", 3, (("P", 0.0), ("A", 0.0), ("D", 0.0))),
    ("XS", "third", -1, (("P", 1.4),)),
    ("XM", "third", -1, (("D", 0.85),)),
    ("FO", "tile", 1, (("G", 0.0),)),
    ("SMa", "tile", 1, (("D", 0.3),)),
    ("SM", "tile", 1, (("D", 0.6), ("G", 2.1))),
    ("TX", "pair", -2, (("P", 0.5), ("A", 0.0), ("D", 0.9))),
    ("XR", "pair", -2, (("G", 3.95),)),
    ("XQ", "pair", -2, (("P", 4.25), ("A", 4.4), ("D", 4.4))),
    ("PVa", "pair", 2, (("P", 5.3),)),
    ("PV", "pair", 2, (("P", 5.65), ("A", 5.8), ("D", 5.7))),
    ("PWa", "pair", 3, (("P", 2.0),)),
    ("PW", "pair", 3, (("P", 2.25), ("A", 2.7), ("D", 2.7))),
    ("XDa", "pair", 4, (("D", 1.7),)),
    ("XD", "pair", 4, (("P", 1.1), ("D", 2.2), ("G", 4.3))),
    ("LN2B", "pair", 4, (("A", 8.5), ("D", 12.5))),
)
NEXT_BATCH = (
    ("KB", -6, 0, (("G", 0.4),)),
    ("KH", -5, 0, (("A", 0.75),)),
    ("KL", -4, 0, (("G", 0.5),)),
    ("VB", -4, 0, (("P", 0.0), ("A", 0.25), ("D", 0.0))),
    ("VC", -3, 0, (("P", 3.05), ("D", 2.9), ("A", 6.5), ("G", 7.0))),
    ("VC", -2, 1, (("P", 3.4), ("D", 3.5), ("A", 6.05), ("G", 6.8))),
    ("VC", -1, 2, (("P", 2.9), ("D", 3.0), ("A", 5.95), ("G", 6.1))),
)

MIX = (
    ("PRE3", 1, (("S", -17.0), ("D", -2.0))),
    ("TY", NJ, (("P", 2.73), ("A", 3.0), ("G", 3.6), ("D", 5.95))),
    ("TH", NJ, (("A", 7.91), ("G", 8.96))),
    ("FR", NJ, (("P", 12.61), ("A", 13.77))),
    ("FKa", NJ, (("A", 11.98),)),
    ("FK", NJ, (("P", 11.42), ("A", 12.43), ("D", 11.98))),
    ("FVa", NJ, (("D", 14.99),)),
    ("FVb", NJ, (("D", 16.24),)),
    ("FV", NJ, (("P", 14.94), ("D", 17.14), ("G", 17.99))),
    ("LN3B", NJ, (("D", 20.9), ("A", 22.09), ("S", 21.44))),
)
PREPARE = (
    ("PRE2", 0, (("S", 48.45), ("D", 53.45), ("G", 66.45))),
    ("K2", 0, (("P", 55.45), ("A", 55.45))),
    ("K2", 1, (("P", 55.45), ("A", 55.45))),
    ("KB", 0, (("G", 56.45),)),
    ("KH", 0, (("A", 58.45),)),
    ("KL", 0, (("G", 58.45),)),
    ("VB", 0, (("P", 56.45), ("A", 57.45), ("D", 57.45))),
    ("VC", 0, (("P", 59.45), ("D", 59.45), ("A", 60.45), ("G", 60.45))),
    ("VC", 1, (("P", 60.45), ("D", 60.45), ("A", 61.45), ("G", 61.45))),
    ("VC", 2, (("P", 61.45), ("D", 62.0), ("A", 62.45), ("G", 62.45))),
    ("KB", 1, (("G", 59.45),)),
    ("KH", 1, (("A", 60.45),)),
    ("KL", 1, (("G", 61.45),)),
    ("XR", 0, (("G", 60.45),)),
    ("TX", 0, (("P", 62.45), ("A", 63.45), ("D", 63.45))),
    ("XQ", 0, (("P", 65.45), ("A", 65.45), ("D", 65.45))),
    ("TX", 1, (("P", 63.45), ("A", 64.45), ("D", 64.45))),
    ("XR", 1, (("G", 63.85),)),
    ("XQ", 1, (("P", 65.45), ("A", 65.45), ("D", 65.45))),
)


def project_slot(i):
    b, t = divmod(i, TB)
    return LOAD_FROM[b] + (2 * t if b else t)


def layer_order():
    order = []

    def put(kind, i, n, engines):
        if 0 <= i < n:
            order.append((kind, i, engines))

    here = []
    for kind, count, per, places in PROJECT:
        for j in range(count):
            i = j - 2 if kind == "XT" else j
            base = project_slot({"tile": i, "first": 2 * i, "second": 2 * i + 1}[per]) if i >= 0 else -99
            here += [(base + at, kind, j, letter) for letter, at in places]
    for kind, count, every, places in ATTEND:
        here += [(every * j + at, kind, j, letter) for j in range(count) for letter, at in places]
    for kind, j, places in PREPARE:
        here += [(at, kind, j, letter) for letter, at in places]
    here.sort(key=lambda x: x[0])
    order += [event[1:] for event in here]

    for k in range(3):
        order += [("XS", k, "P"), ("XM", k, "D")]
    order += [("LN1S", NG - 1, "DG"), ("LN1B", NG - 1, "D")]
    for i in range(NT + P3_START + NJ + 8):
        s, odd = divmod(i, 2)
        here = []
        for kind, per, lag, places in CROSS:
            for letter, at in places:
                if per == "third":
                    here += [(at + k, kind, 3 * (i - lag) + k, 3 * NT, letter) for k in range(3)]
                elif per == "tile":
                    here.append((at, kind, i - lag, NT, letter))
                elif int(at) % 6 // 3 == odd:
                    here.append((at % 3, kind, s - lag - int(at) // 6, NJ, letter))
        for kind, b_slot, what, places in NEXT_BATCH:
            for bb in range(1, B):
                for letter, at in places:
                    if i - bb * TB == b_slot + int(at // 3) and (kind[0] != "K" or bb > 1):
                        here.append((at % 3, kind, (3 * bb + what if kind == "VC" else bb), 3 * B, letter))
        for kind, count, places in MIX:
            for letter, at in places:
                here.append((at % 3, kind, i - P3_START - int(at // 3), count, letter))
        here.sort(key=lambda x: x[0])
        for _, kind, n, end, letter in here:
            put(kind, n, end, letter)
    return order


def decoder_layer(nc, io):
    ctx = ExitStack()
    with ctx:
        def sem(name):
            return ctx.enter_context(nc.semaphore(name))

        def tensor(stack, name, shape, dt=F32):
            return stack.enter_context(nc.sbuf_tensor(name, shape, dt))

        def halves(stack, name, shape):
            return tensor(stack, name + "_hi", shape, F32R), tensor(stack, name + "_lo", shape, F32R)

        big = ctx.enter_context(nc.psum_tensor("big", [P, 3 * BANK], F32))
        ring = ctx.enter_context(nc.psum_tensor("ring", [P, RING, BANK], F32))
        acc = big[:, 0:2 * BANK].rearrange("p (t d) -> p t d", d=D)
        logits = [big[:, BANK * k:BANK * k + (h1 - h0) * SC] for k, (h0, h1) in enumerate(PIECES)]

        xs = tensor(ctx, "xs", [P, NT, D])
        ident = tensor(ctx, "ident", [P, P])
        consts = tensor(ctx, "consts", [P, 12])
        nlogs = tensor(ctx, "nlogs", [P, 1])
        eps4, half4, minus4 = (consts[:, 4 * n:4 * n + 4] for n in range(3))
        st1, mv1, rs1 = tensor(ctx, "st1", [P, 4, 2, 6]), tensor(ctx, "mv1", [P, 4, 2, 2]), tensor(ctx, "rs1", [P, 4, 2])
        stl, mvl, rsl = tensor(ctx, "stl", [P, 4, 6]), tensor(ctx, "mvl", [P, 4, 2]), tensor(ctx, "rsl", [P, 4])
        st2, mv2, rs2 = tensor(ctx, "st2", [P, 2, 2, 6]), tensor(ctx, "mv2", [P, 2, 2, 2]), tensor(ctx, "rs2", [P, 2, 2])
        nb2 = tensor(ctx, "nb2", [P, 2, 2])
        nb3 = tensor(ctx, "nb3", [P, 2, 2])
        st3, mv3, rs3 = tensor(ctx, "st3", [P, 2, 2, 6]), tensor(ctx, "mv3", [P, 2, 2, 2]), tensor(ctx, "rs3", [P, 2, 2])

        with ExitStack() as ph:
            qkT0, vv0 = halves(ph, "qkT0", [P, 4, S]), halves(ph, "vv0", [P, TB, D])
            xT = halves(ph, "xT", [P, NX, KC, 2 * P])
            xraw = tensor(ph, "xraw", [P, NXR, KC, 2 * P])
            w_qk = halves(ph, "wqk", [P, KC, 2 * D])
            wraw = tensor(ph, "wraw", [P, KC, 2 * D])
            w_vo = halves(ph, "wvo", [P, KC, D])
            wv_raw = tensor(ph, "wv_raw", [P, KC, D])
            wo_ls = tensor(ph, "wo_ls", [P, KC, D])
            bvwide = tensor(ph, "bvwide", [P, KC, P])
            qk_sb = tensor(ph, "qk_sb", [P, 4, 2 * D])
            v_sb = tensor(ph, "v_sb", [P, 2, 2 * D])
            qkT1, vv1 = halves(ph, "qkT1", [P, 4, S]), halves(ph, "vv1", [P, TB, D])
            qkT, vv = (qkT0, qkT1), (vv0, vv1)
            aT = halves(ph, "aT", [P, NA, BANK])
            a_sb = tensor(ph, "a_sb", [P, NAR, BANK])
            bqk = tensor(ph, "bqk", [P, 2 * D])
            bvcol = tensor(ph, "bvcol", [P, KC])
            bvo = tensor(ph, "bvo", [P, D])
            bo = tensor(ph, "bo", [P, D])
            ls = tensor(ph, "ls", [P, D])

        with ExitStack() as ph:
            kb0 = halves(ph, "kb0", [P, KC, WK])
            vb0 = halves(ph, "vb0", [P, RV, KC, P])
            wx_raw = tensor(ph, "wx_raw", [P, 4, KC, D])
            cT = tensor(ph, "cT", [P, KC, B * SC])
            kT = tensor(ph, "kT", [P, KC, B * SC])
            mask_k = tensor(ph, "mask_k", [P, HC])
            mask_v = tensor(ph, "mask_v", [P, RV, P])
            sel_raw = tensor(ph, "sel_raw", [SC, RV * P])
            sel = tensor(ph, "sel", [SC, RV * P], F32R)
            kb32 = tensor(ph, "kb32", [P, KC, WK])
            v32 = tensor(ph, "v32", [SC, D])
            vc = halves(ph, "vc", [SC, D])
            vm = tensor(ph, "vm", [P, RV, KC, P])
            x1T = halves(ph, "x1T", [P, 2, BANK])
            xqT = halves(ph, "xqT", [P, 2, BANK])
            kb1 = halves(ph, "kb1", [P, KC, WK])
            w_x = halves(ph, "wx", [P, 2, KC, D])
            bqcol, bkcol = tensor(ph, "bqcol", [P, KC]), tensor(ph, "bkcol", [P, KC])
            bxv, bxd = tensor(ph, "bxv", [P, D]), tensor(ph, "bxd", [P, D])
            vb1 = halves(ph, "vb1", [P, RV, KC, P])
            kb, vb = (kb0, kb1), (vb0, vb1)
            p_sb = tensor(ph, "p_sb", [P, NP, PPAD])
            neg_mx, sm, rc = (tensor(ph, name, [P, 2, H]) for name in ("neg_mx", "sm", "rc"))
            pT = halves(ph, "pT", [P, 2, 2 * RV, 2 * P])
            oT = halves(ph, "oT", [P, 2, BANK])
            fold = tensor(ph, "fold", [P, H * FO])

        with ExitStack() as ph:
            wf_raw = tensor(ph, "wf_raw", [P, 3, KC, D])
            w_f = halves(ph, "wf", [P, 3, KC, D])
            mu = tensor(ph, "mu", [P, 2, KC])
            x2T = tensor(ph, "x2T", [P, 2, KC, 2 * P + 1])
            dd = tensor(ph, "dd", [P, 2, KC, 2 * P])
            xm = tensor(ph, "xm", [P, 2, 2, KC, 2 * P])
            xmT = halves(ph, "xmT", [P, 2, 2, KC, 2 * P])
            gate = tensor(ph, "gate", [P, 3, 2 * D])
            kr = tensor(ph, "kr", [P, 2, BANK])
            kk = tensor(ph, "kk", [P, 2, BANK])
            kkT = halves(ph, "kkT", [P, 2, BANK])
            y = tensor(ph, "y", [P, NY, 2, D])

        names = {
            "W.dve": 4, "WO.dve": 1, "WO.pool": 2, "W.pe": 1, "W.act": 1, "W.pool": 1,
            "XT.dma0": 16, "XT.dma1": 16, "XT.act": 1, "XT.pool": 1, "QK.pe": 1, "QK.dve": 5, "QK.pool": 2,
            "QN.dve": 2, "TQK.pe": 1, "TQK.act": 1, "TQK.dve": 1, "V.pe": 1, "V.dve": 1,
            "V.act": 1, "V.pool": 1, "ST.pe": 1, "ST.act": 2, "ST.dve": 1, "AV.pe": 1,
            "LN1A.dve": 2, "LN1S.dve": 8, "LN1S.pool": 2, "LN1B.dve": 4, "XB.pool": 1,
            "PRE2.dve": 3, "PRE2.pool": 1, "K2.pe": 1, "K2.act": 1,
            "KB.pool": 4, "KZ.pool": 1, "KH.act": 2, "KL.pool": 2, "VB.pe": 1, "VB.dve": 2, "VB.act": 1,
            "VC.pe": 1, "VC.dve": 1, "VC.act": 1, "VC.pool": 1,
            "TX.pe": 1, "TX.act": 1, "TX.dve": 1, "XR.pool": 1, "XQ.pe": 1, "XQ.act": 2,
            "XQ.dve": 2, "XS.pe": 1, "XM.dve": 1, "EX.act": 1, "FO.pool": 1, "SMa.dve": 1, "SM.dve": 1, "SM.pool": 1,
            "TP.pe": 1, "TP.act": 1, "TP.dve": 1, "PV.pe": 1, "PV.act": 1, "PV.dve": 1, "PW.pe": 1, "PW.act": 1, "PW.dve": 1,
            "XD.pe": 1, "XDa.dve": 1, "XD.dve": 4, "XD.pool": 4, "LN2B.act": 1, "LN2B.dve": 1,
            "PRE3.dve": 2, "TY.pe": 1, "TY.act": 1, "TY.pool": 2, "TY.dve": 4, "TH.act": 1, "TH.pool": 1,
            "FR.pe": 1, "FR.act": 1, "FK.pe": 1, "FKa.act": 1, "FK.act": 2, "FK.dve": 1,
            "FV.pe": 1, "FVa.dve": 1, "FVb.dve": 1, "FV.dve": 4, "FV.pool": 2, "LN3B.dve": 1, "LN3B.act": 2,
            "OUT.dma0": 16, "OUT.dma1": 16, "OUT.dma2": 16,
        }
        c = {name: Count(sem("s_" + name.replace(".", "_")), per) for name, per in names.items()}
        load_w, load_b, load_id, load1, load2, load3 = (sem(n) for n in ("load_w", "load_b", "load_id", "load1", "load2", "load3"))
        load_x = [sem(f"load_x{g}") for g in range(NG)]
        LOAD_W, LOAD_B, LOAD1, LOAD2, LOAD3 = (n * 16 for n in (2, 2, 5, 12, 5))
        W_QK_LO, W_VO_LO, W_BVO = 2, 3, 4
        XQW, XDW, XKW, XVW = range(4)
        MIX_R, MIX_K, VW = range(3)

        order = layer_order()
        let_go = {
            "QK": lambda i: c["QK.dve"].at(i, 1), "TQK": c["TQK.dve"].at, "V": c["V.dve"].at,
            "ST": lambda n: c["ST.act"].at(n, 1), "K2": c["K2.act"].at,
            "VB": lambda i: c["VB.dve"].at(i, 1), "VC": c["VC.dve"].at,
            "TX": c["TX.dve"].at, "XQ": c["XQ.dve"].at, "TP": c["TP.dve"].at, "PVa": c["PV.dve"].at, "PWa": c["PW.dve"].at,
            "XD": c["XDa.dve"].at, "FV": c["FVa.dve"].at,
        }
        own_bank = {"TY": (0, c["TY.act"].at), "FR": (1, c["FR.act"].at),
                    "FK": (2, c["FKa.act"].at)}
        takers = [step for step in steps(order, "P") if step[0] in let_go]
        place = {step: n for n, step in enumerate(takers)}

        def bank(kind, i):
            if kind in own_bank:
                n = own_bank[kind][0]
                return big[:, n * BANK:(n + 1) * BANK]
            return ring[:, place[kind, i] % RING, :]

        def bank_free(w, kind, i):
            if kind in own_bank:
                w(own_bank[kind][1](i - 1) if i else c["EX.act"].at(3 * NT - 1))
                return
            n = place[kind, i]
            if n >= RING:
                k, m = takers[n - RING]
                w(let_go[k](m))

        def split_product(eng, out, stationary, moving, first=True, last=True, check=True):
            n = len(stationary)
            for k in range(n):
                (sh, sl), (mh, ml) = stationary[k], moving[k]
                for q, (s_, m_) in enumerate(((sh, mh), (sh, ml), (sl, mh))):
                    mm = eng.matmul(out, s_, m_, start=first and k == 0 and q == 0,
                                    stop=last and k == n - 1 and q == 2, skip_group_check=not check)
            return mm

        def hi_lo(pair, *at):
            return tuple(t[(slice(None),) + at] for t in pair)

        def f(ap):
            return ap.bitcast(F32)

        def bc(name, n=D):
            return io[name].rearrange("(o n) -> o n", o=1).to_broadcast([P, n])

        def rows(name):
            return io[name].rearrange("(k p) n -> p k n", p=P)

        def tiles(ap, n=2):
            return ap.rearrange("p (t d) -> p t d", t=n)

        def each_tile(ap, n):
            return ap.rearrange("p (o d) -> p o d", o=1).to_broadcast([P, n, D])

        def heads(ap):
            return ap.rearrange("p (h k) -> p h k", k=SC)

        def weights(t):
            return p_sb[:, t % NP, 0:PW].rearrange("p (h k) -> p h k", k=SP)

        def vc_rows(n):
            b, q = divmod(n, 3)
            return b, 2 * q, min(2 * q + 2, RV)

        def tp_parts(n):
            t, u = divmod(n, 3)
            return t, t // 2, 4 * u, min(4 * u + 4, 2 * RV), slice((t % 2) * P, (t % 2 + 1) * P)

        def logits_made(t):
            return c["XS.pe"].at(3 * t + 2)

        def early_buffers_free(w):
            w(c["ST.pe"].at(16 * 3 - 1), c["AV.pe"].at(16 * 3 - 1), c["TQK.dve"].at(NT - 1),
              c["V.pool"].at(NJ - 1))

        def phase1_over(w):
            w(c["ST.pe"].at(16 * B - 1), c["AV.pe"].at(16 * B - 1), c["ST.dve"].at(16 * B - 1),
              c["XB.pool"].at(NG - 1))

        def weights_place_free(w):
            w(logits_made(3 * TB - 1), c["PW.pe"].at(3 * TB // 2 - 1))

        def phase2_buffers_free(w):
            weights_place_free(w)
            w(logits_made(NT - 1), c["XQ.pe"].at(NJ - 1), c["KL.pool"].at(B - 1), c["VC.pool"].at(3 * B - 1),
              c["PRE2.dve"].at(0))

        xT_dram = rows("xT")
        x_dram = io["x"].rearrange("(i p) d -> p i d", p=P)
        out_dram = io["out"].rearrange("(i p) d -> p i d", p=P)

        with nc.Block() as block:
            @block.sync
            def _(sp):
                w = Waiter(sp)
                for kind, i in steps(order, "S"):
                    if kind == "XT":
                        if i >= NXR:
                            w(c["XT.pool"].at(i - NXR))
                        sp.dma_start(xraw[:, i % NXR], xT_dram[:, :, i * 2 * P:(i + 1) * 2 * P])\
                            .then_inc(c[f"XT.dma{i % NXR}"].sem, 16)
                        if i == 0:
                            sp.dma_start(wraw[:, :, D:2 * D], rows("wkT")).then_inc(load_w, 16)
                            sp.dma_start(bqk[:, 0:D], bc("bq")).then_inc(load_b, 16)
                            sp.dma_start(bqk[:, D:2 * D], bc("bk")).then_inc(load_b, 16)
                        if i == 1:
                            sp.dma_start(wv_raw[:], rows("wv")).then_inc(load1, 16)
                            sp.dma_start(wo_ls[:], rows("woT")).then_inc(load1, 16)
                            sp.dma_start(ls[:], bc("ls")).then_inc(load1, 16)
                            sp.dma_start(bvcol[:], io["bv"]).then_inc(load1, 16)
                            sp.dma_start(bo[:], bc("bo")).then_inc(load1, 16)
                            sp.dma_start(ident[:], io["ident"]).then_inc(load_id, 16)
                    elif kind == "XL":
                        sp.dma_start(xs[:, 4 * i:4 * i + 4, :], x_dram[:, 4 * i:4 * i + 4, :]).then_inc(load_x[i], 16)
                    elif kind == "PRE2":
                        early_buffers_free(w)
                        for n, name in enumerate(("xwqT", "xwdT", "xwkT", "xwvT")):
                            sp.dma_start(wx_raw[:, n], rows(name)).then_inc(load2, 16)
                        for buffer, name in ((mask_k, "mask_k"), (mask_v, "mask_v"), (sel_raw, "sel"),
                                             (bqcol, "xbq"), (bkcol, "xbk")):
                            sp.dma_start(buffer[:], io[name]).then_inc(load2, 16)
                        sp.dma_start(cT[:], rows("cT")).then_inc(load2, 16)
                        sp.dma_start(bxv[:], bc("xbv")).then_inc(load2, 16)
                        sp.dma_start(bxd[:], bc("xbd")).then_inc(load2, 16)
                    elif kind == "PRE3":
                        weights_place_free(w)
                        for n, name in enumerate(("wrT", "wkcT", "wvcT")):
                            sp.dma_start(wf_raw[:, n], rows(name)).then_inc(load3, 16)
                        for n, name in enumerate(("mu_r", "mu_k")):
                            sp.dma_start(mu[:, n], io[name]).then_inc(load3, 16)
                    elif kind == "LN3B":
                        w(c["LN3B.act"].at(i))
                        sp.dma_start(out_dram[:, 2 * i:2 * i + 2, :], y[:, i % NY])\
                            .then_inc(c[f"OUT.dma{i % NY}"].sem, 16)
                for n in range(NY):
                    w(c[f"OUT.dma{n}"].at((NJ - 1 - n) // NY))

            @block.scalar
            def _(act):
                w = Waiter(act)
                act.dma_start(wraw[:, :, 0:D], rows("wqT")).then_inc(load_w, 16)

                def copy(out, in_, done, **kw):
                    act.activation(out, in_, ACT.Identity, **kw).then_inc(done.sem, 1)

                for kind, i in steps(order, "A"):
                    if kind == "XT":
                        w(c[f"XT.dma{i % NXR}"].at(i // NXR))
                        if i >= NX:
                            w(c["QK.pe"].at(2 * (i - NX) + 1), c["V.pe"].at(i - NX))
                        copy(xT[0][:, i % NX], xraw[:, i % NXR], c["XT.act"])
                    elif kind == "WV":
                        w(c["W.pe"].at(0))
                        copy(w_vo[0][:].rearrange("p k d -> p (k d)"), big[:, 0:2 * D], c["W.act"])
                    elif kind == "TQK":
                        b, t = divmod(i, TB)
                        w(c["TQK.pe"].at(i))
                        if b >= 2:
                            w(c["ST.pe"].at(16 * (b - 1) - 1))
                        copy(qkT[b % 2][0][:, :, t * P:(t + 1) * P], tiles(bank("TQK", i), 4), c["TQK.act"])
                    elif kind == "V":
                        b, t = divmod(i, TB // 2)
                        w(c["V.dve"].at(i))
                        if b >= 2:
                            w(c["AV.pe"].at(16 * (b - 1) - 1))
                        copy(vv[b % 2][0][:, 2 * t:2 * t + 2, :], tiles(v_sb[:, i % 2]), c["V.act"])
                    elif kind == "ST":
                        w(c["ST.pe"].at(i))
                        if i == 0:
                            w(c["W.pool"].at(0))
                        if i >= NAR:
                            w(c["ST.dve"].at(i - NAR))
                        act.activation(a_sb[:, i % NAR], bank("ST", i), ACT.Sigmoid,
                                       bias=nlogs[:, 0:1], scale=1.0 / 16).then_inc(c["ST.act"].sem, 1)
                        w(c["ST.act"].at(i, 1))
                        if i >= NA:
                            w(c["AV.pe"].at(i - NA))
                        copy(aT[0][:, i % NA], a_sb[:, i % NAR], c["ST.act"])
                    elif kind == "K2":
                        w(c["K2.pe"].at(i))
                        copy(kT[:, i, :], bank("K2", i)[:, 0:B * SC], c["K2.act"], bias=bkcol[:, i:i + 1])
                    elif kind == "KH":
                        if i >= 2:
                            w(logits_made(TB * (i - 1) - 1))
                        for e in range(KC):
                            w(c["KB.pool"].at(i, 2 * e + 2))
                            copy(kb[i % 2][0][:, e, :], kb32[:, e], c["KH.act"])
                    elif kind == "VB":
                        w(c["VB.dve"].at(i, 1))
                        if i >= 1:
                            w(c["VC.pe"].at(3 * i - 1))
                        copy(vc[0][:], v32[:], c["VB.act"])
                    elif kind == "VC":
                        b, r0, r1 = vc_rows(i)
                        w(c["VC.dve"].at(i))
                        if b == 1:
                            phase1_over(w)
                        if b >= 2:
                            w(c["PW.pe"].at(TB // 2 * (b - 1) - 1))
                        copy(vb[b % 2][0][:, r0:r1].rearrange("p r k d -> p (r k d)"),
                             vm[:, r0:r1].rearrange("p r k d -> p (r k d)"), c["VC.act"])
                    elif kind == "TX":
                        w(c["TX.pe"].at(i))
                        if i >= 2:
                            w(c["XQ.pe"].at(i - 2))
                        copy(x1T[0][:, i % 2], bank("TX", i), c["TX.act"])
                    elif kind == "XQ":
                        w(c["XQ.pe"].at(i))
                        if i >= 2:
                            w(logits_made(2 * (i - 2) + 1))
                        for e in range(KC):
                            cut = slice(e * D, (e + 1) * D)
                            copy(xqT[0][:, i % 2, cut], bank("XQ", i)[:, cut], c["XQ.act"], bias=bqcol[:, e:e + 1])
                    elif kind == "EX":
                        t, k = divmod(i, 3)
                        w(c["XM.dve"].at(i))
                        if t >= NP:
                            w(c["TP.pe"].at(3 * (t - NP) + 2))
                        h0, h1 = PIECES[k]
                        for h in range(h0, h1):
                            e = act.activation(p_sb[:, t % NP, h * SP:h * SP + SC],
                                               logits[k][:, (h - h0) * SC:(h - h0 + 1) * SC], ACT.Exp,
                                               bias=neg_mx[:, t % 2, h:h + 1], scale=-1.0)
                        e.then_inc(c["EX.act"].sem, 1)
                    elif kind == "TP":
                        t, j, k0, k1, half = tp_parts(i)
                        w(c["TP.pe"].at(i))
                        if j >= 2:
                            w(c["PW.pe"].at(j - 2))
                        copy(pT[0][:, j % 2, k0:k1, half],
                             bank("TP", i)[:, 0:(k1 - k0) * P].rearrange("p (k t) -> p k t", t=P), c["TP.act"])
                    elif kind in ("PV", "PW"):
                        w(c[kind + ".pe"].at(i))
                        if i >= 2:
                            w(c["XD.pe"].at(i - 2))
                        part = slice(0, D) if kind == "PV" else slice(D, 2 * D)
                        copy(oT[0][:, i % 2, part], bank(kind + "a", i)[:, 0:D], c[kind + ".act"])
                    elif kind == "LN2B":
                        w(c["XD.pool"].at(i))
                        copy(xs[:, 2 * i], xs[:, 2 * i], c["LN2B.act"], bias=nb2[:, i % 2, 0:1],
                             scale=rs2[:, i % 2, 0:1])
                    elif kind == "TY":
                        w(c["TY.pe"].at(i))
                        if i == 0:
                            phase2_buffers_free(w)
                        if i >= 2:
                            w(c["TY.dve"].at(i - 2), c["TY.pool"].at(i - 1))
                        copy(x2T[:, i % 2, :, 1:2 * P + 1], tiles(bank("TY", i)), c["TY.act"])
                    elif kind == "TH":
                        w(c["TY.dve"].at(i))
                        if i >= 2:
                            w(c["FR.pe"].at(i - 2), c["FK.pe"].at(i - 2))
                        copy(xmT[0][:, i % 2].rearrange("p m k t -> p (m k t)"),
                             xm[:, i % 2].rearrange("p m k t -> p (m k t)"), c["TH.act"])
                    elif kind == "FR":
                        w(c["FR.pe"].at(i))
                        if i >= 3:
                            w(c["FVa.dve"].at(i - 3))
                        act.activation(gate[:, i % 3], bank("FR", i), ACT.Sigmoid).then_inc(c["FR.act"].sem, 1)
                    elif kind == "FKa":
                        w(c["FK.pe"].at(i))
                        act.activation(kr[:, i % 2], bank("FK", i), ACT.Relu).then_inc(c["FKa.act"].sem, 1)
                    elif kind == "FK":
                        w(c["FKa.act"].at(i))
                        if i >= 2:
                            w(c["FK.dve"].at(i - 2), c["FV.pe"].at(i - 2))
                        for square in (kkT[0], kk):
                            act.activation(square[:, i % 2], kr[:, i % 2], ACT.Square)\
                                .then_inc(c["FK.act"].sem, 1)

                    elif kind == "LN3B":
                        w(c["LN3B.dve"].at(i))
                        for t in range(2):
                            yt = y[:, i % NY, t]
                            copy(yt, yt, c["LN3B.act"], bias=nb3[:, i % 2, t:t + 1], scale=rs3[:, i % 2, t:t + 1])

            @block.gpsimd
            def _(pool):
                w = Waiter(pool)
                pool.memset(nlogs[:], -float(np.log(np.float32(S))))
                pool.memset(eps4, EPS)
                pool.memset(minus4, -1.0)
                pool.memset(half4, -0.5).then_inc(c["W.pool"].sem, 1)
                w(c["W.pool"].at(0))

                def inverse_deviation(out, variance, n, done, i):
                    pool.tensor_tensor(out, variance, eps4[:, 0:n], ALU.add).then_inc(done.sem, 1)
                    w(done.at(i, 1))
                    pool.tensor_tensor(out, out, half4[:, 0:n], ALU.pow).then_inc(done.sem, 1)

                for kind, i in steps(order, "G"):
                    if kind == "WO":
                        w((load1, LOAD1))
                        pool.tensor_tensor(wo_ls[:], wo_ls[:], each_tile(ls[:], KC), ALU.mult)\
                            .then_inc(c["WO.pool"].sem, 1)
                        pool.tensor_tensor(bo[:], bo[:], ls[:], ALU.mult).then_inc(c["WO.pool"].sem, 1)
                    elif kind == "XT":
                        w(c["XT.act"].at(i))
                        if i >= NX:
                            w(c["QK.pe"].at(2 * (i - NX) + 1), c["V.pe"].at(i - NX))
                        pool.tensor_tensor(xT[1][:, i % NX], xraw[:, i % NXR], f(xT[0][:, i % NX]),
                                           ALU.subtract).then_inc(c["XT.pool"].sem, 1)
                    elif kind == "QK":
                        w(c["QK.dve"].at(i))
                        if i >= 4:
                            w(c["QN.dve"].at(i - 4))
                        inverse_deviation(rs1[:, i % 4], mv1[:, i % 4, :, 1], 2, c["QK.pool"], i)
                    elif kind == "V":
                        b, t = divmod(i, TB // 2)
                        w(c["V.act"].at(i))
                        if b >= 2:
                            w(c["AV.pe"].at(16 * (b - 1) - 1))
                        hi, lo = hi_lo(vv[b % 2], slice(2 * t, 2 * t + 2))
                        pool.tensor_tensor(lo, tiles(v_sb[:, i % 2]), f(hi), ALU.subtract)\
                            .then_inc(c["V.pool"].sem, 1)
                    elif kind == "ST" and i % TB == TB // 2:
                        g = i // TB
                        w((load_x[g], 16), c["WO.pool"].at(0))
                        x4 = xs[:, 4 * g:4 * g + 4, :]
                        pool.tensor_tensor(x4, x4, each_tile(bo[:], 4), ALU.add).then_inc(c["XB.pool"].sem, 1)
                    elif kind == "LN1S":
                        w(c["LN1S.dve"].at(i))
                        if i:
                            w(c["LN1B.dve"].at(i - 1))
                        inverse_deviation(rsl[:], mvl[:, :, 1], 4, c["LN1S.pool"], i)
                    elif kind == "PRE2":
                        phase1_over(w)
                        for n in range(NP):
                            pool.memset(weights(n)[:, :, SC:SP], 0.0)
                            ms = pool.memset(p_sb[:, n, PW:PPAD], 0.0)
                        ms.then_inc(c["PRE2.pool"].sem, 1)
                    elif kind == "KB":
                        w((load2, LOAD2), c["K2.act"].at(KC - 1))
                        if i:
                            w(c["KL.pool"].at(i - 1))
                        else:
                            pool.memset(kb32[:], 0.0).then_inc(c["KZ.pool"].sem, 1)
                            w(c["KZ.pool"].at(0))
                        for e, h0, h1, to in KEYS:
                            n, first = h1 - h0, h0 - e * HC
                            pool.tensor_tensor(heads(kb32[:, e, to:to + n * SC]),
                                               kT[:, e, i * SC:(i + 1) * SC].rearrange("p (o k) -> p o k", o=1)
                                               .to_broadcast([P, n, SC]),
                                               mask_k[:, first:first + n].rearrange("p (h o) -> p h o", o=1)
                                               .to_broadcast([P, n, SC]), ALU.mult)\
                                .then_inc(c["KB.pool"].sem, 1)
                    elif kind == "KL":
                        for e in range(KC):
                            w(c["KH.act"].at(i, e + 1))
                            pool.tensor_tensor(kb[i % 2][1][:, e, :], kb32[:, e], f(kb[i % 2][0][:, e, :]),
                                               ALU.subtract).then_inc(c["KL.pool"].sem, 1)
                    elif kind == "VC":
                        b, r0, r1 = vc_rows(i)
                        w(c["VC.act"].at(i))
                        hi, lo = (t[:, r0:r1].rearrange("p r k d -> p (r k d)") for t in vb[b % 2])
                        pool.tensor_tensor(lo, vm[:, r0:r1].rearrange("p r k d -> p (r k d)"), f(hi),
                                           ALU.subtract).then_inc(c["VC.pool"].sem, 1)
                    elif kind == "XR":
                        w(c["TX.pe"].at(i))
                        x2 = xs[:, 2 * i:2 * i + 2, :]
                        pool.tensor_tensor(x2, x2, each_tile(bxd[:], 2), ALU.add).then_inc(c["XR.pool"].sem, 1)
                    elif kind == "FO":
                        w(c["EX.act"].at(3 * i + 2), c["PRE2.pool"].at(0))
                        if i:
                            w(c["SMa.dve"].at(i - 1))
                        p = weights(i)
                        pool.tensor_tensor(fold[:].rearrange("p (h k) -> p h k", k=FO), p[:, :, 0:FO],
                                           p[:, :, FO:2 * FO], ALU.add).then_inc(c["FO.pool"].sem, 1)
                    elif kind == "SM":
                        w(c["SM.dve"].at(i))
                        pool.tensor_tensor(weights(i), weights(i), rc[:, i % 2].rearrange("p (h o) -> p h o", o=1)
                                           .to_broadcast([P, H, SP]), ALU.mult).then_inc(c["SM.pool"].sem, 1)
                    elif kind == "XD":
                        w(c["XD.dve"].at(i))
                        if i >= 2:
                            w(c["LN2B.act"].at(i - 2), c["LN2B.dve"].at(i - 2))
                        r, nb = rs2[:, i % 2], nb2[:, i % 2]
                        pool.tensor_tensor(r, mv2[:, i % 2, :, 1], eps4[:, 0:2], ALU.add)\
                            .then_inc(c["XD.pool"].sem, 1)
                        pool.tensor_tensor(nb, mv2[:, i % 2, :, 0], minus4[:, 0:2], ALU.mult)\
                            .then_inc(c["XD.pool"].sem, 1)
                        w(c["XD.pool"].at(i, 1))
                        pool.tensor_tensor(r, r, half4[:, 0:2], ALU.pow).then_inc(c["XD.pool"].sem, 1)
                        w(c["XD.pool"].at(i, 3))
                        pool.tensor_tensor(nb, nb, r, ALU.mult).then_inc(c["XD.pool"].sem, 1)
                    elif kind == "TY":
                        if i == 0:
                            phase2_buffers_free(w)
                        if i >= 2:
                            w(c["TY.dve"].at(i - 2))
                        if i % (TB // 2) == 0:
                            pool.memset(x2T[:, i % 2, :, 0:1], 0.0).then_inc(c["TY.pool"].sem, 1)
                        else:
                            w(c["TY.act"].at(i - 1))
                            pool.tensor_copy(x2T[:, i % 2, :, 0:1], x2T[:, (i - 1) % 2, :, 2 * P:2 * P + 1])\
                                .then_inc(c["TY.pool"].sem, 1)
                        w(c["TY.act"].at(i), c["TY.pool"].at(i, 1))
                        pool.tensor_tensor(dd[:, i % 2], x2T[:, i % 2, :, 1:2 * P + 1], x2T[:, i % 2, :, 0:2 * P],
                                           ALU.subtract).then_inc(c["TY.pool"].sem, 1)
                    elif kind == "TH":
                        w(c["TH.act"].at(i))
                        hi, lo = (t[:, i % 2].rearrange("p m k t -> p (m k t)") for t in xmT)
                        pool.tensor_tensor(lo, xm[:, i % 2].rearrange("p m k t -> p (m k t)"), f(hi),
                                           ALU.subtract).then_inc(c["TH.pool"].sem, 1)
                    elif kind == "FV":
                        w(c["FV.dve"].at(i))
                        if i >= 2:
                            w(c["LN3B.act"].at(i - 2))
                        inverse_deviation(rs3[:, i % 2], mv3[:, i % 2, :, 1], 2, c["FV.pool"], i)

            @block.vector
            def _(dve):
                w = Waiter(dve)

                def add_sub(out, in0, in1, op, done):
                    dve.tensor_tensor(out, in0, in1, op).then_inc(done.sem, 1)

                def low_part(hi, lo, whole, done):
                    add_sub(lo, whole, f(hi), ALU.subtract, done)

                ready = c["W.dve"]
                w((load_w, LOAD_W))
                dve.tensor_copy(w_qk[0][:], wraw[:]).then_inc(ready.sem, 1)
                w(ready.at(0, 1))
                low_part(w_qk[0][:], w_qk[1][:], wraw[:], ready)
                for kind, i in steps(order, "D"):
                    if kind == "WO":
                        w((load1, LOAD1))
                        dve.tensor_copy(bvwide[:], bvcol[:].rearrange("p (k o) -> p k o", o=1)
                                        .to_broadcast([P, KC, P])).then_inc(c["WO.dve"].sem, 1)
                    elif kind == "WV":
                        w(c["W.act"].at(0))
                        low_part(w_vo[0][:].rearrange("p k d -> p (k d)"),
                                 w_vo[1][:].rearrange("p k d -> p (k d)"), big[:, 0:2 * D], ready)
                        dve.tensor_copy(bvo[:], big[:, BANK:BANK + D]).then_inc(ready.sem, 1)
                    elif kind == "QK":
                        w(c["QK.pe"].at(i), (load_b, LOAD_B))
                        if i >= 4:
                            w(c["TQK.pe"].at(i - 4), c["QK.pool"].at(i - 4))
                        add_sub(qk_sb[:, i % 4], bank("QK", i), bqk[:], ALU.add, c["QK.dve"])
                        w(c["QK.dve"].at(i, 1))
                        for m in range(2):
                            dve.bn_stats(st1[:, i % 4, m], qk_sb[:, i % 4, m * D:(m + 1) * D])\
                                .then_inc(c["QK.dve"].sem, 1)
                        for m in range(2):
                            w(c["QK.dve"].at(i, 2 + m))
                            dve.bn_aggr(mv1[:, i % 4, m], st1[:, i % 4, m]).then_inc(c["QK.dve"].sem, 1)
                    elif kind == "QN":
                        w(c["QK.pool"].at(i))
                        for m in range(2):
                            s_ = qk_sb[:, i % 4, m * D:(m + 1) * D]
                            dve.tensor_scalar(s_, s_, mv1[:, i % 4, m, 0:1], rs1[:, i % 4, m:m + 1],
                                              ALU.subtract, ALU.mult).then_inc(c["QN.dve"].sem, 1)
                    elif kind == "TQK":
                        b, t = divmod(i, TB)
                        w(c["TQK.act"].at(i))
                        low_part(*hi_lo(qkT[b % 2], slice(None), slice(t * P, (t + 1) * P)),
                                 tiles(bank("TQK", i), 4), c["TQK.dve"])
                    elif kind == "V":
                        w(c["V.pe"].at(i), ready.at(0, W_BVO))
                        if i >= 2:
                            w(c["V.pool"].at(i - 2))
                        add_sub(tiles(v_sb[:, i % 2]), tiles(bank("V", i)), each_tile(bvo[:], 2), ALU.add, c["V.dve"])
                    elif kind == "ST":
                        w(c["ST.act"].at(i))
                        low_part(*hi_lo(aT, i % NA), a_sb[:, i % NAR], c["ST.dve"])
                    elif kind == "LN1A":
                        w(c["AV.pe"].at(TB * i + TB - 1), c["XB.pool"].at(i))
                        for t in (0, 2):
                            x2 = xs[:, 4 * i + t:4 * i + t + 2]
                            add_sub(x2, acc[:, t:t + 2], x2, ALU.add, c["LN1A.dve"])
                    elif kind == "LN1S":
                        for t in range(4):
                            w(c["LN1A.dve"].at(i, t // 2 + 1))
                            dve.bn_stats(stl[:, t], xs[:, 4 * i + t]).then_inc(c["LN1S.dve"].sem, 1)
                        if i:
                            w(c["LN1S.pool"].at(i - 1))
                        for t in range(4):
                            w(c["LN1S.dve"].at(i, 1 + t))
                            dve.bn_aggr(mvl[:, t], stl[:, t]).then_inc(c["LN1S.dve"].sem, 1)
                    elif kind == "LN1B":
                        w(c["LN1S.pool"].at(i))
                        for t in range(4):
                            x1 = xs[:, 4 * i + t]
                            dve.tensor_scalar(x1, x1, mvl[:, t, 0:1], rsl[:, t:t + 1],
                                              ALU.subtract, ALU.mult).then_inc(c["LN1B.dve"].sem, 1)
                    elif kind == "PRE2":
                        w((load2, LOAD2))
                        dve.tensor_copy(w_x[0][:], wx_raw[:, 0:2]).then_inc(c["PRE2.dve"].sem, 1)
                        w(c["PRE2.dve"].at(0, 1))
                        flat = "p m k d -> p (m k d)"
                        low_part(w_x[0][:].rearrange(flat), w_x[1][:].rearrange(flat),
                                 wx_raw[:, 0:2].rearrange(flat), c["PRE2.dve"])
                        dve.tensor_copy(sel[:], sel_raw[:]).then_inc(c["PRE2.dve"].sem, 1)
                    elif kind == "VB":
                        w(c["VB.pe"].at(i))
                        add_sub(v32[:], bank("VB", i)[0:SC, 0:D], bxv[0:SC, :], ALU.add, c["VB.dve"])
                        w(c["VB.act"].at(i))
                        if i >= 1:
                            w(c["VC.pe"].at(3 * i - 1))
                        low_part(vc[0][:], vc[1][:], v32[:], c["VB.dve"])
                    elif kind == "VC":
                        b, r0, r1 = vc_rows(i)
                        w(c["VC.pe"].at(i))
                        if b:
                            w(c["VC.pool"].at(i - 3))
                        add_sub(vm[:, r0:r1],
                                bank("VC", i)[:, 0:(r1 - r0) * D].rearrange("p (r k d) -> p r k d", k=KC, d=P),
                                mask_v[:, r0:r1].rearrange("p r (o d) -> p r o d", o=1)
                                .to_broadcast([P, r1 - r0, KC, P]), ALU.mult, c["VC.dve"])
                    elif kind == "TX":
                        w(c["TX.act"].at(i))
                        low_part(*hi_lo(x1T, i % 2), bank("TX", i), c["TX.dve"])
                    elif kind == "XQ":
                        w(c["XQ.act"].at(i))
                        for e in range(KC):
                            cut = slice(e * D, (e + 1) * D)
                            dve.scalar_tensor_tensor(out=xqT[1][:, i % 2, cut], in0=bank("XQ", i)[:, cut],
                                                     scalar=bqcol[:, e:e + 1], in1=f(xqT[0][:, i % 2, cut]),
                                                     op0=ALU.add, op1=ALU.subtract)\
                                .then_inc(c["XQ.dve"].sem, 1)
                    elif kind == "XM":
                        t, k = divmod(i, 3)
                        w(c["XS.pe"].at(i))
                        if t >= 2:
                            w(c["EX.act"].at(i - 6))
                        dve.tensor_reduce(neg_mx[:, t % 2, slice(*PIECES[k])], heads(logits[k]), AX, ALU.min)\
                            .then_inc(c["XM.dve"].sem, 1)
                    elif kind == "SMa":
                        w(c["FO.pool"].at(i))
                        dve.tensor_reduce(sm[:, i % 2], fold[:].rearrange("p (h k) -> p h k", k=FO), AX, ALU.add)\
                            .then_inc(c["SMa.dve"].sem, 1)
                    elif kind == "SM":
                        w(c["SMa.dve"].at(i))
                        if i >= 2:
                            w(c["SM.pool"].at(i - 2))
                        dve.reciprocal(rc[:, i % 2], sm[:, i % 2]).then_inc(c["SM.dve"].sem, 1)
                    elif kind == "TP":
                        t, j, k0, k1, half = tp_parts(i)
                        w(c["TP.act"].at(i))
                        low_part(*hi_lo(pT, j % 2, slice(k0, k1), half),
                                 bank("TP", i)[:, 0:(k1 - k0) * P].rearrange("p (k t) -> p k t", t=P), c["TP.dve"])
                    elif kind in ("PV", "PW"):
                        w(c[kind + ".act"].at(i))
                        part = slice(0, D) if kind == "PV" else slice(D, 2 * D)
                        low_part(*hi_lo(oT, i % 2, part), bank(kind + "a", i)[:, 0:D], c[kind + ".dve"])
                    elif kind == "XDa":
                        w(c["XD.pe"].at(i), c["XR.pool"].at(i))
                        x2 = xs[:, 2 * i:2 * i + 2, :]
                        add_sub(x2, tiles(bank("XD", i)), x2, ALU.add, c["XDa.dve"])
                    elif kind == "XD":
                        w(c["XDa.dve"].at(i))
                        for t in range(2):
                            dve.bn_stats(st2[:, i % 2, t], xs[:, 2 * i + t]).then_inc(c["XD.dve"].sem, 1)
                        if i >= 2:
                            w(c["XD.pool"].at(i - 2))
                        for t in range(2):
                            w(c["XD.dve"].at(i, 1 + t))
                            dve.bn_aggr(mv2[:, i % 2, t], st2[:, i % 2, t]).then_inc(c["XD.dve"].sem, 1)
                    elif kind == "LN2B":
                        w(c["XD.pool"].at(i))
                        x2 = xs[:, 2 * i + 1]
                        dve.tensor_scalar(x2, x2, mv2[:, i % 2, 1, 0:1], rs2[:, i % 2, 1:2],
                                          ALU.subtract, ALU.mult).then_inc(c["LN2B.dve"].sem, 1)
                    elif kind == "PRE3":
                        w((load3, LOAD3))
                        flat = "p m k d -> p (m k d)"
                        dve.tensor_copy(w_f[0][:], wf_raw[:]).then_inc(c["PRE3.dve"].sem, 1)
                        w(c["PRE3.dve"].at(0, 1))
                        low_part(w_f[0][:].rearrange(flat), w_f[1][:].rearrange(flat), wf_raw[:].rearrange(flat),
                                 c["PRE3.dve"])
                    elif kind == "TY":
                        w(c["TY.pool"].at(i))
                        if i >= 2:
                            w(c["TH.pool"].at(i - 2))
                        for m in range(2):
                            for k in range(KC):
                                dve.scalar_tensor_tensor(out=xm[:, i % 2, m, k], in0=dd[:, i % 2, k],
                                                         scalar=mu[:, m, k:k + 1], in1=x2T[:, i % 2, k, 0:2 * P],
                                                         op0=ALU.mult, op1=ALU.add)\
                                    .then_inc(c["TY.dve"].sem, 1)
                    elif kind == "FK":
                        w(c["FK.act"].at(i))
                        if i >= 2:
                            w(c["FV.pe"].at(i - 2))
                        low_part(*hi_lo(kkT, i % 2), kk[:, i % 2], c["FK.dve"])
                    elif kind == "FVa":
                        w(c["FV.pe"].at(i), c["FR.act"].at(i))
                        if i >= NY:
                            w(c[f"OUT.dma{i % NY}"].at(i // NY - 1))
                        yy = y[:, i % NY]
                        add_sub(yy, tiles(bank("FV", i)), tiles(gate[:, i % 3]), ALU.mult, c["FVa.dve"])
                    elif kind == "FVb":
                        yy = y[:, i % NY]
                        w(c["FVa.dve"].at(i))
                        add_sub(yy, yy, xs[:, 2 * i:2 * i + 2, :], ALU.add, c["FVb.dve"])
                    elif kind == "FV":
                        yy = y[:, i % NY]
                        w(c["FVb.dve"].at(i))
                        for t in range(2):
                            dve.bn_stats(st3[:, i % 2, t], yy[:, t]).then_inc(c["FV.dve"].sem, 1)
                        if i >= 2:
                            w(c["FV.pool"].at(i - 2))
                        for t in range(2):
                            w(c["FV.dve"].at(i, 1 + t))
                            dve.bn_aggr(mv3[:, i % 2, t], st3[:, i % 2, t]).then_inc(c["FV.dve"].sem, 1)
                    elif kind == "LN3B":
                        w(c["FV.pool"].at(i))
                        if i >= 2:
                            w(c["LN3B.act"].at(i - 2))
                        dve.scalar_tensor_tensor(out=nb3[:, i % 2], in0=mv3[:, i % 2, :, 0], scalar=-1.0,
                                                 in1=rs3[:, i % 2], op0=ALU.mult, op1=ALU.mult)\
                            .then_inc(c["LN3B.dve"].sem, 1)

            @block.tensor
            def _(pe):
                w = Waiter(pe)

                def transposed(out, i):
                    for k in range(KC):
                        for t in range(2):
                            mm = pe.transpose(out[:, k * D + t * P:k * D + (t + 1) * P],
                                              xs[:, 2 * i + t, k * P:(k + 1) * P], ident[:])
                    return mm

                w(c["W.dve"].at(0, W_QK_LO))
                for kind, i in steps(order, "P"):
                    if kind in let_go or kind in own_bank:
                        bank_free(w, kind, i)
                    if kind == "WV":
                        w(c["WO.dve"].at(0), c["WO.pool"].at(0, 1))
                        for m in range(KC):
                            for e in range(KC):
                                pe.matmul(big[:, m * D:(m + 1) * D], wv_raw[:, e, m * P:(m + 1) * P],
                                          wo_ls[:, e, :], start=e == 0, stop=e == KC - 1)
                        for e in range(KC):
                            mm = pe.matmul(big[:, BANK:BANK + D], bvwide[:, e, :], wo_ls[:, e, :],
                                           start=e == 0, stop=e == KC - 1)
                        mm.then_inc(c["W.pe"].sem, 1)
                    elif kind == "QK":
                        j, t = divmod(i, 2)
                        w(c["XT.act"].at(j), c["XT.pool"].at(j))
                        split_product(pe, bank("QK", i),
                                      [hi_lo(xT, j % NX, k, slice(t * P, (t + 1) * P)) for k in range(KC)],
                                      [hi_lo(w_qk, k) for k in range(KC)])\
                            .then_inc(c["QK.pe"].sem, 1)
                    elif kind == "V":
                        w(c["W.dve"].at(0, W_VO_LO), c["XT.pool"].at(i))
                        for t in range(2):
                            mm = split_product(pe, bank("V", i)[:, t * D:(t + 1) * D],
                                               [hi_lo(xT, i % NX, k, slice(t * P, (t + 1) * P)) for k in range(KC)],
                                               [hi_lo(w_vo, k) for k in range(KC)])
                        mm.then_inc(c["V.pe"].sem, 1)
                    elif kind == "TQK":
                        w(c["QN.dve"].at(i), (load_id, 16))
                        for m in range(4):
                            mm = pe.transpose(bank("TQK", i)[:, m * P:(m + 1) * P],
                                              qk_sb[:, i % 4, m * P:(m + 1) * P], ident[:])
                        mm.then_inc(c["TQK.pe"].sem, 1)
                    elif kind == "ST":
                        g, kt = divmod(i, TB)
                        b = g // 2
                        w(c["TQK.dve"].at(max(TB * b + kt, 4 * g + 3)))
                        q0 = (g % 2) * BANK
                        split_product(pe, bank("ST", i),
                                      [hi_lo(qkT[b % 2], 2 + e, slice(kt * P, (kt + 1) * P)) for e in range(KC)],
                                      [hi_lo(qkT[b % 2], e, slice(q0, q0 + BANK)) for e in range(KC)])\
                            .then_inc(c["ST.pe"].sem, 1)
                    elif kind == "AV":
                        g, kt = divmod(i, TB)
                        b = g // 2
                        w(c["ST.dve"].at(i), c["V.pool"].at(TB // 2 * b + kt // 2))
                        if i == 0:
                            w(c["W.dve"].at(0))
                        for t in range(4):
                            if kt == 0 and g:
                                w(c["LN1A.dve"].at(g - 1, t // 2 + 1))
                            mm = split_product(pe, acc[:, t],
                                               [hi_lo(aT, i % NA, slice(t * P, (t + 1) * P))],
                                               [hi_lo(vv[b % 2], kt)],
                                               first=kt == 0 and t % 2 == 0, last=kt == TB - 1, check=False)
                        mm.then_inc(c["AV.pe"].sem, 1)
                    elif kind == "K2":
                        w((load2, LOAD2))
                        for k in range(KC):
                            mm = pe.matmul(bank("K2", i)[:, 0:B * SC], wx_raw[:, XKW, k, i * P:(i + 1) * P],
                                           cT[:, k, :], start=k == 0, stop=k == KC - 1)
                        mm.then_inc(c["K2.pe"].sem, 1)
                    elif kind == "VB":
                        for k in range(KC):
                            mm = pe.matmul(bank("VB", i)[0:SC, 0:D], cT[:, k, i * SC:(i + 1) * SC],
                                           wx_raw[:, XVW, k, :], start=k == 0, stop=k == KC - 1)
                        mm.then_inc(c["VB.pe"].sem, 1)
                    elif kind == "VC":
                        b, r0, r1 = vc_rows(i)
                        w(c["VB.dve"].at(b), c["PRE2.dve"].at(0))
                        for r in range(r0, r1):
                            for n in range(2):
                                mm = pe.matmul(bank("VC", i)[:, (r % 2) * D:(r % 2 + 1) * D],
                                               sel[:, r * P:(r + 1) * P], vc[n][:], start=n == 0, stop=n == 1)
                        mm.then_inc(c["VC.pe"].sem, 1)
                    elif kind == "TX":
                        w(c["LN1B.dve"].at(i // 2))
                        transposed(bank("TX", i), i).then_inc(c["TX.pe"].sem, 1)
                    elif kind == "XQ":
                        w(c["TX.dve"].at(i), c["PRE2.dve"].at(0))
                        for e in range(KC):
                            mm = split_product(pe, bank("XQ", i)[:, e * D:(e + 1) * D],
                                               [hi_lo(w_x, XQW, k, slice(e * P, (e + 1) * P)) for k in range(KC)],
                                               [hi_lo(x1T, i % 2, slice(k * D, (k + 1) * D)) for k in range(KC)])
                        mm.then_inc(c["XQ.pe"].sem, 1)
                    elif kind == "XS":
                        t, k = divmod(i, 3)
                        j, u = divmod(t, 2)
                        b = t // TB
                        w(c["XQ.dve"].at(j), c["KL.pool"].at(b),
                          c["EX.act"].at(i - 3) if i >= 3 else c["LN1A.dve"].at(NG - 1, min(k + 1, 2)))
                        for n, (part, lo, hi, to) in enumerate(PRODUCTS[k]):
                            mm = split_product(pe, big[:, k * BANK + to:k * BANK + to + hi - lo],
                                               [hi_lo(xqT, j % 2, slice(part * D + u * P, part * D + (u + 1) * P))],
                                               [hi_lo(kb[b % 2], part, slice(lo, hi))], first=n == 0, check=False)
                        mm.then_inc(c["XS.pe"].sem, 1)
                    elif kind == "TP":
                        t, j, k0, k1, half = tp_parts(i)
                        w(c["SM.pool"].at(t), c["PRE2.pool"].at(0))
                        for k in range(k0, k1):
                            c0 = (k // RV) * WP + (k % RV) * P
                            mm = pe.transpose(bank("TP", i)[:, (k % 4) * P:(k % 4 + 1) * P],
                                              p_sb[:, t % NP, c0:c0 + P], ident[:])
                        mm.then_inc(c["TP.pe"].sem, 1)
                    elif kind in ("PVa", "PV", "PWa", "PW"):
                        b, k = i // (TB // 2), int(kind[1] == "W")
                        w(c["TP.dve"].at(3 * (2 * i + 1) + 2), c["VC.pool"].at(3 * b + 2))
                        starts = kind.endswith("a")
                        first_rows = 2 if k else 3
                        mm = split_product(pe, bank(kind[:2] + "a", i)[:, 0:D],
                                           [hi_lo(vb[b % 2], r, k) for r in range(RV) if (r < first_rows) == starts],
                                           [hi_lo(pT, i % 2, k * RV + r) for r in range(RV)
                                            if (r < first_rows) == starts], first=starts, last=not starts)
                        if not starts:
                            mm.then_inc(c[kind + ".pe"].sem, 1)
                    elif kind == "XD":
                        w(c["PV.dve"].at(i), c["PW.dve"].at(i))
                        for t in range(2):
                            mm = split_product(pe, bank("XD", i)[:, t * D:(t + 1) * D],
                                               [hi_lo(oT, i % 2, slice(k * D + t * P, k * D + (t + 1) * P)) for k in range(KC)],
                                               [hi_lo(w_x, XDW, k) for k in range(KC)])
                        mm.then_inc(c["XD.pe"].sem, 1)
                    elif kind == "TY":
                        w(c["LN2B.act"].at(i), c["LN2B.dve"].at(i))
                        transposed(bank("TY", i), i).then_inc(c["TY.pe"].sem, 1)
                    elif kind == "FR":
                        w(c["TH.pool"].at(i), c["PRE3.dve"].at(0))
                        for t in range(2):
                            mm = split_product(pe, bank("FR", i)[:, t * D:(t + 1) * D],
                                               [hi_lo(xmT, i % 2, MIX_R, k, slice(t * P, (t + 1) * P)) for k in range(KC)],
                                               [hi_lo(w_f, MIX_R, k) for k in range(KC)])
                        mm.then_inc(c["FR.pe"].sem, 1)
                    elif kind == "FK":
                        w(c["TH.pool"].at(i), c["PRE3.dve"].at(0))
                        for e in range(KC):
                            mm = split_product(pe, bank("FK", i)[:, e * D:(e + 1) * D],
                                               [hi_lo(w_f, MIX_K, k, slice(e * P, (e + 1) * P)) for k in range(KC)],
                                               [hi_lo(xmT, i % 2, MIX_K, k) for k in range(KC)])
                        mm.then_inc(c["FK.pe"].sem, 1)
                    elif kind == "FV":
                        w(c["FK.dve"].at(i))
                        for t in range(2):
                            mm = split_product(pe, bank("FV", i)[:, t * D:(t + 1) * D],
                                               [hi_lo(kkT, i % 2, slice(k * D + t * P, k * D + (t + 1) * P)) for k in range(KC)],
                                               [hi_lo(w_f, VW, k) for k in range(KC)])
                        mm.then_inc(c["FV.pe"].sem, 1)


def shape_constants():
    row = np.arange(P)
    mask_k = (row[:, None] // DH == np.arange(HC)[None, :]).astype(np.float32) * np.float32(-DH ** -0.5)
    flat = np.arange(RV * P)
    sel = ((flat[None, :] % SP == np.arange(SC)[:, None]) & (flat[None, :] < WP)).astype(np.float32)
    head = flat.reshape(RV, P).T // SP
    mask_v = (head[:, :, None] == (row // DH)[None, None, :]).astype(np.float32)
    return {"ident": np.eye(P, dtype=np.float32), "mask_k": mask_k, "sel": sel,
            "mask_v": np.ascontiguousarray(mask_v)}


def kernel(**inputs):
    import numpy as _np
    import concourse.bacc as _bacc
    from concourse.bass_utils import run_bass_kernel_spmd as _run

    a = {k: _np.asarray(v) for k, v in inputs.items()}
    x = a["x"].reshape(B * S, D)
    laid = {
        "x": x, "xT": x.T, "cT": a["ctx_1024"].reshape(B * SC, D).T,
        "wqT": a["L0_attn_Wq"].T, "wkT": a["L0_attn_Wk"].T, "wv": a["L0_attn_Wv"], "woT": a["L0_attn_Wo"].T,
        "bq": a["L0_attn_bq"], "bk": a["L0_attn_bk"], "bv": a["L0_attn_bv"], "bo": a["L0_attn_bo"],
        "ls": a["L0_attn_layerscale"],
        "xwqT": a["L0_xattn_wq_w"].T, "xwkT": a["L0_xattn_wk_w"].T, "xwvT": a["L0_xattn_wv_w"].T,
        "xwdT": a["L0_xattn_dense_w"].T,
        "xbq": a["L0_xattn_wq_b"], "xbk": a["L0_xattn_wk_b"], "xbv": a["L0_xattn_wv_b"],
        "xbd": a["L0_xattn_dense_b"],
        "wrT": a["L0_ffn_W_r"].T, "wkcT": a["L0_ffn_W_k"].T, "wvcT": a["L0_ffn_W_v"].T,
        "mu_r": a["L0_ffn_mu_r"], "mu_k": a["L0_ffn_mu_k"],
    }
    for name in ("bv", "xbq", "xbk", "mu_r", "mu_k"):
        laid[name] = laid[name].reshape(KC, P).T
    laid.update(shape_constants())
    nc = _bacc.Bacc("TRN2", target_bir_lowering=False, num_devices=1)
    arrays, io = {}, {}
    for name, v in laid.items():
        v = _np.ascontiguousarray(v)
        arrays[f"in_{name}"] = v
        io[name] = nc.dram_tensor(f"in_{name}", v.shape, mybir.dt.from_np(v.dtype), kind="ExternalInput").ap()
    io["out"] = nc.dram_tensor("out_y", (B * S, D), F32, kind="ExternalOutput").ap()
    decoder_layer(nc, io)
    r = _run(nc, [arrays], core_ids=[0])
    return r.results[0]["out_y"].reshape(B, S, D)
```
